# Optimizing a Trainium2 kernel written in Bass

```python
import numpy as np
import jax
import jax.numpy as jnp

def _softmax(x, axis=-1):
    return jax.nn.softmax(x, axis=axis)

def _gelu(x):
    return jax.nn.gelu(x, approximate=True)

def _silu(x):
    return jax.nn.silu(x)

def _sigmoid(x):
    return jax.nn.sigmoid(x)

def _layernorm(x, axis=-1, eps=1e-05):
    m = jnp.mean(x, axis=axis, keepdims=True)
    v = jnp.var(x, axis=axis, keepdims=True)
    return (x - m) / jnp.sqrt(v + eps)

def _scatter_add(tgt, idx, src, axis=0):
    return tgt.at[idx].add(src)

def _segment_sum(src, seg, n):
    return jax.ops.segment_sum(src, seg, n)
kernel_name = 'mk_hybrid_d1_jaxref_r8_c20243'

def setup_inputs(seed: int=0):
    np.random.seed(seed)
    _w = jnp.asarray

    def _L0_attn_a_setup():
        import jax, jax.numpy as jnp
        import numpy as np
        B, N, E, H = (1, 512, 256, 16)
        D = E // H
        DEGREE = 4
        LN_EPS = 1e-05
        ROPE_BASE = 10000.0

        def rope_cos_sin(n, d):
            inv_freq = 1.0 / ROPE_BASE ** (jnp.arange(0, d, 2, dtype=jnp.float32) / d)
            t = jnp.arange(n, dtype=jnp.float32)[:, None] * inv_freq[None, :]
            return (jnp.cos(t), jnp.sin(t))

        def apply_rope(x, cos, sin):
            x1, x2 = jnp.split(x, 2, axis=-1)
            c = cos[None, :, None, :]
            s = sin[None, :, None, :]
            return jnp.concatenate([x1 * c - x2 * s, x1 * s + x2 * c], axis=-1)

        def layernorm(x, scale, bias, eps=LN_EPS):
            m = jnp.mean(x, axis=-1, keepdims=True)
            v = jnp.var(x, axis=-1, keepdims=True)
            return (x - m) * jax.lax.rsqrt(v + eps) * scale + bias

        def polynomial_attention(q, k, v, degree, is_causal):
            a = jnp.einsum('bhnd,bhmd->bhnm', q, k) ** degree
            if is_causal:
                a = jnp.tril(a)
            denom = jnp.sum(a, axis=-1, keepdims=True)
            return jnp.einsum('bhnm,bhmd->bhnd', a / denom, v)
        key = jax.random.key(seed)
        k0, k1, k2 = jax.random.split(key, 3)
        x = jax.random.normal(k0, (B, N, E), dtype=jnp.float32)
        w_qkv = jax.random.normal(k1, (E, 3 * E), dtype=jnp.float32) * (1.0 / np.sqrt(E))
        w_out = jax.random.normal(k2, (E, E), dtype=jnp.float32) * (1.0 / np.sqrt(E))
        ln_scale = jnp.ones((D,), dtype=jnp.float32)
        ln_bias = jnp.zeros((D,), dtype=jnp.float32)
        return {'x': x, 'w_qkv': w_qkv, 'w_out': w_out, 'ln_scale': ln_scale, 'ln_bias': ln_bias}
    _L0_attn_a_in = _L0_attn_a_setup()

    def _L0_attn_b_setup():
        import jax, jax.numpy as jnp
        import numpy as np
        NH = 16
        key = jax.random.key(seed)
        ks = jax.random.split(key, 5)
        B, T, D = (2, 256, 256)
        scale = 0.02
        return {'x': jax.random.normal(ks[0], (B, T, D), dtype=jnp.float32), 'Wq': jax.random.normal(ks[1], (D, D), dtype=jnp.float32) * scale, 'Wk': jax.random.normal(ks[2], (D, D), dtype=jnp.float32) * scale, 'Wv': jax.random.normal(ks[3], (D, D), dtype=jnp.float32) * scale, 'Wo': jax.random.normal(ks[4], (D, D), dtype=jnp.float32) * scale}
    _L0_attn_b_in = _L0_attn_b_setup()

    def _L0_ffn_setup():
        import jax, jax.numpy as jnp
        import numpy as np
        B, S, D = (2, 256, 256)
        I = 128
        E = 32
        K = 4
        NS = 1
        ALPHA = 7.0

        def _clamped_swiglu(x, wg, wu, wd):
            g = jnp.clip(x @ wg.T, -ALPHA, ALPHA)
            u = jnp.clip(x @ wu.T, -ALPHA, ALPHA)
            return jax.nn.silu(g) * u @ wd.T
        key = jax.random.key(seed)
        ks = jax.random.split(key, 9)
        s = 0.02
        return {'hidden': jax.random.normal(ks[0], (B, S, D), jnp.float32), 'router_w': jax.random.normal(ks[1], (E, D), jnp.float32) * s, 'expert_bias': jax.random.normal(ks[2], (E,), jnp.float32) * s, 'gate_w': jax.random.normal(ks[3], (E, I, D), jnp.float32) * s, 'up_w': jax.random.normal(ks[4], (E, I, D), jnp.float32) * s, 'down_w': jax.random.normal(ks[5], (E, D, I), jnp.float32) * s, 'shared_gate_w': jax.random.normal(ks[6], (NS * I, D), jnp.float32) * s, 'shared_up_w': jax.random.normal(ks[7], (NS * I, D), jnp.float32) * s, 'shared_down_w': jax.random.normal(ks[8], (D, NS * I), jnp.float32) * s}
    _L0_ffn_in = _L0_ffn_setup()
    _d = {'L0_attn_a_x': _L0_attn_a_in['x'], 'L0_attn_a_w_qkv': _L0_attn_a_in['w_qkv'], 'L0_attn_a_w_out': _L0_attn_a_in['w_out'], 'L0_attn_a_ln_scale': _L0_attn_a_in['ln_scale'], 'L0_attn_a_ln_bias': _L0_attn_a_in['ln_bias'], 'L0_attn_b_Wq': _L0_attn_b_in['Wq'], 'L0_attn_b_Wk': _L0_attn_b_in['Wk'], 'L0_attn_b_Wv': _L0_attn_b_in['Wv'], 'L0_attn_b_Wo': _L0_attn_b_in['Wo'], 'L0_ffn_router_w': _L0_ffn_in['router_w'], 'L0_ffn_expert_bias': _L0_ffn_in['expert_bias'], 'L0_ffn_gate_w': _L0_ffn_in['gate_w'], 'L0_ffn_up_w': _L0_ffn_in['up_w'], 'L0_ffn_down_w': _L0_ffn_in['down_w'], 'L0_ffn_shared_gate_w': _L0_ffn_in['shared_gate_w'], 'L0_ffn_shared_up_w': _L0_ffn_in['shared_up_w'], 'L0_ffn_shared_down_w': _L0_ffn_in['shared_down_w']}
    _x0 = _d['L0_attn_a_x']
    _d['L0_attn_a_x'] = jax.random.normal(jax.random.fold_in(jax.random.key(seed), 1), (4, 512, 256), dtype=_x0.dtype)
    del _x0
    return _d

def reference(L0_attn_a_x, L0_attn_a_w_qkv, L0_attn_a_w_out, L0_attn_a_ln_scale, L0_attn_a_ln_bias, L0_attn_b_Wq, L0_attn_b_Wk, L0_attn_b_Wv, L0_attn_b_Wo, L0_ffn_router_w, L0_ffn_expert_bias, L0_ffn_gate_w, L0_ffn_up_w, L0_ffn_down_w, L0_ffn_shared_gate_w, L0_ffn_shared_up_w, L0_ffn_shared_down_w):

    def _L0_attn_a_ref(x, w_qkv, w_out, ln_scale, ln_bias):
        import jax, jax.numpy as jnp
        import numpy as np
        B, N, E, H = (1, 512, 256, 16)
        D = E // H
        DEGREE = 4
        LN_EPS = 1e-05
        ROPE_BASE = 10000.0

        def rope_cos_sin(n, d):
            inv_freq = 1.0 / ROPE_BASE ** (jnp.arange(0, d, 2, dtype=jnp.float32) / d)
            t = jnp.arange(n, dtype=jnp.float32)[:, None] * inv_freq[None, :]
            return (jnp.cos(t), jnp.sin(t))

        def apply_rope(x, cos, sin):
            x1, x2 = jnp.split(x, 2, axis=-1)
            c = cos[None, :, None, :]
            s = sin[None, :, None, :]
            return jnp.concatenate([x1 * c - x2 * s, x1 * s + x2 * c], axis=-1)

        def layernorm(x, scale, bias, eps=LN_EPS):
            m = jnp.mean(x, axis=-1, keepdims=True)
            v = jnp.var(x, axis=-1, keepdims=True)
            return (x - m) * jax.lax.rsqrt(v + eps) * scale + bias

        def polynomial_attention(q, k, v, degree, is_causal):
            a = jnp.einsum('bhnd,bhmd->bhnm', q, k) ** degree
            if is_causal:
                a = jnp.tril(a)
            denom = jnp.sum(a, axis=-1, keepdims=True)
            return jnp.einsum('bhnm,bhmd->bhnd', a / denom, v)
        b, n, e = x.shape
        proj = x @ w_qkv
        q, k, v = jnp.split(proj, 3, axis=-1)
        q = q.reshape(b, n, H, D)
        k = k.reshape(b, n, H, D)
        v = v.reshape(b, n, H, D)
        cos, sin = rope_cos_sin(n, D)
        q = apply_rope(q, cos, sin)
        k = apply_rope(k, cos, sin)
        q = q.transpose(0, 2, 1, 3)
        k = k.transpose(0, 2, 1, 3)
        v = v.transpose(0, 2, 1, 3)
        q = layernorm(q, ln_scale, ln_bias)
        k = layernorm(k, ln_scale, ln_bias)
        out = polynomial_attention(q, k, v, DEGREE, True)
        out = out.transpose(0, 2, 1, 3).reshape(b, n, e)
        out = out @ w_out
        return out

    def _L0_attn_b_ref(x, Wq, Wk, Wv, Wo):
        import jax, jax.numpy as jnp
        import numpy as np
        NH = 16
        B, T, D = x.shape
        hd = D // NH
        q = (x @ Wq.T).reshape(B, T, NH, hd).transpose(0, 2, 1, 3)
        k = (x @ Wk.T).reshape(B, T, NH, hd).transpose(0, 2, 1, 3)
        v = (x @ Wv.T).reshape(B, T, NH, hd).transpose(0, 2, 1, 3)
        att = jnp.einsum('bhtd,bhsd->bhts', q, k) / jnp.sqrt(jnp.asarray(hd, x.dtype))
        neg = jnp.finfo(att.dtype).min
        mask = jnp.triu(jnp.full((T, T), neg, dtype=att.dtype), k=1)
        att = att + mask
        w = jax.nn.softmax(att, axis=-1)
        z = jnp.einsum('bhts,bhsd->bhtd', w, v)
        z = z.transpose(0, 2, 1, 3).reshape(B, T, D)
        return z @ Wo.T

    def _L0_ffn_ref(hidden, router_w, expert_bias, gate_w, up_w, down_w, shared_gate_w, shared_up_w, shared_down_w):
        import jax, jax.numpy as jnp
        import numpy as np
        B, S, D = (2, 256, 256)
        I = 128
        E = 32
        K = 4
        NS = 1
        ALPHA = 7.0

        def _clamped_swiglu(x, wg, wu, wd):
            g = jnp.clip(x @ wg.T, -ALPHA, ALPHA)
            u = jnp.clip(x @ wu.T, -ALPHA, ALPHA)
            return jax.nn.silu(g) * u @ wd.T
        Bb, Ss, Dd = hidden.shape
        flat = hidden.reshape(-1, Dd)
        T = flat.shape[0]
        logits = flat @ router_w.T
        scores = jnp.sqrt(jax.nn.softplus(logits))
        _, idx = jax.lax.top_k(scores + expert_bias, K)
        topv = jnp.take_along_axis(scores, idx, axis=1)
        topv = topv / (topv.sum(axis=-1, keepdims=True) + 1e-20)
        probs = jnp.zeros((T, E), flat.dtype).at[jnp.arange(T)[:, None], idx].set(topv)

        def body(acc, xs):
            wg, wu, wd, p = xs
            return (acc + p[:, None] * _clamped_swiglu(flat, wg, wu, wd), None)
        out, _ = jax.lax.scan(body, jnp.zeros_like(flat), (gate_w, up_w, down_w, probs.T))
        out = out + _clamped_swiglu(flat, shared_gate_w, shared_up_w, shared_down_w)
        return out.reshape(Bb, Ss, Dd)
    x = L0_attn_a_x
    x = x + _L0_attn_a_ref(_layernorm(x, axis=-1), L0_attn_a_w_qkv, L0_attn_a_w_out, L0_attn_a_ln_scale, L0_attn_a_ln_bias)
    x = x + _L0_ffn_ref(_layernorm(x, axis=-1), L0_ffn_router_w, L0_ffn_expert_bias, L0_ffn_gate_w, L0_ffn_up_w, L0_ffn_down_w, L0_ffn_shared_gate_w, L0_ffn_shared_up_w, L0_ffn_shared_down_w)
    x = x + _L0_attn_b_ref(_layernorm(x, axis=-1), L0_attn_b_Wq, L0_attn_b_Wk, L0_attn_b_Wv, L0_attn_b_Wo)
    x = x + _L0_ffn_ref(_layernorm(x, axis=-1), L0_ffn_router_w, L0_ffn_expert_bias, L0_ffn_gate_w, L0_ffn_up_w, L0_ffn_down_w, L0_ffn_shared_gate_w, L0_ffn_shared_up_w, L0_ffn_shared_down_w)
    return x

_drawn_inputs = setup_inputs


def setup_inputs(seed=0):
    import zlib

    import numpy as np

    out = dict(_drawn_inputs(seed))
    spreads = {'L0_attn_a_ln_scale': (1.0, 0.2), 'L0_attn_a_ln_bias': (0.0, 0.1)}
    factors = {'L0_attn_b_Wq': 8.0,
     'L0_attn_b_Wk': 8.0,
     'L0_attn_b_Wv': 3.409,
     'L0_attn_b_Wo': 3.49,
     'L0_ffn_router_w': 5.278,
     'L0_ffn_expert_bias': 8.0,
     'L0_ffn_gate_w': 4.956,
     'L0_ffn_up_w': 4.893,
     'L0_ffn_down_w': 4.903}
    for name, (base, spread) in spreads.items():
        noise = np.random.default_rng([zlib.crc32(name.encode()), seed]).standard_normal(out[name].shape)
        drawn = base * np.exp(spread * noise) if base else spread * noise
        out[name] = jnp.asarray(drawn.astype(out[name].dtype))
    for name, factor in factors.items():
        out[name] = (out[name] * factor).astype(out[name].dtype)
    return out
```

```python
from contextlib import ExitStack

import numpy as np

import concourse.bass as bass
from concourse import mybir

F32 = mybir.dt.float32
BF16 = mybir.dt.bfloat16
I32 = mybir.dt.int32
U32 = mybir.dt.uint32
ALU = mybir.AluOpType
ACT = mybir.ActivationFunctionType
AX = mybir.AxisListType

P = 128
D = 256
NB, T = 4, 512
TJ = T // P
NT = NB * TJ
H, HD = 16, 16
HG = H // 4
QK = 2 * H * HD
EPS = 1e-5
E, I, K = 32, 128, 4
CLIP = 7.0
MASKED = -3.0e38

PARTS = 6
KS = PARTS * HD
Q_PARTS = {"h": (0, 2, 5), "m": (1, 3), "l": (4,)}
K_PARTS = {"h": (0, 1, 4), "m": (2, 3), "l": (5,)}

UNITS = [(0, 0, 0, 256, True), (0, 1, 128, 128, True),
         (1, 0, 0, 256, False), (1, 1, 0, 256, False), (1, 2, 0, 256, True), (1, 3, 128, 128, True)]
NU = len(UNITS)

SLOT = P
REG = T * NB + P
ROW = D + 2 * K
MT = NT * K + E
FAR = float(1 << 17)
NRES = NT * P * K

C_ID, C_LT, C_KEEP, C_MASK, C_MASKT, C_COS, C_SIN, C_IOTA, C_RES = range(9)
C_COLS = [P, P, P, P, P, TJ * HD, TJ * HD, E + 16 + 1 + 1, NT * K]
C_AT = [sum(C_COLS[:i]) for i in range(len(C_COLS) + 1)]


def constants():
    c = np.zeros((P, C_AT[-1]), np.float32)
    p = np.arange(P)[:, None]
    n = np.arange(P)[None, :]
    c[:, C_AT[C_ID]:C_AT[C_ID] + P] = p == n
    c[:, C_AT[C_LT]:C_AT[C_LT] + P] = p < n
    c[:, C_AT[C_KEEP]:C_AT[C_KEEP] + P] = n >= p
    c[:, C_AT[C_MASK]:C_AT[C_MASK] + P] = np.where(n > p, MASKED, 0.0)
    c[:, C_AT[C_MASKT]:C_AT[C_MASKT] + P] = np.where(p > n, MASKED, 0.0)
    inv = (1.0 / 10000.0 ** (np.arange(0, HD, 2, dtype=np.float32) / HD)).astype(np.float32)
    pos = (np.arange(TJ)[None, :] * P + p).astype(np.float32)
    ang = pos[:, :, None] * inv[None, None, :]
    cos, sin = np.cos(ang), np.sin(ang)
    c[:, C_AT[C_COS]:C_AT[C_COS + 1]] = np.concatenate([cos, cos], -1).reshape(P, -1)
    c[:, C_AT[C_SIN]:C_AT[C_SIN + 1]] = np.concatenate([-sin, sin], -1).reshape(P, -1)
    a = C_AT[C_IOTA]
    c[:, a:a + E] = np.arange(E)
    c[:, a + E:a + E + 16] = SLOT * np.arange(16)
    c[:, a + E + 16] = np.arange(P)
    token = np.arange(NT)[None, :, None] * P + np.arange(P)[:, None, None]
    c[:, C_AT[C_RES]:] = (K * token + np.arange(K) - FAR).reshape(P, -1)
    return c


def wait(eng, sem, n):
    if not isinstance(n, int) or n > 0:
        eng.wait_ge(sem, n)


class Count:

    def __init__(self, sem, base=0, per=None):
        self.sem, self.base, self.per, self.n = sem, base, per, 0

    def next(self):
        self.n += 1
        return self.base + self.n

    def close(self):
        assert self.per is None or self.n == self.per, (self.n, self.per)


def attention(nc, sb, rotary, w_qkv, w_out, ln):
    X, ps, const = sb["X"], sb["ps"], sb["const"]
    ident_bf, mask_bf, maskT_bf = sb["ident_bf"], sb["mask_bf"], sb["maskT_bf"]
    keep = const[:, C_AT[C_KEEP]:C_AT[C_KEEP] + P]
    ident = const[:, C_AT[C_ID]:C_AT[C_ID] + P]
    cos = const[:, C_AT[C_COS]:C_AT[C_COS + 1]].rearrange("p (j d) -> p j d", j=TJ)
    sin = const[:, C_AT[C_SIN]:C_AT[C_SIN + 1]].rearrange("p (j d) -> p j d", j=TJ)
    KR = KS if rotary else KS + 3
    tag = "a" if rotary else "b"

    sems = []
    with ExitStack() as ctx:
        def buf(name, shape, dt=F32):
            return ctx.enter_context(nc.sbuf_tensor(f"{name}_{tag}_sb", shape, dt))

        def sem(name):
            sems.append(nc.alloc_semaphore(f"{name}_{tag}"))
            return sems[-1]

        wqkv = buf("wqkv", [P, 2, 3 * D])
        wout = buf("wout", [P, 2, D])
        lnv = buf("lnv", [P, 2, HD])
        stats = buf("stats", [P, TJ, 6])
        mv = buf("mv", [P, TJ, 2])
        rstd = buf("rstd", [P, TJ])
        power = buf("power", [P, 2 * H])
        pad = buf("pad", [P, 1])
        xn = buf("xn", [P, 2, D])
        xT = buf("xT", [P, 2, 2, P])
        qk = buf("qk", [P, TJ, QK])
        tmp = buf("tmp", [P, 2, QK])
        msum = buf("msum", [P, TJ, 2 * H])
        stk = buf("stk", [P, 2, 2, H, KS], BF16)
        Vs = buf("Vs", [P, TJ, H, 32])
        st = buf("st", [KR, 2, H, T], BF16)
        s2 = buf("s2", [P, 2, 4, 256])
        pr = buf("pr", [P, 3, 4, 256])
        oT = buf("oT", [P, 2, 256])
        rec = buf("rec", [P, 8])
        z = buf("z", [P, TJ, D])
        zT = buf("zT", [P, 2, 2, P])
        nm = buf("nm", [P, TJ, H])
        nmr = buf("nmr", [P, TJ, H])
        nms = buf("nms", [P, TJ, P // H, H], BF16)
        nmT = buf("nmT", [3 * H, T], BF16)

        scores = [ps[:, 2 * k:2 * k + 2, :].rearrange("p a (b n) -> p (a b) n", n=256) for k in range(2)]
        stackT = ps[:, 0:4, :].bitcast(BF16)
        oacc = [ps[:, 4 + k, 0:256] for k in range(2)]
        misc = [ps[:, 6 + k, 0:256] for k in range(2)]
        miscb = ps[:, 6, :].bitcast(BF16)
        p_qk = ps[:, 4, :]
        p_v = ps[:, 5, 0:D]
        p_o = [ps[:, 4 + k, 0:D] for k in range(2)]

        w_in = sem("w_in")
        v_ones = sem("v_ones")
        dve_done = sem("dve_done")
        pool_done = sem("pool_done")
        var_ready = sem("var_ready")
        stats_ready, rstd0_ready = sem("stats_ready"), sem("rstd0_ready")
        xn_ready, xT_psum, xT_ready = sem("xn_ready"), sem("xT_psum"), sem("xT_ready")
        qkv_psum, qk_read, v_ready = sem("qkv_psum"), sem("qk_read"), sem("v_ready")
        rot_parts, rotated, centred, squared = sem("rot_parts"), sem("rotated"), sem("centred"), sem("squared")
        rstd_ready, normed, hi_ready, rest_ready = sem("rstd_ready"), sem("normed"), sem("hi_ready"), sem("rest_ready")
        mid_ready, lo_ready, stack_ready = sem("mid_ready"), sem("lo_ready"), sem("stack_ready")
        stQ_psum, stK_psum, stA_ready, stD_ready = sem("stQ_psum"), sem("stK_psum"), sem("stA_ready"), sem("stD_ready")
        s_psum, s_read, s_masked, p_ready, pv_done = (
            sem("s_psum"), sem("s_read"), sem("s_masked"), sem("p_ready"), sem("pv_done"))
        oT_ready, o_psum, o_read = sem("oT_ready"), sem("o_psum"), sem("o_read")
        zT_psum, zT_ready, y_psum, x_added = sem("zT_psum"), sem("zT_ready"), sem("y_psum"), sem("x_added")
        m_psum, m_read, nms_ready, nmT_psum, nmT_ready, max_rows = (
            sem("m_psum"), sem("m_read"), sem("nms_ready"), sem("nmT_psum"), sem("nmT_ready"), sem("max_rows"))
        max_out = sem("max_out")

        NUB = HG * NU
        NMB = TJ * H // 2
        NQ = 2 * HG

        def parts(t, which, s):
            return t[:, which, :, s * HD:(s + 1) * HD]

        def evac_stack(act, b, j):
            act.wait_ge(stQ_psum, TJ * b + j + 1)
            act.activation(st[0:KS, 0, :, j * P:(j + 1) * P],
                           stackT[0:KS, 0:2, :].rearrange("p g (h n) -> p (g h) n", n=P), ACT.Copy).then_inc(stA_ready, 1)

        def evac_out(act, b, c):
            last = NU * (c // 2) + (2 if c % 2 == 0 else NU)
            act.wait_ge(pv_done, NUB * b + last)
            if c >= 2:
                act.wait_ge(o_psum, NQ * b + c - 1)
            act.activation(oT[:, c % 2, :], oacc[c % 2], ACT.Copy).then_inc(oT_ready, 1)

        def weigh(pe, b, g, u, qc, mt, off, w):
            c = 2 * g + qc
            pe.wait_ge(p_ready, NUB * b + u)
            if mt == 0 and c >= 2:
                pe.wait_ge(oT_ready, NQ * b + c - 1)
            last = 1 if qc == 0 else 3
            for i in range(4):
                mm = pe.matmul(oacc[qc][32 * i:32 * i + 32, off:off + w],
                               Vs[:, mt, 4 * g + i, :], pr[:, (u - 1) % 3, i, 0:w],
                               start=(mt == 0), stop=(mt == last), skip_group_check=True)
            mm.then_inc(pv_done, 1)
            if mt == last and c >= 1:
                turn_out(pe, b, c - 1)

        def turn_out(pe, b, c):
            pe.wait_ge(oT_ready, NQ * b + c + 1)
            if c < 2:
                pe.wait_ge(xT_ready, TJ * b + TJ)
                if not rotary:
                    pe.wait_ge(nmT_ready, b + 1)
            else:
                pe.wait_ge(o_read, NQ * b + c - 1)
            for i in range(2):
                mm = pe.transpose(misc[c % 2][:, i * P:(i + 1) * P],
                                  oT[:, c % 2, i * P:(i + 1) * P], ident)
            mm.then_inc(o_psum, 1)

        def rotate(v, b, j):
            v.wait_ge(qkv_psum, TJ * b + j + 1)
            if j >= 2:
                v.wait_ge(rotated, TJ * b + j - 1)
            src = p_qk.rearrange("p (h s d) -> p h s d", s=2, d=HD // 2)
            dst = tmp[:, j % 2, :].rearrange("p (h s d) -> p h s d", s=2, d=HD // 2)
            s8 = sin[:, j, :].rearrange("p (s d) -> p s d", s=2)
            for s in range(2):
                v.tensor_tensor(dst[:, :, s, :], src[:, :, 1 - s, :], s8[:, s:s + 1, :].broadcast_to((P, 2 * H, HD // 2)),
                                ALU.mult)
            v.tensor_tensor(qk[:, j, :].rearrange("p (h d) -> p h d", d=HD), p_qk.rearrange("p (h d) -> p h d", d=HD),
                            cos[:, j:j + 1, :].broadcast_to((P, 2 * H, HD)), ALU.mult).then_inc(rot_parts, 1)

        def normalise(v, b, c, own):
            v.wait_ge(o_psum, NQ * b + c + 1)
            o = misc[c % 2].rearrange("p (i h d) -> p i h d", i=2, d=32)
            wait(v, o_read, NQ * b + c)
            r = rec[:, :].rearrange("p (i h o) -> p i h o", i=2, o=1)
            v.reciprocal(r, o[:, :, :, HD:HD + 1]).then_inc(dve_done, 1)
            v.wait_ge(dve_done, own.next())
            g, qc = c // 2, c % 2
            zz = z[:, 2 * qc:2 * qc + 2, 4 * HD * g:4 * HD * (g + 1)].rearrange("p i (h d) -> p i h d", d=HD)
            v.tensor_tensor(zz, o[:, :, :, 0:HD], r.broadcast_to((P, 2, 4, HD)), ALU.mult).then_inc(o_read, 1)

        block = ctx.enter_context(nc.Block())

        @block.sync
        def _(sp):
            sp.dma_start(wqkv[:, :, :], w_qkv.rearrange("(c p) n -> p c n", p=P)).then_inc(w_in, 16)
            sp.dma_start(wout[:, :, :], w_out.rearrange("(c p) n -> p c n", p=P)).then_inc(w_in, 16)
            sp.dma_start(lnv[:, :, :], ln).then_inc(w_in, 16)
            if not rotary:
                def batch(b):
                    sp.wait_ge(nmT_ready, b + 1)
                    sp.dma_start(sb["max_d"], nmT[:, :]).then_inc(max_out, 16)
                    sp.wait_ge(max_out, 16 * b + 16)
                    sp.dma_start(st[KS:KR, 0, :, :], sb["max_d"].rearrange("(a h) t -> a h t", a=3)).then_inc(max_rows, 16)

                batch(0)
                with sp.Fori(1, NB) as b:
                    batch(b)
                sp.wait_ge(max_rows, 16 * NB)

        @block.gpsimd
        def _(pool):
            pool.memset(power[:, :], -0.5).then_inc(v_ones, 1)
            pool.memset(Vs[:, :, :, HD:HD + 1], 1.0).then_inc(v_ones, 1)
            pool.memset(Vs[:, :, :, HD + 1:32], 0.0).then_inc(v_ones, 1)
            if not rotary:
                pool.memset(nms[:, :, :, :], 0.0).then_inc(v_ones, 1)
                pool.wait_ge(v_ones, 4)
                pool.memset(st[KS:KR, 1, :, :], 1.0).then_inc(v_ones, 1)
            pool.wait_ge(v_ones, 3 if rotary else 5)
            pool.wait_ge(w_in, 48)
            PER = 2 * TJ if rotary else 0
            def batch(b):
                own = Count(pool_done, b * PER, PER)
                pool.wait_ge(stats_ready, b + 1)
                pool.tensor_tensor(rstd[:, :], mv[:, :, 1], power[:, 0:TJ], ALU.pow).then_inc(rstd0_ready, 1)
                if rotary:
                    for j in range(TJ):
                        pool.wait_ge(rot_parts, TJ * b + j + 1)
                        pool.tensor_tensor(qk[:, j, :], qk[:, j, :], tmp[:, j % 2, :], ALU.add).then_inc(rotated, 1)
                    for j in range(TJ):
                        pool.wait_ge(var_ready, TJ * b + j + 1)
                        pool.tensor_tensor(msum[:, j, :], msum[:, j, :], power[:, :], ALU.pow).then_inc(rstd_ready, 1)
                        pool.wait_ge(rstd_ready, TJ * b + j + 1)
                        v = qk[:, j, :].rearrange("p (h d) -> p h d", d=HD)
                        r = msum[:, j, :].rearrange("p (h o) -> p h o", o=1).broadcast_to((P, 2 * H, HD))
                        pool.tensor_tensor(v, v, r, ALU.mult).then_inc(pool_done, 1)
                        pool.wait_ge(pool_done, own.next())
                        g = lnv[:, 0:1, :].broadcast_to((P, 2 * H, HD))
                        pool.tensor_tensor(v, v, g, ALU.mult).then_inc(pool_done, 1)
                        pool.wait_ge(pool_done, own.next())
                        g = lnv[:, 1:2, :].broadcast_to((P, 2 * H, HD))
                        pool.tensor_tensor(v, v, g, ALU.add).then_inc(normed, 1)
                for j in range(TJ):
                    v = qk[:, j, :].rearrange("p (w h d) -> p w h d", w=2, d=HD)
                    pool.wait_ge(hi_ready, TJ * b + j + 1)
                    pool.tensor_tensor(v, v, stk[:, j % 2, :, :, 0:HD], ALU.subtract).then_inc(rest_ready, 1)
                    pool.wait_ge(rest_ready, TJ * b + j + 1)
                    pool.wait_ge(mid_ready, TJ * b + j + 1)
                    for w, at in ((0, Q_PARTS), (1, K_PARTS)):
                        pool.tensor_tensor(parts(stk[:, j % 2], w, at["l"][0]), v[:, w], parts(stk[:, j % 2], w, at["m"][0]),
                                           ALU.subtract).then_inc(lo_ready, 1)
                if rotary:
                    u = 0
                    for g in range(HG):
                        for qc, mt, off, w, diag in UNITS:
                            u += 1
                            if diag:
                                pool.wait_ge(s_read, NUB * b + u)
                                d = s2[:, (u - 1) % 2, :, 0:P]
                                m = keep[:, :].rearrange("p (o n) -> p o n", o=1).broadcast_to((P, 4, P))
                                pool.tensor_tensor(d, d, m, ALU.mult).then_inc(s_masked, 1)

            batch(0)
            with pool.Fori(1, NB) as b:
                batch(b)

        @block.scalar
        def _(act):
            def batch(b):
                for j in range(TJ):
                    act.wait_ge(xT_psum, TJ * b + j + 1)
                    act.activation(xT[:, j % 2], misc[j % 2].rearrange(
                        "p (c n) -> p c n", c=2), ACT.Copy).then_inc(xT_ready, 1)
                    act.wait_ge(qkv_psum, TJ * b + j + 1)
                    if j == 0:
                        act.wait_ge(v_ones, 3)
                        wait(act, pv_done, NUB * b)
                    act.activation(Vs[:, j, :, 0:HD], p_v.rearrange("p (h d) -> p h d", d=HD), ACT.Copy
                                   ).then_inc(v_ready, 1)
                    if not rotary:
                        act.activation(qk[:, j, 0:D], p_qk[:, 0:D], ACT.Copy, scale=HD ** -0.5)
                        act.activation(qk[:, j, D:QK], p_qk[:, D:QK], ACT.Copy).then_inc(qk_read, 1)
                if rotary:
                    act.wait_ge(rotated, TJ * b + TJ)
                    for j in range(TJ):
                        act.wait_ge(centred, TJ * b + j + 1)
                        if j >= 2:
                            act.wait_ge(var_ready, TJ * b + j - 1)
                        act.activation(tmp[:, j % 2, :], qk[:, j, :], ACT.Square).then_inc(squared, 1)
                for j in range(TJ):
                    if rotary:
                        act.wait_ge(normed, TJ * b + j + 1)
                    else:
                        act.wait_ge(qk_read, TJ * b + j + 1)
                    if j >= 2:
                        act.wait_ge(stK_psum, TJ * b + j - 1)
                    v = qk[:, j, :].rearrange("p (w h d) -> p w h d", w=2, d=HD)
                    act.activation(stk[:, j % 2, :, :, 0:HD], v, ACT.Copy).then_inc(hi_ready, 1)
                    act.wait_ge(rest_ready, TJ * b + j + 1)
                    act.activation(parts(stk[:, j % 2], 0, Q_PARTS["m"][0]), v[:, 0], ACT.Copy)
                    act.activation(parts(stk[:, j % 2], 1, K_PARTS["m"][0]), v[:, 1], ACT.Copy).then_inc(mid_ready, 1)
                    if j >= 1:
                        evac_stack(act, b, j - 1)
                evac_stack(act, b, TJ - 1)
                if not rotary:
                    act.wait_ge(nmT_psum, b + 1)
                    act.activation(nmT[:, :], miscb[0:3 * H, 0:T], ACT.Copy).then_inc(nmT_ready, 1)
                u = 0
                for g in range(HG):
                    for qc, mt, off, w, diag in UNITS:
                        u += 1
                        act.wait_ge(s_psum, NUB * b + u)
                        src = scores[(u - 1) % 2][:, :, 0:w]
                        if rotary:
                            if u > 2:
                                act.wait_ge(p_ready, NUB * b + u - 2)
                            act.activation(s2[:, (u - 1) % 2, :, 0:w], src, ACT.Square).then_inc(s_read, 1)
                        else:
                            if u > 3:
                                act.wait_ge(pv_done, NUB * b + u - 3)
                            act.activation(pr[:, (u - 1) % 3, :, 0:w], src, ACT.Exp).then_inc(p_ready, 1)
                        if (u - 1) % NU == 1 and g >= 1:
                            evac_out(act, b, 2 * g - 1)
                        if (u - 1) % NU == 3:
                            evac_out(act, b, 2 * g)
                evac_out(act, b, NQ - 1)
                for j in range(TJ):
                    act.wait_ge(zT_psum, TJ * b + j + 1)
                    act.activation(zT[:, j % 2], misc[j % 2].rearrange(
                        "p (c n) -> p c n", c=2), ACT.Copy).then_inc(zT_ready, 1)

            batch(0)
            with act.Fori(1, NB) as b:
                batch(b)

        @block.tensor
        def _(pe):
            pe.wait_ge(w_in, 48)
            if not rotary:
                pe.wait_ge(v_ones, 5)
            def batch(b):
                for j in range(TJ):
                    pe.wait_ge(xn_ready, TJ * b + j + 1)
                    if j < 2:
                        wait(pe, zT_ready, TJ * b)
                    else:
                        pe.wait_ge(xT_ready, TJ * b + j - 1)
                    for c in range(2):
                        mm = pe.transpose(misc[j % 2][:, c * P:(c + 1) * P],
                                          xn[:, j % 2, c * P:(c + 1) * P], ident)
                    mm.then_inc(xT_psum, 1)
                    pe.wait_ge(xT_ready, TJ * b + j + 1)
                    wait(pe, rot_parts if rotary else qk_read, TJ * b + j)
                    wait(pe, v_ready, TJ * b + j)
                    wait(pe, x_added, TJ * b)
                    for c in range(2):
                        pe.matmul(p_qk, xT[:, j % 2, c, :], wqkv[:, c, 0:QK], start=(c == 0), stop=(c == 1))
                    for c in range(2):
                        mm = pe.matmul(p_v, xT[:, j % 2, c, :], wqkv[:, c, QK:], start=(c == 0), stop=(c == 1))
                    mm.then_inc(qkv_psum, 1)
                for j in range(TJ):
                    pe.wait_ge(stack_ready, TJ * b + j + 1)
                    pe.wait_ge(lo_ready, 2 * (TJ * b + j + 1))
                    if j == 0:
                        wait(pe, s_read if rotary else p_ready, NUB * b)
                    for w, evacuated, done in ((0, stA_ready, stQ_psum), (1, stD_ready, stK_psum)):
                        wait(pe, evacuated, TJ * b + j)
                        for h in range(H):
                            mm = pe.transpose(stackT[0:KS, 2 * w + h // 8, (h % 8) * P:(h % 8 + 1) * P],
                                              stk[:, j % 2, w, h, :], ident_bf[:, :])
                        mm.then_inc(done, 1)
                pe.wait_ge(stA_ready, TJ * b + TJ)
                pe.wait_ge(stD_ready, TJ * b + TJ)
                if not rotary:
                    n = 0
                    for j in range(TJ):
                        for hp in range(H // 2):
                            n += 1
                            if n > 2:
                                pe.wait_ge(m_read, NMB * b + n - 2)
                            for i in range(2):
                                h = 2 * hp + i
                                bank = 2 * ((n - 1) % 2) + i
                                pe.matmul(ps[:, bank, 0:(j + 1) * P], st[0:KS, 0, h, j * P:(j + 1) * P],
                                          st[0:KS, 1, h, 0:(j + 1) * P], start=True, stop=False)
                                mm = pe.matmul(ps[:, bank, j * P:(j + 1) * P], ident_bf[:, :], mask_bf[:, :],
                                               start=False, stop=True)
                            mm.then_inc(m_psum, 1)
                    pe.wait_ge(nms_ready, b + 1)
                    for j in range(TJ):
                        mm = pe.transpose(miscb[:, j * P:(j + 1) * P],
                                          nms[:, j].rearrange("p a h -> p (a h)"), ident_bf[:, :])
                    mm.then_inc(nmT_psum, 1)
                    pe.wait_ge(m_read, NMB * b + NMB)
                    pe.wait_ge(max_rows, 16 * b + 16)
                pe.wait_ge(v_ready, TJ * b + TJ)
                pe.wait_ge(rot_parts if rotary else qk_read, TJ * b + TJ)
                u = 0
                todo = []
                for g in range(HG):
                    for qc, mt, off, w, diag in UNITS:
                        u += 1
                        if u > 2:
                            pe.wait_ge(s_read if rotary else p_ready, NUB * b + u - 2)
                        for i in range(4):
                            h = 4 * g + i
                            masked = diag and not rotary
                            mm = pe.matmul(scores[(u - 1) % 2][:, i, 0:w], st[0:KR, 1, h, mt * P:(mt + 1) * P],
                                           st[0:KR, 0, h, qc * 256 + off:qc * 256 + off + w], start=True, stop=not masked)
                            if masked:
                                mm = pe.matmul(scores[(u - 1) % 2][:, i, 0:P], ident_bf[:, :], maskT_bf[:, :],
                                               start=False, stop=True)
                        mm.then_inc(s_psum, 1)
                        todo.append((g, u, qc, mt, off, w))
                        if len(todo) > 2:
                            weigh(pe, b, *todo.pop(0))
                while todo:
                    weigh(pe, b, *todo.pop(0))
                turn_out(pe, b, NQ - 1)
                for j in range(TJ):
                    pe.wait_ge(o_read, NQ * b + NQ)
                    if j >= 2:
                        pe.wait_ge(zT_ready, TJ * b + j - 1)
                    for c in range(2):
                        mm = pe.transpose(misc[j % 2][:, c * P:(c + 1) * P],
                                          z[:, j, c * P:(c + 1) * P], ident)
                    mm.then_inc(zT_psum, 1)
                    pe.wait_ge(zT_ready, TJ * b + j + 1)
                    if j >= 2:
                        pe.wait_ge(x_added, TJ * b + j - 1)
                    for c in range(2):
                        mm = pe.matmul(p_o[j % 2], zT[:, j % 2, c, :], wout[:, c, :], start=(c == 0), stop=(c == 1))
                    mm.then_inc(y_psum, 1)

            batch(0)
            with pe.Fori(1, NB) as b:
                batch(b)

        @block.vector
        def _(v):
            PER = 2 * TJ + NQ + (2 * TJ if rotary else 3)
            def batch(b):
                own = Count(dve_done, b * PER, PER)
                xs = [X[:, bass.ds(TJ * b + j, 1), :].rearrange("p o d -> p (o d)") for j in range(TJ)]
                wait(v, x_added, TJ * b)
                for j in range(TJ):
                    v.bn_stats(stats[:, j, :], xs[j]).then_inc(dve_done, 1)
                    own.next()
                v.wait_ge(dve_done, own.base + own.n)
                v.memset(pad[:, :], 0.0)
                for j in range(TJ):
                    v.bn_aggr(mv[:, j, :], stats[:, j, :]).then_inc(dve_done, 1)
                    own.next()
                v.wait_ge(dve_done, own.base + own.n)
                v.tensor_scalar(mv[:, :, 1], mv[:, :, 1], EPS, None, ALU.add).then_inc(stats_ready, 1)
                for j in range(TJ):
                    v.wait_ge(rstd0_ready, b + 1)
                    if j >= 2:
                        v.wait_ge(xT_psum, TJ * b + j - 1)
                    v.tensor_scalar(xn[:, j % 2, :], xs[j], mv[:, j, 0:1], rstd[:, j:j + 1], ALU.subtract, ALU.mult
                                    ).then_inc(xn_ready, 1)
                    if rotary:
                        if j >= 1:
                            rotate(v, b, j - 1)
                if rotary:
                    rotate(v, b, TJ - 1)
                    for j in range(TJ):
                        hv = qk[:, j, :].rearrange("p (h d) -> p h d", d=HD)
                        v.wait_ge(rotated, TJ * b + j + 1)
                        v.tensor_reduce(msum[:, j, :], hv, AX.X, ALU.add).then_inc(dve_done, 1)
                        v.wait_ge(dve_done, own.next())
                        m = msum[:, j, :].rearrange("p (h o) -> p h o", o=1).broadcast_to((P, 2 * H, HD))
                        v.scalar_tensor_tensor(out=hv, in0=m, scalar=-1.0 / HD, in1=hv, op0=ALU.mult, op1=ALU.add
                                               ).then_inc(centred, 1)
                    for j in range(TJ):
                        v.wait_ge(squared, TJ * b + j + 1)
                        v.wait_ge(centred, TJ * b + j + 1)
                        v.tensor_reduce(msum[:, j, :], tmp[:, j % 2, :].rearrange("p (h d) -> p h d", d=HD),
                                        AX.X, ALU.add).then_inc(dve_done, 1)
                        v.wait_ge(dve_done, own.next())
                        v.tensor_scalar(msum[:, j, :], msum[:, j, :], 1.0 / HD, EPS, ALU.mult, ALU.add
                                        ).then_inc(var_ready, 1)
                for j in range(TJ):
                    v.wait_ge(hi_ready, TJ * b + j + 1)
                    v.wait_ge(mid_ready, TJ * b + j + 1)
                    for w, at in ((0, Q_PARTS), (1, K_PARTS)):
                        for p in "hm":
                            for s in at[p][1:]:
                                last = v.tensor_copy(parts(stk[:, j % 2], w, s), parts(stk[:, j % 2], w, at[p][0]))
                    last.then_inc(stack_ready, 1)
                    v.wait_ge(stK_psum, TJ * b + j + 1)
                    v.tensor_copy(st[0:KS, 1, :, j * P:(j + 1) * P],
                                  stackT[0:KS, 2:4, :].rearrange("p g (h n) -> p (g h) n", n=P)).then_inc(stD_ready, 1)
                if not rotary:
                    n = 0
                    for j in range(TJ):
                        for hp in range(H // 2):
                            n += 1
                            v.wait_ge(m_psum, NMB * b + n)
                            bank = 2 * ((n - 1) % 2)
                            v.tensor_reduce(nm[:, j, 2 * hp:2 * hp + 2], ps[:, bank:bank + 2, 0:(j + 1) * P],
                                            AX.X, ALU.max, negate=True).then_inc(m_read, 1)
                    v.wait_ge(m_read, NMB * b + NMB)
                    v.tensor_copy(nms[:, :, 0, :], nm[:, :, :]).then_inc(dve_done, 1)
                    v.wait_ge(dve_done, own.next())
                    v.tensor_tensor(nmr[:, :, :], nm[:, :, :], nms[:, :, 0, :], ALU.subtract).then_inc(dve_done, 1)
                    v.wait_ge(dve_done, own.next())
                    v.tensor_copy(nms[:, :, 1, :], nmr[:, :, :]).then_inc(dve_done, 1)
                    v.wait_ge(dve_done, own.next())
                    v.tensor_tensor(nms[:, :, 2, :], nmr[:, :, :], nms[:, :, 1, :], ALU.subtract).then_inc(nms_ready, 1)
                u = diags = 0
                for g in range(HG):
                    for n, (qc, mt, off, w, diag) in enumerate(UNITS):
                        u += 1
                        if rotary:
                            v.wait_ge(s_read, NUB * b + u)
                            if diag:
                                diags += 1
                                v.wait_ge(s_masked, 4 * HG * b + diags)
                            if u > 3:
                                v.wait_ge(pv_done, NUB * b + u - 3)
                            s = s2[:, (u - 1) % 2, :, 0:w]
                            v.tensor_tensor(pr[:, (u - 1) % 3, :, 0:w], s, s, ALU.mult).then_inc(p_ready, 1)
                        if n in (1, 3) and g >= 1:
                            normalise(v, b, 2 * g - 2 + n // 2, own)
                normalise(v, b, NQ - 2, own)
                normalise(v, b, NQ - 1, own)
                for j in range(TJ):
                    v.wait_ge(y_psum, TJ * b + j + 1)
                    x = X[:, bass.ds(TJ * b + j, 1), :].rearrange("p o d -> p (o d)")
                    v.tensor_tensor(x, x, p_o[j % 2], ALU.add).then_inc(x_added, 1)
                own.close()

            batch(0)
            with v.Fori(1, NB) as b:
                batch(b)
    return sems


def experts(nc, sb, xs_d, y_d, down_d, tag):
    X, ps, const, Wgu = sb["X"], sb["ps"], sb["const"], sb["Wgu"]
    before_bf, ones_bf = sb["before_bf"], sb["ones_bf"]
    ident = const[:, C_AT[C_ID]:C_AT[C_ID] + P]
    io = C_AT[C_IOTA]
    iota_e, steps, iota_p = const[:, io:io + E], const[:, io + E:io + E + 16], const[:, io + E + 16:io + E + 17]
    res_c = const[:, C_AT[C_RES]:].rearrange("p (t k) -> p t k", k=K)
    RING = 4
    CLS = bass.IndirectOffsetOnAxis

    sems = []
    with ExitStack() as ctx:
        def buf(name, shape, dt=F32):
            return ctx.enter_context(nc.sbuf_tensor(f"{name}_{tag}_sb", shape, dt))

        def sem(name):
            sems.append(nc.alloc_semaphore(f"{name}_{tag}"))
            return sems[-1]

        Wd = buf("Wd", [P, E + 1, D])
        stats, mv, rstd = buf("stats", [P, TJ, 6]), buf("mv", [P, TJ, 2]), buf("rstd", [P, TJ])
        power, root = buf("power", [P, TJ]), buf("root", [P, TJ * E])
        pad, padp = buf("pad", [P, 1]), buf("padp", [P, 1])
        rows = buf("rows", [P, 2, TJ, ROW])
        xT = buf("xT", [P, 2, 2, P])
        gu, sg, h, hT = buf("gu", [P, 2, 2 * I]), buf("sg", [P, 2, I]), buf("h", [P, 2, I]), buf("hT", [P, 2, P])
        mag, ex, lg1, sp = (buf(n, [P, TJ * E]) for n in ("mag", "ex", "lg1", "sp"))
        score, biased = buf("score", [P, TJ, E]), buf("biased", [P, TJ, E])
        top = buf("top", [P, TJ, 8])
        topi = buf("topi", [P, TJ, 8], U32)
        topf = buf("topf", [P, TJ, K])
        hot, prod = buf("hot", [P, TJ, K, E]), buf("prod", [P, TJ, K, E])
        mask = buf("mask", [P, TJ, E], BF16)
        place, place0 = buf("place", [P, TJ, E]), buf("place0", [P, E])
        count, base = buf("count", [P, E]), buf("base", [P, E])
        picked, total, posf = buf("picked", [P, TJ, K]), buf("total", [P, TJ]), buf("posf", [P, TJ, K])
        posi = buf("posi", [P, 2, TJ, K], I32)
        weight = buf("weight", [P, NT, K])
        dummy = buf("dummy", [P, ROW])
        many = buf("many", [P, E, 16])
        tiles_e, ends, starts, one_e = (buf(n, [P, E]) for n in ("tiles_e", "ends", "starts", "one_e"))
        hot_e = buf("hot_e", [P, E])
        meta = buf("meta", [P, 8])
        diag, ones = buf("diag", [P, P]), buf("ones", [P, P])
        tile_e = buf("tile_e", [P, P])
        plan = buf("plan", [1, 2, P], I32)
        tails = buf("tails", [1, E], I32)
        xs = buf("xs", [P, RING, ROW])
        ys = buf("ys", [P, RING, D])
        toi = buf("toi", [P, RING], I32)
        tof = buf("tof", [P, RING])
        to4 = buf("to4", [P, RING, K])
        yk = buf("yk", [P, RING, K, D])
        router = buf("router", [P, 2, E])
        bias = buf("bias", [P, E])

        p_logit = ps[:, 0, 0:TJ * E]
        p_rank = ps[:, 1, 0:TJ * E]
        p_total = ps[:, 1, TJ * E:(TJ + 1) * E]
        p_gu = [ps[:, 2 + k, 0:2 * I] for k in range(2)]
        p_y = [ps[:, 4 + k, 0:D] for k in range(2)]
        p_xT = [ps[:, 6 + k, 0:D] for k in range(2)]
        p_hT = [ps[:, k, 0:P] for k in range(2)]

        w_in, wd_in, set_up = sem("w_in"), sem("wd_in"), sem("set_up")
        dve_done, stats_ready, rstd_ready, xn_ready = sem("dve_done"), sem("stats_ready"), sem("rstd_ready"), sem("xn_ready")
        xT_psum, xT_ready, gu_psum, clipped = sem("xT_psum"), sem("xT_ready"), sem("gu_psum"), sem("clipped")
        sig_ready, h_ready, hT_psum, hT_ready = sem("sig_ready"), sem("h_ready"), sem("hT_psum"), sem("hT_ready")
        y_psum, x_added = sem("y_psum"), sem("x_added")
        logit_psum, mag_ready, ex_ready, plus1, ln_ready = (
            sem("logit_psum"), sem("mag_ready"), sem("ex_ready"), sem("plus1"), sem("ln_ready"))
        soft_ready, score_ready, mask_ready, rank_psum, pos_ready = (
            sem("soft_ready"), sem("score_ready"), sem("mask_ready"), sem("rank_psum"), sem("pos_ready"))
        sent = [sem(f"sent{k}") for k in range(2)]
        dummy_ready, meta_ready, plan_psum, plan_ready, tails_in = (
            sem("dummy_ready"), sem("meta_ready"), sem("plan_psum"), sem("plan_ready"), sem("tails_in"))
        loaded = [sem(f"loaded{k}") for k in range(RING)]
        stored = [sem(f"stored{k}") for k in range(RING)]
        t_xT_psum, t_xT, t_gu_psum, t_clip = sem("t_xT_psum"), sem("t_xT"), sem("t_gu_psum"), sem("t_clip")
        t_sig, t_h, t_hT_psum, t_hT = sem("t_sig"), sem("t_h"), sem("t_hT_psum"), sem("t_hT")
        t_y_psum, t_y, t_to, t_acc = sem("t_y_psum"), sem("t_y"), sem("t_to"), sem("t_acc")
        back = [sem(f"back{k}") for k in range(RING)]
        summed = sem("summed")

        def turns(eng, step, n_lag):
            for g in range(2):
                for u in range(RING):
                    step(eng, g, u)
            with eng.Fori(2, MT // RING) as g:
                for u in range(RING):
                    step(eng, g, u)
            for u in range(n_lag):
                step(eng, MT // RING, u)

        def at(g, u, lag):
            i = RING * g + (u - lag)
            if isinstance(g, int) and not 0 <= i < MT:
                return None
            return i, (u - lag) % RING, g + (u - lag) // RING

        L_CLIP = 0
        L_H, L_TH, L_DOWN = 1, 2, 3

        def sp_step(sp, g, u):
            i, q, turn = at(g, u, 0)
            row = sp.value_load(plan[0:1, 1, bass.ds(i, 1)], min_val=0, max_val=E * REG)
            if not isinstance(g, int) or g >= 1:
                sp.wait_ge(t_xT_psum, i - RING + 1)
                sp.wait_ge(t_acc, i - RING + 1)
            sp.dma_start(xs[:, q, :], xs_d[bass.ds(row, P), :]).then_inc(loaded[q], 16)

        def pe_step(pe, g, u):
            a = at(g, u, 0)
            if a:
                i, q, turn = a
                pe.wait_ge(loaded[q], 16 * (turn + 1))
                if not isinstance(i, int) or i >= 2:
                    pe.wait_ge(t_xT, i - 1)
                for c in range(2):
                    mm = pe.transpose(p_xT[q % 2][:, c * P:(c + 1) * P], xs[:, q, c * P:(c + 1) * P], ident)
                mm.then_inc(t_xT_psum, 1)
            a = at(g, u, L_TH)
            if a:
                i, q, turn = a
                pe.wait_ge(t_h, i + 1)
                if not isinstance(i, int) or i >= 2:
                    pe.wait_ge(t_hT, i - 1)
                pe.transpose(p_hT[q % 2], h[:, q % 2, :], ident).then_inc(t_hT_psum, 1)
            a = at(g, u, 0)
            if a:
                i, q, turn = a
                e = pe.value_load(plan[0:1, 0, bass.ds(i, 1)], min_val=0, max_val=E - 1)
                pe.wait_ge(t_xT, i + 1)
                if not isinstance(i, int) or i >= 2:
                    pe.wait_ge(t_clip, i - 1)
                for c in range(2):
                    mm = pe.matmul(p_gu[q % 2], xT[:, q % 2, c, :],
                                   Wgu[:, c, bass.ds(e, 1), :].rearrange("p o n -> p (o n)"), start=(c == 0), stop=(c == 1))
                mm.then_inc(t_gu_psum, 1)
            a = at(g, u, L_DOWN)
            if a:
                i, q, turn = a
                e = pe.value_load(plan[0:1, 0, bass.ds(i, 1)], min_val=0, max_val=E - 1)
                pe.wait_ge(t_hT, i + 1)
                if not isinstance(i, int) or i >= 2:
                    pe.wait_ge(t_y, i - 1)
                pe.matmul(p_y[q % 2], hT[:, q % 2, :], Wd[:, bass.ds(e, 1), :].rearrange("p o n -> p (o n)"),
                          start=True, stop=True).then_inc(t_y_psum, 1)

        def act_step(act, g, u):
            a = at(g, u, 0)
            if a:
                i, q, turn = a
                act.wait_ge(t_xT_psum, i + 1)
                if not isinstance(i, int) or i >= 2:
                    act.wait_ge(t_gu_psum, i - 1)
                act.activation(xT[:, q % 2], p_xT[q % 2].rearrange("p (c n) -> p c n", c=2), ACT.Copy).then_inc(t_xT, 1)
            a = at(g, u, L_TH)
            if a:
                i, q, turn = a
                act.wait_ge(t_hT_psum, i + 1)
                if not isinstance(i, int) or i >= 2:
                    act.wait_ge(t_y_psum, i - 1)
                act.activation(hT[:, q % 2, :], p_hT[q % 2], ACT.Copy).then_inc(t_hT, 1)
            a = at(g, u, 0)
            if a:
                i, q, turn = a
                act.wait_ge(t_clip, i + 1)
                if not isinstance(i, int) or i >= 2:
                    act.wait_ge(t_h, i - 1)
                act.activation(sg[:, q % 2, :], gu[:, q % 2, 0:I], ACT.Sigmoid).then_inc(t_sig, 1)

        def dve_step(v, g, u):
            a = at(g, u, L_CLIP)
            if a:
                i, q, turn = a
                v.wait_ge(t_gu_psum, i + 1)
                if not isinstance(i, int) or i >= 2:
                    v.wait_ge(t_h, i - 1)
                v.tensor_scalar(gu[:, q % 2, :], p_gu[q % 2], CLIP, -CLIP, ALU.min, ALU.max).then_inc(t_clip, 1)
                v.wait_ge(loaded[q], 16 * (turn + 1))
                if not isinstance(i, int) or i >= RING:
                    v.wait_ge(stored[q], 16 * turn)
                v.scalar_tensor_tensor(out=to4[:, q, :], in0=xs[:, q, D:D + K], scalar=tile_e[:, bass.ds(i, 1)],
                                       in1=xs[:, q, D + K:ROW], op0=ALU.is_equal, op1=ALU.mult,
                                       accum_out=tof[:, q:q + 1]).then_inc(t_acc, 1)
                v.wait_ge(t_acc, i + 1)
                v.tensor_scalar(toi[:, q:q + 1], tof[:, q:q + 1], FAR, None, ALU.add).then_inc(t_to, 1)
            a = at(g, u, L_H)
            if a:
                i, q, turn = a
                v.wait_ge(t_sig, i + 1)
                if not isinstance(i, int) or i >= 2:
                    v.wait_ge(t_hT_psum, i - 1)
                v.tensor_tensor(sg[:, q % 2, :], sg[:, q % 2, :], gu[:, q % 2, 0:I], ALU.mult).then_inc(t_gs, 1)
                v.wait_ge(t_gs, i + 1)
                v.tensor_tensor(h[:, q % 2, :], sg[:, q % 2, :], gu[:, q % 2, I:], ALU.mult).then_inc(t_h, 1)
            a = at(g, u, L_DOWN)
            if a:
                i, q, turn = a
                v.wait_ge(t_y_psum, i + 1)
                if not isinstance(i, int) or i >= RING:
                    v.wait_ge(stored[q], 16 * turn)
                v.tensor_copy(ys[:, q, :], p_y[q % 2]).then_inc(t_y, 1)

        def absorb(pool, n):
            wait(pool, absorbed, n)
            pool.tensor_tensor(padp[:, :], base[:, 0:1], base[:, 0:1], ALU.add).then_inc(absorbed, 1)

        def pool_step(pool, g, u):
            a = at(g, u, L_DOWN)
            if a:
                i, q, turn = a
                pool.wait_ge(t_to, i + 1)
                pool.wait_ge(t_y, i + 1)
                absorb(pool, NB + i)
                pool.indirect_dma_start(y_d, CLS(ap=toi[:, q:q + 1], axis=0), ys[:, q, :], None,
                                        bounds_check=NRES - 1, oob_is_err=False).then_inc(stored[q], 16)

        absorbed, t_gs, h_half, planned, part_sum = sem("absorbed"), sem("t_gs"), sem("h_half"), sem("planned"), sem("part_sum")
        block = ctx.enter_context(nc.Block())

        @block.sync
        def _(sp):
            sp.dma_start(router[:, :, :], sb["router_d"].rearrange("(c p) n -> p c n", p=P)).then_inc(w_in, 16)
            sp.dma_start(bias[:, :], sb["bias_d"]).then_inc(w_in, 16)
            sp.dma_start(Wd[:, :, :], down_d).then_inc(wd_in, 16)
            sp.wait_ge(dummy_ready, 4)
            sp.dma_start(xs_d[E * REG:E * REG + P, :], dummy[:, :]).then_inc(tails_in, 16)
            sp.wait_ge(plan_ready, 3)
            with sp.Fori(0, E) as e:
                row = sp.value_load(tails[0:1, bass.ds(e, 1)], min_val=0, max_val=E * REG)
                sp.dma_start(xs_d[bass.ds(row, P), :], dummy[:, :]).then_inc(tails_in, 16)
            sp.wait_ge(tails_in, 16 * (E + 1))
            for k in range(2):
                sp.wait_ge(sent[k], 16 * NT * K // 2)
            turns(sp, sp_step, 0)
            for q in range(RING):
                sp.wait_ge(stored[q], 16 * MT // RING)
            y_v = y_d.rearrange("(t p k) d -> p t (k d)", p=P, k=K)
            def four_tiles(g):
                for q in range(RING):
                    wait(sp, summed, RING * g)
                    sp.dma_start(yk[:, q], y_v[:, bass.ds(RING * g + q, 1), :]).then_inc(back[q], 16)

            four_tiles(0)
            with sp.Fori(1, NT // RING) as g:
                four_tiles(g)

        @block.gpsimd
        def _(pool):
            pool.memset(power[:, :], -0.5).then_inc(set_up, 1)
            pool.memset(root[:, :], 0.5).then_inc(set_up, 1)
            pool.memset(ones[:, :], 1.0).then_inc(set_up, 1)
            pool.memset(one_e[:, :], 1.0).then_inc(set_up, 1)
            pool.memset(count[:, :], 0.0).then_inc(set_up, 1)
            pool.memset(dummy[:, 0:D], 0.0).then_inc(dummy_ready, 1)
            pool.memset(dummy[:, D:D + K], -1.0).then_inc(dummy_ready, 1)
            pool.memset(dummy[:, D + K:ROW], 0.0).then_inc(dummy_ready, 1)
            pool.tensor_scalar(base[:, :], iota_e, float(REG), None, ALU.mult).then_inc(dummy_ready, 1)
            pool.wait_ge(set_up, 5)
            pool.wait_ge(dummy_ready, 4)
            def two_batches(b2):
                for bb in range(2):
                    b = 2 * b2 + bb
                    pool.wait_ge(stats_ready, b + 1)
                    pool.tensor_tensor(rstd[:, :], mv[:, :, 1], power[:, :], ALU.pow).then_inc(rstd_ready, 1)
                    pool.wait_ge(soft_ready, b + 1)
                    pool.tensor_tensor(score[:, :, :].rearrange("p t e -> p (t e)"), sp[:, :], root[:, :], ALU.pow
                                       ).then_inc(score_ready, 1)
                    pool.wait_ge(pos_ready, b + 1)
                    absorb(pool, b)
                    for j in range(TJ):
                        for k in range(K):
                            pool.indirect_dma_start(xs_d, CLS(ap=posi[:, bb, j, k:k + 1], axis=0), rows[:, bb, j, :],
                                                    None).then_inc(sent[bb], 16)

            two_batches(0)
            with pool.Fori(1, NB // 2) as b2:
                two_batches(b2)
            turns(pool, pool_step, L_DOWN)
            for q in range(RING):
                pool.wait_ge(stored[q], 16 * MT // RING)

        @block.scalar
        def _(act):
            def batch(b):
                for j in range(TJ):
                    n = TJ * b + j
                    act.wait_ge(xT_psum, n + 1)
                    act.activation(xT[:, j % 2], p_xT[0].rearrange("p (c n) -> p c n", c=2), ACT.Copy).then_inc(xT_ready, 1)
                    act.wait_ge(clipped, n + 1)
                    act.activation(sg[:, j % 2, :], gu[:, j % 2, 0:I], ACT.Sigmoid).then_inc(sig_ready, 1)
                    act.wait_ge(hT_psum, n + 1)
                    act.activation(hT[:, j % 2, :], p_xT[1][:, 0:P], ACT.Copy).then_inc(hT_ready, 1)
                act.wait_ge(logit_psum, b + 1)
                act.activation(mag[:, :], p_logit, ACT.Abs).then_inc(mag_ready, 1)
                act.wait_ge(mag_ready, b + 1)
                act.activation(ex[:, :], mag[:, :], ACT.Exp, scale=-1.0).then_inc(ex_ready, 1)
                act.wait_ge(plus1, b + 1)
                act.activation(lg1[:, :], sp[:, :], ACT.Ln).then_inc(ln_ready, 1)

            batch(0)
            with act.Fori(1, NB) as b:
                batch(b)
            turns(act, act_step, L_DOWN)

        @block.tensor
        def _(pe):
            pe.wait_ge(w_in, 32)
            pe.wait_ge(sb["wgu_in"], 16)
            pe.wait_ge(wd_in, 16)
            def two_batches(b2):
                for bb in range(2):
                    b = 2 * b2 + bb
                    for j in range(TJ):
                        n = TJ * b + j
                        pe.wait_ge(xn_ready, n + 1)
                        wait(pe, xT_ready, n)
                        for c in range(2):
                            mm = pe.transpose(p_xT[0][:, c * P:(c + 1) * P], rows[:, bb, j, c * P:(c + 1) * P], ident)
                        mm.then_inc(xT_psum, 1)
                        pe.wait_ge(xT_ready, n + 1)
                        if j == 0:
                            wait(pe, soft_ready, b)
                        for c in range(2):
                            mm = pe.matmul(p_logit[:, j * E:(j + 1) * E], xT[:, j % 2, c, :], router[:, c, :],
                                           start=(c == 0), stop=(c == 1))
                        if j == TJ - 1:
                            mm.then_inc(logit_psum, 1)
                        wait(pe, clipped, n)
                        for c in range(2):
                            mm = pe.matmul(p_gu[j % 2], xT[:, j % 2, c, :], Wgu[:, c, E, :], start=(c == 0), stop=(c == 1))
                        mm.then_inc(gu_psum, 1)
                        pe.wait_ge(h_ready, n + 1)
                        wait(pe, hT_ready, n)
                        pe.transpose(p_xT[1][:, 0:P], h[:, j % 2, :], ident).then_inc(hT_psum, 1)
                        pe.wait_ge(hT_ready, n + 1)
                        wait(pe, x_added, n)
                        pe.matmul(p_y[j % 2], hT[:, j % 2, :], Wd[:, E, :], start=True, stop=True).then_inc(y_psum, 1)
                    pe.wait_ge(mask_ready, b + 1)
                    pe.matmul(p_rank, before_bf[:, :], mask[:, :, :].rearrange("p t e -> p (t e)"),
                              start=True, stop=False, skip_group_check=True)
                    for j in range(TJ - 1):
                        pe.matmul(p_rank[:, (j + 1) * E:].rearrange("p (t e) -> p t e", e=E), ones_bf[:, :],
                                  mask[:, j:j + 1, :].broadcast_to((P, TJ - 1 - j, E)), start=False, stop=False,
                                  skip_group_check=True)
                    for j in range(TJ):
                        mm = pe.matmul(p_total, ones_bf[:, :], mask[:, j, :], start=False, stop=(j == TJ - 1),
                                       skip_group_check=True)
                    mm.then_inc(rank_psum, 1)

            two_batches(0)
            with pe.Fori(1, NB // 2) as b2:
                two_batches(b2)
            pe.wait_ge(meta_ready, 1)
            pe.matmul(ps[0:1, 0, 0:P], meta[:, 6:7], ident, start=True, stop=True)
            pe.matmul(ps[0:1, 0, P:2 * P], meta[:, 5:6], ident, start=True, stop=True)
            pe.matmul(ps[:, 1, 0:P], ones[:, :], diag[:, :], start=True, stop=True).then_inc(plan_psum, 1)
            pe.wait_ge(plan_ready, 3)
            turns(pe, pe_step, L_DOWN)

        @block.vector
        def _(v):
            v.wait_ge(w_in, 32)
            v.wait_ge(set_up, 5)
            v.wait_ge(dummy_ready, 4)
            PER = 2 * TJ + 20
            def two_batches(b2):
                for bb in range(2):
                    b = 2 * b2 + bb
                    own = Count(dve_done, b * PER, PER)

                    def then(ins):
                        ins.then_inc(dve_done, 1)
                        v.wait_ge(dve_done, own.next())

                    x4 = [X[:, bass.ds(TJ * b + j, 1), :].rearrange("p o d -> p (o d)") for j in range(TJ)]
                    for j in range(TJ):
                        v.bn_stats(stats[:, j, :], x4[j]).then_inc(dve_done, 1)
                        own.next()
                    v.wait_ge(dve_done, own.base + own.n)
                    v.memset(pad[:, :], 0.0)
                    for j in range(TJ):
                        v.bn_aggr(mv[:, j, :], stats[:, j, :]).then_inc(dve_done, 1)
                        own.next()
                    v.wait_ge(dve_done, own.base + own.n)
                    v.tensor_scalar(mv[:, :, 1], mv[:, :, 1], EPS, None, ALU.add).then_inc(stats_ready, 1)
                    v.wait_ge(rstd_ready, b + 1)
                    wait(v, sent[bb], 16 * TJ * K * b2)
                    for j in range(TJ):
                        v.tensor_scalar(rows[:, bb, j, 0:D], x4[j], mv[:, j, 0:1], rstd[:, j:j + 1],
                                        ALU.subtract, ALU.mult).then_inc(xn_ready, 1)
                    for j in range(TJ):
                        n = TJ * b + j
                        v.wait_ge(gu_psum, n + 1)
                        v.tensor_scalar(gu[:, j % 2, :], p_gu[j % 2], CLIP, -CLIP, ALU.min, ALU.max).then_inc(clipped, 1)
                        v.wait_ge(sig_ready, n + 1)
                        v.tensor_tensor(sg[:, j % 2, :], sg[:, j % 2, :], gu[:, j % 2, 0:I], ALU.mult).then_inc(h_half, 1)
                        v.wait_ge(h_half, n + 1)
                        v.tensor_tensor(h[:, j % 2, :], sg[:, j % 2, :], gu[:, j % 2, I:], ALU.mult).then_inc(h_ready, 1)
                        v.wait_ge(y_psum, n + 1)
                        v.wait_ge(xn_ready, TJ * b + TJ)
                        v.tensor_tensor(x4[j], x4[j], p_y[j % 2], ALU.add).then_inc(x_added, 1)
                    v.wait_ge(ex_ready, b + 1)
                    v.tensor_scalar(sp[:, :], ex[:, :], 1.0, None, ALU.add).then_inc(plus1, 1)
                    v.wait_ge(plus1, b + 1)
                    then(v.scalar_tensor_tensor(out=ex[:, :], in0=sp[:, :], scalar=1.0, in1=ex[:, :],
                                                op0=ALU.subtract, op1=ALU.subtract))
                    v.wait_ge(ln_ready, b + 1)
                    then(v.tensor_tensor(ex[:, :], lg1[:, :], ex[:, :], ALU.subtract))
                    v.scalar_tensor_tensor(out=sp[:, :], in0=p_logit, scalar=0.0, in1=ex[:, :],
                                           op0=ALU.max, op1=ALU.add).then_inc(soft_ready, 1)
                    v.wait_ge(score_ready, b + 1)
                    b4 = bias[:, :].rearrange("p (o e) -> p o e", o=1).broadcast_to((P, TJ, E))
                    then(v.tensor_tensor(biased[:, :, :], score[:, :, :], b4, ALU.add))
                    v.memset(pad[:, :], 0.0)
                    for j in range(TJ):
                        last = v.max(top[:, j, :], biased[:, j, :])
                    then(last)
                    v.memset(pad[:, :], 0.0)
                    for j in range(TJ):
                        last = v.max_index(topi[:, j, :], top[:, j, :], biased[:, j, :])
                    then(last)
                    then(v.tensor_copy(topf[:, :, :], topi[:, :, 0:K]))
                    for j in range(TJ):
                        it = iota_e.rearrange("p (o e) -> p o e", o=1).broadcast_to((P, K, E))
                        tk = topf[:, j, :].rearrange("p (k o) -> p k o", o=1).broadcast_to((P, K, E))
                        last = v.tensor_tensor(hot[:, j], it, tk, ALU.is_equal)
                    then(last)
                    with nc.allow_low_precision(reason="zeros and ones, exact in bf16"):
                        v.tensor_reduce(mask[:, :, :], hot[:, :, :, :].rearrange("p t k e -> p t e k"), AX.X, ALU.add
                                        ).then_inc(mask_ready, 1)
                    sk = [score[:, j:j + 1, :].broadcast_to((P, K, E)) for j in range(TJ)]
                    for j in range(TJ):
                        last = v.tensor_tensor(prod[:, j], hot[:, j], sk[j], ALU.mult)
                    then(last)
                    then(v.tensor_reduce(picked[:, :, :], prod[:, :, :, :], AX.X, ALU.add))
                    then(v.tensor_reduce(total[:, :], picked[:, :, :], AX.X, ALU.add))
                    then(v.tensor_scalar(total[:, :], total[:, :], 1e-20, None, ALU.add))
                    then(v.reciprocal(total[:, :], total[:, :]))
                    then(v.tensor_tensor(weight[:, bass.ds(TJ * b, TJ), :], picked[:, :, :],
                                         total[:, :].rearrange("p (t o) -> p t o", o=1).broadcast_to((P, TJ, K)), ALU.mult))
                    v.wait_ge(rank_psum, b + 1)
                    c4 = place0[:, :].rearrange("p (o e) -> p o e", o=1).broadcast_to((P, TJ, E))
                    then(v.tensor_tensor(place0[:, :], base[:, :], count[:, :], ALU.add))
                    then(v.tensor_tensor(place[:, :, :], p_rank.rearrange("p (t e) -> p t e", e=E), c4, ALU.add))
                    then(v.tensor_tensor(count[:, :], count[:, :], p_total, ALU.add))
                    for j in range(TJ):
                        last = v.tensor_tensor(prod[:, j], hot[:, j], place[:, j:j + 1, :].broadcast_to((P, K, E)), ALU.mult)
                    then(last)
                    then(v.tensor_reduce(posf[:, :, :], prod[:, :, :, :], AX.X, ALU.add))
                    then(v.tensor_copy(rows[:, bb, :, D:D + K], topf[:, :, :]))
                    then(v.tensor_copy(rows[:, bb, :, D + K:ROW], res_c[:, bass.ds(TJ * b, TJ), :]))
                    v.tensor_copy(posi[:, bb], posf[:, :, :]).then_inc(pos_ready, 1)
                    own.close()

            two_batches(0)
            with v.Fori(1, NB // 2) as b2:
                two_batches(b2)
            chain = Count(planned)

            def then(ins):
                ins.then_inc(planned, 1)
                v.wait_ge(planned, chain.next())

            v.wait_ge(pos_ready, NB)
            v.wait_ge(dve_done, NB * PER)
            n3 = count[:, :].rearrange("p (e o) -> p e o", o=1).broadcast_to((P, E, 16))
            s3 = steps.rearrange("p (o s) -> p o s", o=1).broadcast_to((P, E, 16))
            then(v.tensor_tensor(many[:, :, :], n3, s3, ALU.is_gt))
            then(v.tensor_reduce(tiles_e[:, :], many[:, :, :], AX.X, ALU.add))
            then(v.tensor_tensor_scan(ends[:, :], one_e[:, :], tiles_e[:, :], 0.0, ALU.mult, ALU.add))
            then(v.tensor_tensor(starts[:, :], ends[:, :], tiles_e[:, :], ALU.subtract))
            then(v.tensor_scalar(hot_e[:, :], ends[:, :], iota_p, None, ALU.is_le))
            then(v.tensor_reduce(meta[:, 0:1], hot_e[:, :], AX.X, ALU.add))
            then(v.scalar_tensor_tensor(out=hot_e[:, :], in0=iota_e, scalar=meta[:, 0:1], in1=starts[:, :],
                                        op0=ALU.is_equal, op1=ALU.mult))
            then(v.tensor_reduce(meta[:, 1:2], hot_e[:, :], AX.X, ALU.add))
            then(v.tensor_tensor(meta[:, 2:3], iota_p, meta[:, 1:2], ALU.subtract))
            then(v.tensor_scalar(meta[:, 2:3], meta[:, 2:3], float(SLOT), -float(E * REG), ALU.mult, ALU.add))
            then(v.scalar_tensor_tensor(out=meta[:, 3:4], in0=meta[:, 0:1], scalar=float(REG), in1=meta[:, 2:3],
                                        op0=ALU.mult, op1=ALU.add))
            then(v.tensor_scalar(meta[:, 4:5], meta[:, 0:1], float(E), None, ALU.is_lt))
            then(v.tensor_tensor(meta[:, 5:6], meta[:, 3:4], meta[:, 4:5], ALU.mult))
            then(v.tensor_scalar(meta[:, 5:6], meta[:, 5:6], float(E * REG), None, ALU.add))
            then(v.tensor_scalar(meta[:, 6:7], meta[:, 0:1], float(E - 1), None, ALU.min))
            then(v.tensor_tensor(place0[:, :], base[:, :], count[:, :], ALU.add))
            v.tensor_scalar(diag[:, :], ident, meta[:, 0:1], None, ALU.mult).then_inc(meta_ready, 1)
            v.tensor_copy(tails[:, :], place0[0:1, :]).then_inc(plan_ready, 1)
            v.wait_ge(plan_psum, 1)
            v.tensor_copy(tile_e[:, :], ps[:, 1, 0:P]).then_inc(plan_ready, 1)
            v.tensor_copy(plan[:, :, :].rearrange("o a n -> o (a n)"), ps[0:1, 0, 0:2 * P]).then_inc(plan_ready, 1)
            v.wait_ge(plan_ready, 3)
            turns(v, dve_step, L_DOWN)
            def four_tiles(g):
                for q in range(RING):
                    n = RING * g + q
                    x = X[:, bass.ds(n, 1), :].rearrange("p o d -> p (o d)")
                    v.wait_ge(back[q], 16 * (g + 1))
                    for k in range(K):
                        w = weight[:, bass.ds(n, 1), k:k + 1].rearrange("p o k -> p (o k)")
                        ins = v.scalar_tensor_tensor(out=x, in0=yk[:, q, k, :], scalar=w, in1=x, op0=ALU.mult, op1=ALU.add)
                        if k < K - 1:
                            ins.then_inc(part_sum, 1)
                            v.wait_ge(part_sum, (K - 1) * n + k + 1)
                    ins.then_inc(summed, 1)

            four_tiles(0)
            with v.Fori(1, NT // RING) as g:
                four_tiles(g)
            v.wait_ge(summed, NT)
    return sems


def load_constants(nc, sb, x, const_d, gate_up):
    with nc.semaphore("c_in") as c_in, nc.semaphore("c_cast") as c_cast, nc.semaphore("c_ones") as c_ones, nc.Block() as block:
        @block.sync
        def _(sp):
            sp.dma_start(sb["const"][:, :], const_d).then_inc(c_in, 16)
            sp.dma_start(sb["X"][:, :, :], x.rearrange("(t p) d -> p t d", p=P)).then_inc(c_in, 16)
            sp.dma_start(sb["Wgu"][:, :, :, :], gate_up.rearrange("(c p) e n -> p c e n", p=P)).then_inc(sb["wgu_in"], 16)
            sp.wait_ge(c_in, 32)

        @block.gpsimd
        def _(pool):
            pool.memset(sb["ones_bf"][:, :], 1.0).then_inc(c_ones, 1)
            pool.wait_ge(c_ones, 1)

        @block.scalar
        def _(act):
            act.wait_ge(c_in, 32)
            for name, at in (("ident_bf", C_ID), ("mask_bf", C_MASK), ("maskT_bf", C_MASKT), ("before_bf", C_LT)):
                act.activation(sb[name][:, :], sb["const"][:, C_AT[at]:C_AT[at] + P], ACT.Copy).then_inc(c_cast, 1)
            act.wait_ge(c_cast, 4)


def store(nc, sb, out):
    with nc.semaphore("stored") as stored, nc.Block() as block:
        @block.sync
        def _(sp):
            sp.dma_start(out.rearrange("(t p) d -> p t d", p=P), sb["X"][:, :, :]).then_inc(stored, 16)
            sp.wait_ge(stored, 16)


def program(nc, x, const_d, wqkv_a, wout_a, ln_a, wqkv_b, wout_b, router, bias, gate_up, down, out, what="afbf"):
    with ExitStack() as ctx:
        def buf(name, shape, dt=F32):
            return ctx.enter_context(nc.sbuf_tensor(name + "_sb", shape, dt))

        sb = {"X": buf("X", [P, NT, D]), "const": buf("const", [P, C_AT[-1]]),
              "ps": ctx.enter_context(nc.psum_tensor("ps", [P, 8, 512], F32))}
        for name in ("ident_bf", "mask_bf", "maskT_bf", "before_bf", "ones_bf"):
            sb[name] = buf(name, [P, P], BF16)
        sb["Wgu"] = buf("Wgu", [P, 2, E + 1, 2 * I])
        sb["wgu_in"] = ctx.enter_context(nc.semaphore("wgu_in"))
        sb["router_d"], sb["bias_d"] = router, bias
        xs_d = nc.dram_tensor("dispatched", (E * REG + P, ROW), F32, kind="Internal").ap()
        y_d = nc.dram_tensor("results", (NRES, D), F32, kind="Internal").ap()
        sb["max_d"] = nc.dram_tensor("maxima", (3 * H, T), BF16, kind="Internal").ap()
        load_constants(nc, sb, x, const_d, gate_up)
        for n, w in enumerate(what):
            if w == "f":
                used = experts(nc, sb, xs_d, y_d, down, str(n))
            else:
                used = attention(nc, sb, w == "a", *((wqkv_a, wout_a) if w == "a" else (wqkv_b, wout_b)), ln_a)
            nc.clear_and_free_semaphores(used)
            nc.all_engine_barrier()
        store(nc, sb, out)


def layout(L0_attn_a_x, L0_attn_a_w_qkv, L0_attn_a_w_out, L0_attn_a_ln_scale, L0_attn_a_ln_bias, L0_attn_b_Wq,
           L0_attn_b_Wk, L0_attn_b_Wv, L0_attn_b_Wo, L0_ffn_router_w, L0_ffn_expert_bias, L0_ffn_gate_w, L0_ffn_up_w,
           L0_ffn_down_w, L0_ffn_shared_gate_w, L0_ffn_shared_up_w, L0_ffn_shared_down_w):
    def rows(*vectors):
        return np.ascontiguousarray(np.broadcast_to(np.stack(vectors)[None], (P, len(vectors), vectors[0].shape[0])))

    t = np.ascontiguousarray
    return {
        "x": L0_attn_a_x.reshape(NT * P, D),
        "const": constants(),
        "wqkv_a": L0_attn_a_w_qkv,
        "wout_a": L0_attn_a_w_out,
        "ln_a": rows(L0_attn_a_ln_scale, L0_attn_a_ln_bias),
        "wqkv_b": t(np.concatenate([L0_attn_b_Wq.T, L0_attn_b_Wk.T, L0_attn_b_Wv.T], axis=1)),
        "wout_b": t(L0_attn_b_Wo.T),
        "router": t(L0_ffn_router_w.T),
        "bias": t(np.broadcast_to(L0_ffn_expert_bias[None], (P, E))),
        "gate_up": t(np.concatenate([
            np.concatenate([L0_ffn_gate_w, L0_ffn_shared_gate_w[None]], 0).transpose(2, 0, 1),
            np.concatenate([L0_ffn_up_w, L0_ffn_shared_up_w[None]], 0).transpose(2, 0, 1)], axis=2)),
        "down": t(np.concatenate([L0_ffn_down_w, L0_ffn_shared_down_w[None]], 0).transpose(2, 0, 1)),
    }


def kernel(**inputs):
    import concourse.bacc as bacc
    from concourse.bass_utils import run_bass_kernel_spmd

    arrays = layout(**{name: np.asarray(a) for name, a in inputs.items()})
    nc = bacc.Bacc("TRN2", target_bir_lowering=False, num_devices=1)
    aps = [nc.dram_tensor(n, a.shape, mybir.dt.from_np(a.dtype), kind="ExternalInput").ap() for n, a in arrays.items()]
    out = nc.dram_tensor("out", (NT * P, D), F32, kind="ExternalOutput").ap()
    program(nc, *aps, out)
    r = run_bass_kernel_spmd(nc, [arrays], core_ids=[0])
    return r.results[0]["out"].reshape(NB, T, D)
```

```python
from contextlib import ExitStack

import numpy as np

import concourse.bass as bass
from concourse import mybir

F32 = mybir.dt.float32
BF16 = mybir.dt.bfloat16
I32 = mybir.dt.int32
U32 = mybir.dt.uint32
ALU = mybir.AluOpType
ACT = mybir.ActivationFunctionType
AX = mybir.AxisListType

P = 128
D = 256
NB, T = 4, 512
TJ = T // P
NT = NB * TJ
H, HD = 16, 16
HG = H // 4
QK = 2 * H * HD
EPS = 1e-5
E, I, K = 32, 128, 4
CLIP = 7.0
MASKED = -3.0e38

PARTS = 6
KS = PARTS * HD
Q_PARTS = {"h": (0, 2, 5), "m": (1, 3), "l": (4,)}
K_PARTS = {"h": (0, 1, 4), "m": (2, 3), "l": (5,)}

UNITS = [(0, 0, 0, 256, True), (0, 1, 128, 128, True),
         (1, 0, 0, 256, False), (1, 1, 0, 256, False), (1, 2, 0, 256, True), (1, 3, 128, 128, True)]
NU = len(UNITS)

SLOT = P
REG = T * NB + P
ROW = D + 2 * K
MT = NT * K + E
FAR = float(1 << 17)
NRES = NT * P * K

C_ID, C_LT, C_KEEP, C_MASK, C_MASKT, C_COS, C_SIN, C_IOTA, C_RES = range(9)
C_COLS = [P, P, P, P, P, TJ * HD, TJ * HD, E + 16 + 1 + 1, NT * K]
C_AT = [sum(C_COLS[:i]) for i in range(len(C_COLS) + 1)]


def constants():
    c = np.zeros((P, C_AT[-1]), np.float32)
    p = np.arange(P)[:, None]
    n = np.arange(P)[None, :]
    c[:, C_AT[C_ID]:C_AT[C_ID] + P] = p == n
    c[:, C_AT[C_LT]:C_AT[C_LT] + P] = p < n
    c[:, C_AT[C_KEEP]:C_AT[C_KEEP] + P] = n >= p
    c[:, C_AT[C_MASK]:C_AT[C_MASK] + P] = np.where(n > p, MASKED, 0.0)
    c[:, C_AT[C_MASKT]:C_AT[C_MASKT] + P] = np.where(p > n, MASKED, 0.0)
    inv = (1.0 / 10000.0 ** (np.arange(0, HD, 2, dtype=np.float32) / HD)).astype(np.float32)
    pos = (np.arange(TJ)[None, :] * P + p).astype(np.float32)
    ang = pos[:, :, None] * inv[None, None, :]
    cos, sin = np.cos(ang), np.sin(ang)
    c[:, C_AT[C_COS]:C_AT[C_COS + 1]] = np.concatenate([cos, cos], -1).reshape(P, -1)
    c[:, C_AT[C_SIN]:C_AT[C_SIN + 1]] = np.concatenate([-sin, sin], -1).reshape(P, -1)
    a = C_AT[C_IOTA]
    c[:, a:a + E] = np.arange(E)
    c[:, a + E:a + E + 16] = SLOT * np.arange(16)
    c[:, a + E + 16] = np.arange(P)
    token = np.arange(NT)[None, :, None] * P + np.arange(P)[:, None, None]
    c[:, C_AT[C_RES]:] = (K * token + np.arange(K) - FAR).reshape(P, -1)
    return c


def wait(eng, sem, n):
    if not isinstance(n, int) or n > 0:
        eng.wait_ge(sem, n)


class Count:

    def __init__(self, sem, base=0, per=None):
        self.sem, self.base, self.per, self.n = sem, base, per, 0

    def next(self):
        self.n += 1
        return self.base + self.n

    def close(self):
        assert self.per is None or self.n == self.per, (self.n, self.per)


def inverse_root(v, y, t, x, done):
    v.reciprocal(y[:, :], y[:, :]).then_inc(done, 1)
    v.wait_ge(done, 1)
    v.tensor_tensor(t[:, :], y[:, :], y[:, :], ALU.mult).then_inc(done, 1)
    v.wait_ge(done, 2)
    v.tensor_tensor(t[:, :], t[:, :], x, ALU.mult).then_inc(done, 1)
    v.wait_ge(done, 3)
    v.tensor_scalar(t[:, :], t[:, :], -0.5, 1.5, ALU.mult, ALU.add).then_inc(done, 1)
    v.wait_ge(done, 4)
    v.tensor_tensor(y[:, :], y[:, :], t[:, :], ALU.mult).then_inc(done, 1)


def attention(nc, sb, rotary, w_qkv, w_out, ln):
    X, ps, const = sb["X"], sb["ps"], sb["const"]
    ident_bf, mask_bf, maskT_bf = sb["ident_bf"], sb["mask_bf"], sb["maskT_bf"]
    keep = const[:, C_AT[C_KEEP]:C_AT[C_KEEP] + P]
    ident = const[:, C_AT[C_ID]:C_AT[C_ID] + P]
    cos = const[:, C_AT[C_COS]:C_AT[C_COS + 1]].rearrange("p (j d) -> p j d", j=TJ)
    sin = const[:, C_AT[C_SIN]:C_AT[C_SIN + 1]].rearrange("p (j d) -> p j d", j=TJ)
    KR = KS if rotary else KS + 3
    tag = "a" if rotary else "b"

    sems = []
    with ExitStack() as ctx:
        def buf(name, shape, dt=F32):
            return ctx.enter_context(nc.sbuf_tensor(f"{name}_{tag}_sb", shape, dt))

        def sem(name):
            sems.append(nc.alloc_semaphore(f"{name}_{tag}"))
            return sems[-1]

        wqkv = buf("wqkv", [P, 2, 3 * D])
        wout = buf("wout", [P, 2, D])
        lnv = buf("lnv", [P, 2, HD])
        stats = buf("stats", [P, NT, 6])
        mv = buf("mv", [P, NT, 2])
        rstd = buf("rstd", [P, NT])
        rt = buf("rt", [P, NT])
        std = buf("std", [P, 2, 2 * H])
        root = buf("root", [P, 2, 2 * H])
        xn = buf("xn", [P, 2, D])
        xT = buf("xT", [P, 2, 2, P])
        qk = buf("qk", [P, TJ, QK])
        tmp = buf("tmp", [P, TJ, QK])
        msum = buf("msum", [P, TJ, 2 * H])
        stk = buf("stk", [P, 2, 2, H, KS], BF16)
        Vs = buf("Vs", [P, TJ, H, 32])
        st = buf("st", [KR, 2, H, T], BF16)
        s2 = buf("s2", [P, 2, 4, 256])
        pr = buf("pr", [P, 3, 4, 256])
        oT = buf("oT", [P, 2, 256])
        rec = buf("rec", [P, 8])
        z = buf("z", [P, TJ, D])
        zT = buf("zT", [P, 2, 2, P])
        nm = buf("nm", [P, TJ, H])
        nmr = buf("nmr", [P, TJ, H])
        nms = buf("nms", [P, TJ, P // H, H], BF16)
        nmT = buf("nmT", [3 * H, T], BF16)

        scores = [ps[:, 2 * k:2 * k + 2, :].rearrange("p a (b n) -> p (a b) n", n=256) for k in range(2)]
        stackT = ps[:, 0:4, :].bitcast(BF16)
        oacc = [ps[:, 4 + k, 0:256] for k in range(2)]
        misc = [ps[:, 6 + k, 0:256] for k in range(2)]
        miscb = ps[:, 6, :].bitcast(BF16)
        p_qk = ps[:, 4, :]
        p_v = ps[:, 5, 0:D]
        p_o = [ps[:, 4 + k, 0:D] for k in range(2)]

        w_in = sem("w_in")
        v_ones = sem("v_ones")
        dve_done = sem("dve_done")
        pool_done = sem("pool_done")
        bn_done, stats_ready, std0_ready, rstd0_ready = (
            sem("bn_done"), sem("stats_ready"), sem("std0_ready"), sem("rstd0_ready"))
        var_ready, std_ready, scaled = sem("var_ready"), sem("std_ready"), sem("scaled")
        xn_ready, xT_psum, xT_ready = sem("xn_ready"), sem("xT_psum"), sem("xT_ready")
        qkv_psum, qk_read, v_ready = sem("qkv_psum"), sem("qk_read"), sem("v_ready")
        rot_parts, rotated, centred, squared = sem("rot_parts"), sem("rotated"), sem("centred"), sem("squared")
        normed, hi_ready, rest_ready = sem("normed"), sem("hi_ready"), sem("rest_ready")
        mid_ready, lo_ready, stack_ready = sem("mid_ready"), sem("lo_ready"), sem("stack_ready")
        stQ_psum, stK_psum, stA_ready, stD_ready = sem("stQ_psum"), sem("stK_psum"), sem("stA_ready"), sem("stD_ready")
        s_psum, s_read, s_masked, p_ready, pv_done = (
            sem("s_psum"), sem("s_read"), sem("s_masked"), sem("p_ready"), sem("pv_done"))
        oT_ready, o_psum, o_read = sem("oT_ready"), sem("o_psum"), sem("o_read")
        zT_psum, zT_ready, y_psum, x_added = sem("zT_psum"), sem("zT_ready"), sem("y_psum"), sem("x_added")
        m_psum, m_read, nms_ready, nmT_psum, nmT_ready, max_rows = (
            sem("m_psum"), sem("m_read"), sem("nms_ready"), sem("nmT_psum"), sem("nmT_ready"), sem("max_rows"))
        max_out = sem("max_out")

        NUB = HG * NU
        NMB = TJ * H // 2
        NQ = 2 * HG
        LAG = 4 if rotary else 2
        STEPS = TJ + LAG + 1

        def parts(t, which, s):
            return t[:, which, :, s * HD:(s + 1) * HD]

        def evac_stack(act, b, j):
            act.wait_ge(stQ_psum, TJ * b + j + 1)
            act.activation(st[0:KS, 0, :, j * P:(j + 1) * P],
                           stackT[0:KS, 0:2, :].rearrange("p g (h n) -> p (g h) n", n=P), ACT.Copy).then_inc(stA_ready, 1)

        def evac_out(act, b, c):
            last = NU * (c // 2) + (2 if c % 2 == 0 else NU)
            act.wait_ge(pv_done, NUB * b + last)
            if c >= 2:
                act.wait_ge(o_psum, NQ * b + c - 1)
            act.activation(oT[:, c % 2, :], oacc[c % 2], ACT.Copy).then_inc(oT_ready, 1)

        def weigh(pe, b, g, u, qc, mt, off, w):
            c = 2 * g + qc
            pe.wait_ge(p_ready, NUB * b + u)
            if mt == 0 and c >= 2:
                pe.wait_ge(oT_ready, NQ * b + c - 1)
            last = 1 if qc == 0 else 3
            for i in range(4):
                mm = pe.matmul(oacc[qc][32 * i:32 * i + 32, off:off + w],
                               Vs[:, mt, 4 * g + i, :], pr[:, (u - 1) % 3, i, 0:w],
                               start=(mt == 0), stop=(mt == last), skip_group_check=True)
            mm.then_inc(pv_done, 1)
            if mt == last and c >= 1:
                turn_out(pe, b, c - 1)

        def turn_out(pe, b, c):
            pe.wait_ge(oT_ready, NQ * b + c + 1)
            if c < 2:
                pe.wait_ge(xT_ready, TJ * b + TJ)
                if not rotary:
                    pe.wait_ge(nmT_ready, b + 1)
            else:
                pe.wait_ge(o_read, NQ * b + c - 1)
            for i in range(2):
                mm = pe.transpose(misc[c % 2][:, i * P:(i + 1) * P],
                                  oT[:, c % 2, i * P:(i + 1) * P], ident)
            mm.then_inc(o_psum, 1)

        def rotate(v, b, j):
            v.wait_ge(qkv_psum, TJ * b + j + 1)
            src = p_qk.rearrange("p (h s d) -> p h s d", s=2, d=HD // 2)
            dst = tmp[:, j, :].rearrange("p (h s d) -> p h s d", s=2, d=HD // 2)
            s8 = sin[:, j, :].rearrange("p (s d) -> p s d", s=2)
            for s in range(2):
                v.tensor_tensor(dst[:, :, s, :], src[:, :, 1 - s, :], s8[:, s:s + 1, :].broadcast_to((P, 2 * H, HD // 2)),
                                ALU.mult)
            v.tensor_tensor(qk[:, j, :].rearrange("p (h d) -> p h d", d=HD), p_qk.rearrange("p (h d) -> p h d", d=HD),
                            cos[:, j:j + 1, :].broadcast_to((P, 2 * H, HD)), ALU.mult).then_inc(rot_parts, 1)

        def normalise(v, b, c, own):
            v.wait_ge(o_psum, NQ * b + c + 1)
            o = misc[c % 2].rearrange("p (i h d) -> p i h d", i=2, d=32)
            wait(v, o_read, NQ * b + c)
            r = rec[:, :].rearrange("p (i h o) -> p i h o", i=2, o=1)
            v.reciprocal(r, o[:, :, :, HD:HD + 1]).then_inc(dve_done, 1)
            v.wait_ge(dve_done, own.next())
            g, qc = c // 2, c % 2
            zz = z[:, 2 * qc:2 * qc + 2, 4 * HD * g:4 * HD * (g + 1)].rearrange("p i (h d) -> p i h d", d=HD)
            v.tensor_tensor(zz, o[:, :, :, 0:HD], r.broadcast_to((P, 2, 4, HD)), ALU.mult).then_inc(o_read, 1)

        block = ctx.enter_context(nc.Block())

        @block.sync
        def _(sp):
            sp.dma_start(wqkv[:, :, :], w_qkv.rearrange("(c p) n -> p c n", p=P)).then_inc(w_in, 16)
            sp.dma_start(wout[:, :, :], w_out.rearrange("(c p) n -> p c n", p=P)).then_inc(w_in, 16)
            sp.dma_start(lnv[:, :, :], ln).then_inc(w_in, 16)
            if not rotary:
                def batch(b):
                    sp.wait_ge(nmT_ready, b + 1)
                    sp.dma_start(sb["max_d"], nmT[:, :]).then_inc(max_out, 16)
                    sp.wait_ge(max_out, 16 * b + 16)
                    sp.dma_start(st[KS:KR, 0, :, :], sb["max_d"].rearrange("(a h) t -> a h t", a=3)).then_inc(max_rows, 16)

                batch(0)
                with sp.Fori(1, NB) as b:
                    batch(b)
                sp.wait_ge(max_rows, 16 * NB)

        def subtract_high(eng, b, j):
            v = qk[:, j, :].rearrange("p (w h d) -> p w h d", w=2, d=HD)
            eng.wait_ge(hi_ready, TJ * b + j + 1)
            eng.tensor_tensor(v, v, stk[:, j % 2, :, :, 0:HD], ALU.subtract).then_inc(rest_ready, 1)

        @block.gpsimd
        def _(pool):
            pool.memset(Vs[:, :, :, HD:HD + 1], 1.0).then_inc(v_ones, 1)
            pool.memset(Vs[:, :, :, HD + 1:32], 0.0).then_inc(v_ones, 1)
            if not rotary:
                pool.memset(nms[:, :, :, :], 0.0).then_inc(v_ones, 1)
                pool.wait_ge(v_ones, 3)
                pool.memset(st[KS:KR, 1, :, :], 1.0).then_inc(v_ones, 1)
            pool.wait_ge(v_ones, 2 if rotary else 4)
            pool.wait_ge(w_in, 48)
            PER = TJ if rotary else 0

            def add_rotated(b, j):
                pool.wait_ge(rot_parts, TJ * b + j + 1)
                pool.tensor_tensor(qk[:, j, :], qk[:, j, :], tmp[:, j, :], ALU.add).then_inc(rotated, 1)

            def subtract_middle(b, j):
                v = qk[:, j, :].rearrange("p (w h d) -> p w h d", w=2, d=HD)
                pool.wait_ge(rest_ready, TJ * b + j + 1)
                pool.wait_ge(mid_ready, TJ * b + j + 1)
                for w, at in ((0, Q_PARTS), (1, K_PARTS)):
                    pool.tensor_tensor(parts(stk[:, j % 2], w, at["l"][0]), v[:, w], parts(stk[:, j % 2], w, at["m"][0]),
                                       ALU.subtract).then_inc(lo_ready, 1)

            def scale_and_bias(b, j, own):
                pool.wait_ge(scaled, TJ * b + j + 1)
                v = qk[:, j, :].rearrange("p (h d) -> p h d", d=HD)
                pool.tensor_tensor(v, v, lnv[:, 0:1, :].broadcast_to((P, 2 * H, HD)), ALU.mult).then_inc(pool_done, 1)
                pool.wait_ge(pool_done, own.next())
                pool.tensor_tensor(v, v, lnv[:, 1:2, :].broadcast_to((P, 2 * H, HD)), ALU.add).then_inc(normed, 1)

            def batch(b):
                own = Count(pool_done, b * PER, PER)
                for s in range(STEPS):
                    if rotary and 0 <= s - 1 < TJ:
                        add_rotated(b, s - 1)
                    if 0 <= s - LAG < TJ:
                        if not rotary:
                            subtract_high(pool, b, s - LAG)
                        subtract_middle(b, s - LAG)
                    if rotary and 0 <= s - 3 < TJ:
                        scale_and_bias(b, s - 3, own)
                if rotary:
                    u = 0
                    for g in range(HG):
                        for qc, mt, off, w, diag in UNITS:
                            u += 1
                            if diag:
                                pool.wait_ge(s_read, NUB * b + u)
                                d = s2[:, (u - 1) % 2, :, 0:P]
                                m = keep[:, :].rearrange("p (o n) -> p o n", o=1).broadcast_to((P, 4, P))
                                pool.tensor_tensor(d, d, m, ALU.mult).then_inc(s_masked, 1)

            batch(0)
            with pool.Fori(1, NB) as b:
                batch(b)

        @block.scalar
        def _(act):
            act.wait_ge(stats_ready, 1)
            act.activation(rstd[:, :], mv[:, :, 1], ACT.Sqrt).then_inc(std0_ready, 1)

            def transposed_x(b, j):
                act.wait_ge(xT_psum, TJ * b + j + 1)
                act.activation(xT[:, j % 2], misc[j % 2].rearrange(
                    "p (c n) -> p c n", c=2), ACT.Copy).then_inc(xT_ready, 1)

            def values(b, j):
                act.wait_ge(qkv_psum, TJ * b + j + 1)
                if j == 0:
                    act.wait_ge(v_ones, 2)
                    wait(act, pv_done, NUB * b)
                act.activation(Vs[:, j, :, 0:HD], p_v.rearrange("p (h d) -> p h d", d=HD), ACT.Copy
                               ).then_inc(v_ready, 1)

            def high(b, j):
                act.wait_ge(normed if rotary else qk_read, TJ * b + j + 1)
                wait(act, stK_psum, TJ * b + j - 1 if j >= 2 else TJ * b)
                v = qk[:, j, :].rearrange("p (w h d) -> p w h d", w=2, d=HD)
                act.activation(stk[:, j % 2, :, :, 0:HD], v, ACT.Copy).then_inc(hi_ready, 1)

            def middle(b, j):
                v = qk[:, j, :].rearrange("p (w h d) -> p w h d", w=2, d=HD)
                act.wait_ge(rest_ready, TJ * b + j + 1)
                act.activation(parts(stk[:, j % 2], 0, Q_PARTS["m"][0]), v[:, 0], ACT.Copy)
                act.activation(parts(stk[:, j % 2], 1, K_PARTS["m"][0]), v[:, 1], ACT.Copy).then_inc(mid_ready, 1)

            def batch(b):
                for s in range(STEPS):
                    if s < TJ:
                        transposed_x(b, s)
                    if 0 <= s - LAG < TJ:
                        high(b, s - LAG)
                        middle(b, s - LAG)
                    if rotary and 0 <= s - 2 < TJ:
                        act.wait_ge(centred, TJ * b + s - 1)
                        act.activation(tmp[:, s - 2, :], qk[:, s - 2, :], ACT.Square).then_inc(squared, 1)
                    if rotary and 0 <= s - 3 < TJ:
                        act.wait_ge(var_ready, TJ * b + s - 2)
                        act.activation(std[:, (s - 3) % 2, :], msum[:, s - 3, :], ACT.Sqrt).then_inc(std_ready, 1)
                    if s < TJ:
                        values(b, s)
                    if 0 <= s - LAG - 1 < TJ:
                        evac_stack(act, b, s - LAG - 1)
                if not rotary:
                    act.wait_ge(nmT_psum, b + 1)
                    act.activation(nmT[:, :], miscb[0:3 * H, 0:T], ACT.Copy).then_inc(nmT_ready, 1)
                u = 0
                for g in range(HG):
                    for qc, mt, off, w, diag in UNITS:
                        u += 1
                        act.wait_ge(s_psum, NUB * b + u)
                        src = scores[(u - 1) % 2][:, :, 0:w]
                        if rotary:
                            if u > 2:
                                act.wait_ge(p_ready, NUB * b + u - 2)
                            act.activation(s2[:, (u - 1) % 2, :, 0:w], src, ACT.Square).then_inc(s_read, 1)
                        else:
                            if u > 3:
                                act.wait_ge(pv_done, NUB * b + u - 3)
                            act.activation(pr[:, (u - 1) % 3, :, 0:w], src, ACT.Exp).then_inc(p_ready, 1)
                        if (u - 1) % NU == 1 and g >= 1:
                            evac_out(act, b, 2 * g - 1)
                        if (u - 1) % NU == 3:
                            evac_out(act, b, 2 * g)
                evac_out(act, b, NQ - 1)
                for j in range(TJ):
                    act.wait_ge(zT_psum, TJ * b + j + 1)
                    act.activation(zT[:, j % 2], misc[j % 2].rearrange(
                        "p (c n) -> p c n", c=2), ACT.Copy).then_inc(zT_ready, 1)

            batch(0)
            with act.Fori(1, NB) as b:
                batch(b)

        @block.tensor
        def _(pe):
            pe.wait_ge(w_in, 48)
            if not rotary:
                pe.wait_ge(v_ones, 4)
            def project(b, j):
                pe.wait_ge(xn_ready, TJ * b + j + 1)
                if j < 2:
                    wait(pe, zT_ready, TJ * b)
                else:
                    pe.wait_ge(xT_ready, TJ * b + j - 1)
                for c in range(2):
                    mm = pe.transpose(misc[j % 2][:, c * P:(c + 1) * P], xn[:, j % 2, c * P:(c + 1) * P], ident)
                mm.then_inc(xT_psum, 1)
                pe.wait_ge(xT_ready, TJ * b + j + 1)
                wait(pe, rot_parts if rotary else qk_read, TJ * b + j)
                wait(pe, v_ready, TJ * b + j)
                wait(pe, x_added, TJ * b)
                for c in range(2):
                    pe.matmul(p_qk, xT[:, j % 2, c, :], wqkv[:, c, 0:QK], start=(c == 0), stop=(c == 1))
                for c in range(2):
                    mm = pe.matmul(p_v, xT[:, j % 2, c, :], wqkv[:, c, QK:], start=(c == 0), stop=(c == 1))
                mm.then_inc(qkv_psum, 1)

            def transpose_stack(b, j):
                pe.wait_ge(stack_ready, TJ * b + j + 1)
                pe.wait_ge(lo_ready, 2 * (TJ * b + j + 1))
                if j == 0:
                    wait(pe, s_read if rotary else p_ready, NUB * b)
                for w, evacuated, done in ((0, stA_ready, stQ_psum), (1, stD_ready, stK_psum)):
                    wait(pe, evacuated, TJ * b + j)
                    for h in range(H):
                        mm = pe.transpose(stackT[0:KS, 2 * w + h // 8, (h % 8) * P:(h % 8 + 1) * P],
                                          stk[:, j % 2, w, h, :], ident_bf[:, :])
                    mm.then_inc(done, 1)

            def batch(b):
                for s in range(STEPS):
                    if s < TJ:
                        project(b, s)
                    if 0 <= s - LAG < TJ:
                        transpose_stack(b, s - LAG)
                pe.wait_ge(stA_ready, TJ * b + TJ)
                pe.wait_ge(stD_ready, TJ * b + TJ)
                if not rotary:
                    n = 0
                    for j in range(TJ):
                        for hp in range(H // 2):
                            n += 1
                            if n > 2:
                                pe.wait_ge(m_read, NMB * b + n - 2)
                            for i in range(2):
                                h = 2 * hp + i
                                bank = 2 * ((n - 1) % 2) + i
                                pe.matmul(ps[:, bank, 0:(j + 1) * P], st[0:KS, 0, h, j * P:(j + 1) * P],
                                          st[0:KS, 1, h, 0:(j + 1) * P], start=True, stop=False)
                                mm = pe.matmul(ps[:, bank, j * P:(j + 1) * P], ident_bf[:, :], mask_bf[:, :],
                                               start=False, stop=True)
                            mm.then_inc(m_psum, 1)
                    pe.wait_ge(nms_ready, b + 1)
                    for j in range(TJ):
                        mm = pe.transpose(miscb[:, j * P:(j + 1) * P],
                                          nms[:, j].rearrange("p a h -> p (a h)"), ident_bf[:, :])
                    mm.then_inc(nmT_psum, 1)
                    pe.wait_ge(m_read, NMB * b + NMB)
                    pe.wait_ge(max_rows, 16 * b + 16)
                pe.wait_ge(v_ready, TJ * b + TJ)
                pe.wait_ge(rot_parts if rotary else qk_read, TJ * b + TJ)
                u = 0
                todo = []
                for g in range(HG):
                    for qc, mt, off, w, diag in UNITS:
                        u += 1
                        if u > 2:
                            pe.wait_ge(s_read if rotary else p_ready, NUB * b + u - 2)
                        for i in range(4):
                            h = 4 * g + i
                            masked = diag and not rotary
                            mm = pe.matmul(scores[(u - 1) % 2][:, i, 0:w], st[0:KR, 1, h, mt * P:(mt + 1) * P],
                                           st[0:KR, 0, h, qc * 256 + off:qc * 256 + off + w], start=True, stop=not masked)
                            if masked:
                                mm = pe.matmul(scores[(u - 1) % 2][:, i, 0:P], ident_bf[:, :], maskT_bf[:, :],
                                               start=False, stop=True)
                        mm.then_inc(s_psum, 1)
                        todo.append((g, u, qc, mt, off, w))
                        if len(todo) > 2:
                            weigh(pe, b, *todo.pop(0))
                while todo:
                    weigh(pe, b, *todo.pop(0))
                turn_out(pe, b, NQ - 1)
                for j in range(TJ):
                    pe.wait_ge(o_read, NQ * b + NQ)
                    if j >= 2:
                        pe.wait_ge(zT_ready, TJ * b + j - 1)
                    for c in range(2):
                        mm = pe.transpose(misc[j % 2][:, c * P:(c + 1) * P],
                                          z[:, j, c * P:(c + 1) * P], ident)
                    mm.then_inc(zT_psum, 1)
                    pe.wait_ge(zT_ready, TJ * b + j + 1)
                    if j >= 2:
                        pe.wait_ge(x_added, TJ * b + j - 1)
                    for c in range(2):
                        mm = pe.matmul(p_o[j % 2], zT[:, j % 2, c, :], wout[:, c, :], start=(c == 0), stop=(c == 1))
                    mm.then_inc(y_psum, 1)

            batch(0)
            with pe.Fori(1, NB) as b:
                batch(b)

        @block.vector
        def _(v):
            for n in range(NT):
                v.bn_stats(stats[:, n, :], X[:, n, :]).then_inc(bn_done, 1)
            v.wait_ge(bn_done, NT)
            for n in range(NT):
                v.bn_aggr(mv[:, n, :], stats[:, n, :]).then_inc(bn_done, 1)
            v.wait_ge(bn_done, 2 * NT)
            v.tensor_scalar(mv[:, :, 1], mv[:, :, 1], EPS, None, ALU.add).then_inc(stats_ready, 1)
            v.wait_ge(std0_ready, 1)
            inverse_root(v, rstd, rt, mv[:, :, 1], rstd0_ready)
            v.wait_ge(rstd0_ready, 5)
            PER = NQ + (6 * TJ if rotary else 3)

            def standardise(b, j):
                if j >= 2:
                    v.wait_ge(xT_psum, TJ * b + j - 1)
                x = X[:, bass.ds(TJ * b + j, 1), :].rearrange("p o d -> p (o d)")
                v.tensor_scalar(xn[:, j % 2, :], x, mv[:, bass.ds(TJ * b + j, 1), 0:1].rearrange("p o d -> p (o d)"),
                                rstd[:, bass.ds(TJ * b + j, 1)], ALU.subtract, ALU.mult).then_inc(xn_ready, 1)

            def copy_qk(b, j):
                v.wait_ge(qkv_psum, TJ * b + j + 1)
                v.tensor_scalar(qk[:, j, 0:D], p_qk[:, 0:D], HD ** -0.5, None, ALU.mult)
                v.tensor_copy(qk[:, j, D:QK], p_qk[:, D:QK]).then_inc(qk_read, 1)

            def centre(b, j, own):
                hv = qk[:, j, :].rearrange("p (h d) -> p h d", d=HD)
                v.wait_ge(rotated, TJ * b + j + 1)
                v.tensor_reduce(msum[:, j, :], hv, AX.X, ALU.add).then_inc(dve_done, 1)
                v.wait_ge(dve_done, own.next())
                m = msum[:, j, :].rearrange("p (h o) -> p h o", o=1).broadcast_to((P, 2 * H, HD))
                v.scalar_tensor_tensor(out=hv, in0=m, scalar=-1.0 / HD, in1=hv, op0=ALU.mult, op1=ALU.add
                                       ).then_inc(centred, 1)

            def variance(b, j, own):
                v.wait_ge(squared, TJ * b + j + 1)
                v.wait_ge(centred, TJ * b + j + 1)
                v.tensor_reduce(msum[:, j, :], tmp[:, j, :].rearrange("p (h d) -> p h d", d=HD),
                                AX.X, ALU.add).then_inc(dve_done, 1)
                v.wait_ge(dve_done, own.next())
                v.tensor_scalar(msum[:, j, :], msum[:, j, :], 1.0 / HD, EPS, ALU.mult, ALU.add).then_inc(var_ready, 1)

            def divide(b, j, own):
                def then(ins):
                    ins.then_inc(dve_done, 1)
                    v.wait_ge(dve_done, own.next())

                y, t = std[:, j % 2, :], root[:, j % 2, :]
                v.wait_ge(std_ready, TJ * b + j + 1)
                then(v.reciprocal(y, y))
                then(v.scalar_tensor_tensor(out=t, in0=y, scalar=-0.5, in1=y, op0=ALU.mult, op1=ALU.mult))
                then(v.tensor_tensor(t, t, msum[:, j, :], ALU.mult))
                then(v.scalar_tensor_tensor(out=y, in0=t, scalar=1.5, in1=y, op0=ALU.add, op1=ALU.mult))
                hv = qk[:, j, :].rearrange("p (h d) -> p h d", d=HD)
                r = y.rearrange("p (h o) -> p h o", o=1).broadcast_to((P, 2 * H, HD))
                v.tensor_tensor(hv, hv, r, ALU.mult).then_inc(scaled, 1)

            def repeat_parts(b, j):
                v.wait_ge(hi_ready, TJ * b + j + 1)
                v.wait_ge(mid_ready, TJ * b + j + 1)
                for w, at in ((0, Q_PARTS), (1, K_PARTS)):
                    for p in "hm":
                        for s in at[p][1:]:
                            last = v.tensor_copy(parts(stk[:, j % 2], w, s), parts(stk[:, j % 2], w, at[p][0]))
                last.then_inc(stack_ready, 1)

            def batch(b):
                own = Count(dve_done, b * PER, PER)
                wait(v, x_added, TJ * b)
                for s in range(STEPS):
                    if s < TJ:
                        standardise(b, s)
                    if rotary and 0 <= s - LAG < TJ:
                        subtract_high(v, b, s - LAG)
                    if 0 <= s - 1 < TJ:
                        if rotary:
                            rotate(v, b, s - 1)
                        else:
                            copy_qk(b, s - 1)
                    if 0 <= s - LAG - 1 < TJ:
                        j = s - LAG - 1
                        v.wait_ge(stK_psum, TJ * b + j + 1)
                        v.tensor_copy(st[0:KS, 1, :, j * P:(j + 1) * P],
                                      stackT[0:KS, 2:4, :].rearrange("p g (h n) -> p (g h) n", n=P)).then_inc(stD_ready, 1)
                    if rotary and 0 <= s - 2 < TJ:
                        centre(b, s - 2, own)
                    if rotary and 0 <= s - 3 < TJ:
                        variance(b, s - 3, own)
                    if 0 <= s - LAG < TJ:
                        repeat_parts(b, s - LAG)
                    if rotary and 0 <= s - 3 < TJ:
                        divide(b, s - 3, own)
                if not rotary:
                    n = 0
                    for j in range(TJ):
                        for hp in range(H // 2):
                            n += 1
                            v.wait_ge(m_psum, NMB * b + n)
                            bank = 2 * ((n - 1) % 2)
                            v.tensor_reduce(nm[:, j, 2 * hp:2 * hp + 2], ps[:, bank:bank + 2, 0:(j + 1) * P],
                                            AX.X, ALU.max, negate=True).then_inc(m_read, 1)
                    v.wait_ge(m_read, NMB * b + NMB)
                    v.tensor_copy(nms[:, :, 0, :], nm[:, :, :]).then_inc(dve_done, 1)
                    v.wait_ge(dve_done, own.next())
                    v.tensor_tensor(nmr[:, :, :], nm[:, :, :], nms[:, :, 0, :], ALU.subtract).then_inc(dve_done, 1)
                    v.wait_ge(dve_done, own.next())
                    v.tensor_copy(nms[:, :, 1, :], nmr[:, :, :]).then_inc(dve_done, 1)
                    v.wait_ge(dve_done, own.next())
                    v.tensor_tensor(nms[:, :, 2, :], nmr[:, :, :], nms[:, :, 1, :], ALU.subtract).then_inc(nms_ready, 1)
                u = diags = 0
                for g in range(HG):
                    for n, (qc, mt, off, w, diag) in enumerate(UNITS):
                        u += 1
                        if rotary:
                            v.wait_ge(s_read, NUB * b + u)
                            if diag:
                                diags += 1
                                v.wait_ge(s_masked, 4 * HG * b + diags)
                            if u > 3:
                                v.wait_ge(pv_done, NUB * b + u - 3)
                            s = s2[:, (u - 1) % 2, :, 0:w]
                            v.tensor_tensor(pr[:, (u - 1) % 3, :, 0:w], s, s, ALU.mult).then_inc(p_ready, 1)
                        if n in (1, 3) and g >= 1:
                            normalise(v, b, 2 * g - 2 + n // 2, own)
                normalise(v, b, NQ - 2, own)
                normalise(v, b, NQ - 1, own)
                for j in range(TJ):
                    v.wait_ge(y_psum, TJ * b + j + 1)
                    x = X[:, bass.ds(TJ * b + j, 1), :].rearrange("p o d -> p (o d)")
                    v.tensor_tensor(x, x, p_o[j % 2], ALU.add).then_inc(x_added, 1)
                own.close()

            batch(0)
            with v.Fori(1, NB) as b:
                batch(b)
    return sems


def experts(nc, sb, xs_d, y_d, down_d, tag):
    X, ps, const, Wgu = sb["X"], sb["ps"], sb["const"], sb["Wgu"]
    before_bf, ones_bf = sb["before_bf"], sb["ones_bf"]
    ident = const[:, C_AT[C_ID]:C_AT[C_ID] + P]
    io = C_AT[C_IOTA]
    iota_e, steps, iota_p = const[:, io:io + E], const[:, io + E:io + E + 16], const[:, io + E + 16:io + E + 17]
    res_c = const[:, C_AT[C_RES]:].rearrange("p (t k) -> p t k", k=K)
    RING, BACK = 8, 4
    CLS = bass.IndirectOffsetOnAxis

    sems = []
    with ExitStack() as ctx:
        def buf(name, shape, dt=F32):
            return ctx.enter_context(nc.sbuf_tensor(f"{name}_{tag}_sb", shape, dt))

        def sem(name):
            sems.append(nc.alloc_semaphore(f"{name}_{tag}"))
            return sems[-1]

        Wd = buf("Wd", [P, E + 1, D])
        stats, mv, rstd = buf("stats", [P, NT, 6]), buf("mv", [P, NT, 2]), buf("rstd", [P, NT])
        rt = buf("rt", [P, NT])
        pad, padp = buf("pad", [P, 1]), buf("padp", [P, 1])
        rows = buf("rows", [P, NT, ROW])
        xT_all = buf("xT_all", [P, 2, NT, P])
        s_gu, s_sg = buf("s_gu", [P, 2, T]), buf("s_sg", [P, T])
        xT = buf("xT", [P, 2, 2, P])
        gu, sg, h, hT = buf("gu", [P, 4, 2 * I]), buf("sg", [P, 4, I]), buf("h", [P, 2, I]), buf("hT", [P, 2, P])
        mag, ex, lg1, sp = (buf(n, [P, NT * E]) for n in ("mag", "ex", "lg1", "sp"))
        score, biased = buf("score", [P, NT, E]), buf("biased", [P, TJ, E])
        top = buf("top", [P, TJ, 8])
        topi = buf("topi", [P, TJ, 8], U32)
        topf = buf("topf", [P, TJ, K])
        hot, prod = buf("hot", [P, TJ, K, E]), buf("prod", [P, TJ, K, E])
        mask = buf("mask", [P, TJ, E], BF16)
        place, place0 = buf("place", [P, TJ, E]), buf("place0", [P, E])
        count, base = buf("count", [P, E]), buf("base", [P, E])
        picked, total, posf = buf("picked", [P, TJ, K]), buf("total", [P, TJ]), buf("posf", [P, TJ, K])
        posi = buf("posi", [P, NT, K], I32)
        weight = buf("weight", [P, NT, K])
        dummy = buf("dummy", [P, ROW])
        many = buf("many", [P, E, 16])
        tiles_e, ends, starts, one_e = (buf(n, [P, E]) for n in ("tiles_e", "ends", "starts", "one_e"))
        hot_e = buf("hot_e", [P, E])
        meta = buf("meta", [P, 8])
        diag, ones = buf("diag", [P, P]), buf("ones", [P, P])
        tile_e = buf("tile_e", [P, P])
        plan = buf("plan", [1, 2, P], I32)
        tails = buf("tails", [1, E], I32)
        xs = buf("xs", [P, RING, ROW])
        ys = rows[:, :, :].rearrange("p t r -> p (t r)")[:, 0:RING * D].rearrange("p (q d) -> p q d", q=RING)
        toi = buf("toi", [P, RING], I32)
        tof = buf("tof", [P, RING])
        to4 = buf("to4", [P, RING, K])
        yk = xT_all[:, :, :, :].rearrange("p c t n -> p (c t n)").rearrange("p (q k d) -> p q k d", q=BACK, k=K)
        router = buf("router", [P, 2, E])
        bias = buf("bias", [P, E])

        p_logit = ps[:, 0, :]
        p_rank = ps[:, 1, 0:TJ * E]
        p_total = ps[:, 1, TJ * E:(TJ + 1) * E]
        p_gu = [ps[:, 2 + k, 0:2 * I] for k in range(2)]
        p_y = [ps[:, 4 + k, 0:D] for k in range(2)]
        p_xT = [ps[:, 6 + k, 0:D] for k in range(2)]
        p_hT = [ps[:, k, 0:P] for k in range(2)]
        p_sgu = [ps[:, 2 + k, :] for k in range(2)]

        w_in, wd_in, set_up = sem("w_in"), sem("wd_in"), sem("set_up")
        dve_done, stats_ready, rstd_ready, xn_ready = sem("dve_done"), sem("stats_ready"), sem("rstd_ready"), sem("xn_ready")
        bn_done, soft_part = sem("bn_done"), sem("soft_part")
        xT_psum, xT_ready, gu_psum, clipped = sem("xT_psum"), sem("xT_ready"), sem("gu_psum"), sem("clipped")
        sig_ready, h_ready, hT_psum, hT_ready = sem("sig_ready"), sem("h_ready"), sem("hT_psum"), sem("hT_ready")
        y_psum, x_added = sem("y_psum"), sem("x_added")
        logit_psum, mag_ready, ex_ready, plus1, ln_ready = (
            sem("logit_psum"), sem("mag_ready"), sem("ex_ready"), sem("plus1"), sem("ln_ready"))
        soft_ready, score_ready, mask_ready, rank_psum, pos_ready = (
            sem("soft_ready"), sem("score_ready"), sem("mask_ready"), sem("rank_psum"), sem("pos_ready"))
        sent = sem("sent")
        dummy_ready, meta_ready, plan_psum, plan_ready, tails_in = (
            sem("dummy_ready"), sem("meta_ready"), sem("plan_psum"), sem("plan_ready"), sem("tails_in"))
        loaded = [sem(f"loaded{k}") for k in range(RING)]
        stored = [sem(f"stored{k}") for k in range(RING)]
        t_xT_psum, t_xT, t_gu_psum, t_clip = sem("t_xT_psum"), sem("t_xT"), sem("t_gu_psum"), sem("t_clip")
        t_sig, t_h, t_hT_psum, t_hT = sem("t_sig"), sem("t_h"), sem("t_hT_psum"), sem("t_hT")
        t_y_psum, t_y, t_to, t_acc = sem("t_y_psum"), sem("t_y"), sem("t_to"), sem("t_acc")
        back = [sem(f"back{k}") for k in range(BACK)]
        summed = sem("summed")

        def turns(eng, step, n_lag):
            for g in range(2):
                for u in range(RING):
                    step(eng, g, u)
            with eng.Fori(2, MT // RING) as g:
                for u in range(RING):
                    step(eng, g, u)
            for u in range(n_lag):
                step(eng, MT // RING, u)

        def at(g, u, lag):
            i = RING * g + (u - lag)
            if isinstance(g, int) and not 0 <= i < MT:
                return None
            return i, (u - lag) % RING, g + (u - lag) // RING

        L_UP, L_SIG, L_H, L_TH, L_DOWN = 1, 2, 2, 3, 4

        def sp_step(sp, g, u):
            i, q, turn = at(g, u, 0)
            row = sp.value_load(plan[0:1, 1, bass.ds(i, 1)], min_val=0, max_val=E * REG)
            if not isinstance(g, int) or g >= 1:
                sp.wait_ge(t_xT_psum, i - RING + 1)
                sp.wait_ge(t_acc, i - RING + 1)
            sp.dma_start(xs[:, q, :], xs_d[bass.ds(row, P), :]).then_inc(loaded[q], 16)

        def pe_step(pe, g, u):
            a = at(g, u, 0)
            if a:
                i, q, turn = a
                pe.wait_ge(loaded[q], 16 * (turn + 1))
                if not isinstance(i, int) or i >= 2:
                    pe.wait_ge(t_xT, i - 1)
                for c in range(2):
                    mm = pe.transpose(p_xT[q % 2][:, c * P:(c + 1) * P], xs[:, q, c * P:(c + 1) * P], ident)
                mm.then_inc(t_xT_psum, 1)
            a = at(g, u, L_UP)
            if a:
                i, q, turn = a
                e = pe.value_load(plan[0:1, 0, bass.ds(i, 1)], min_val=0, max_val=E - 1)
                pe.wait_ge(t_xT, i + 1)
                if not isinstance(i, int) or i >= 2:
                    pe.wait_ge(t_clip, i - 1)
                for c in range(2):
                    mm = pe.matmul(p_gu[q % 2], xT[:, q % 2, c, :],
                                   Wgu[:, c, bass.ds(e, 1), :].rearrange("p o n -> p (o n)"), start=(c == 0), stop=(c == 1))
                mm.then_inc(t_gu_psum, 1)
            a = at(g, u, L_TH)
            if a:
                i, q, turn = a
                pe.wait_ge(t_h, i + 1)
                if not isinstance(i, int) or i >= 2:
                    pe.wait_ge(t_hT, i - 1)
                pe.transpose(p_hT[q % 2], h[:, q % 2, :], ident).then_inc(t_hT_psum, 1)
            a = at(g, u, L_DOWN)
            if a:
                i, q, turn = a
                e = pe.value_load(plan[0:1, 0, bass.ds(i, 1)], min_val=0, max_val=E - 1)
                pe.wait_ge(t_hT, i + 1)
                if not isinstance(i, int) or i >= 2:
                    pe.wait_ge(t_y, i - 1)
                pe.matmul(p_y[q % 2], hT[:, q % 2, :], Wd[:, bass.ds(e, 1), :].rearrange("p o n -> p (o n)"),
                          start=True, stop=True).then_inc(t_y_psum, 1)

        def act_step(act, g, u):
            a = at(g, u, 0)
            if a:
                i, q, turn = a
                act.wait_ge(t_xT_psum, i + 1)
                if not isinstance(i, int) or i >= 2:
                    act.wait_ge(t_gu_psum, i - 1)
                act.activation(xT[:, q % 2], p_xT[q % 2].rearrange("p (c n) -> p c n", c=2), ACT.Copy).then_inc(t_xT, 1)
            a = at(g, u, L_SIG)
            if a:
                i, q, turn = a
                act.wait_ge(t_clip, i + 1)
                if not isinstance(i, int) or i >= 4:
                    act.wait_ge(t_h, i - 3)
                act.activation(sg[:, q % 4, :], gu[:, q % 4, 0:I], ACT.Sigmoid).then_inc(t_sig, 1)
            a = at(g, u, L_TH)
            if a:
                i, q, turn = a
                act.wait_ge(t_hT_psum, i + 1)
                if not isinstance(i, int) or i >= 2:
                    act.wait_ge(t_y_psum, i - 1)
                act.activation(hT[:, q % 2, :], p_hT[q % 2], ACT.Copy).then_inc(t_hT, 1)

        def dve_step(v, g, u):
            a = at(g, u, L_UP)
            if a:
                i, q, turn = a
                v.wait_ge(t_gu_psum, i + 1)
                if not isinstance(i, int) or i >= 4:
                    v.wait_ge(t_h, i - 3)
                v.tensor_scalar(gu[:, q % 4, :], p_gu[q % 2], CLIP, -CLIP, ALU.min, ALU.max).then_inc(t_clip, 1)
                v.wait_ge(loaded[q], 16 * (turn + 1))
                v.scalar_tensor_tensor(out=to4[:, q, :], in0=xs[:, q, D:D + K], scalar=tile_e[:, bass.ds(i, 1)],
                                       in1=xs[:, q, D + K:ROW], op0=ALU.is_equal, op1=ALU.mult,
                                       accum_out=tof[:, q:q + 1]).then_inc(t_acc, 1)
            a = at(g, u, L_H)
            if a:
                i, q, turn = a
                v.wait_ge(t_sig, i + 1)
                v.tensor_tensor(sg[:, q % 4, :], sg[:, q % 4, :], gu[:, q % 4, 0:I], ALU.mult).then_inc(t_gs, 1)
            a = at(g, u, L_UP)
            if a:
                i, q, turn = a
                v.wait_ge(t_acc, i + 1)
                if not isinstance(i, int) or i >= RING:
                    v.wait_ge(stored[q], 16 * turn)
                v.tensor_scalar(toi[:, q:q + 1], tof[:, q:q + 1], FAR, None, ALU.add).then_inc(t_to, 1)
            a = at(g, u, L_H)
            if a:
                i, q, turn = a
                v.wait_ge(t_gs, i + 1)
                if not isinstance(i, int) or i >= 2:
                    v.wait_ge(t_hT_psum, i - 1)
                v.tensor_tensor(h[:, q % 2, :], sg[:, q % 4, :], gu[:, q % 4, I:], ALU.mult).then_inc(t_h, 1)
            a = at(g, u, L_DOWN)
            if a:
                i, q, turn = a
                v.wait_ge(t_y_psum, i + 1)
                if not isinstance(i, int) or i >= RING:
                    v.wait_ge(stored[q], 16 * turn)
                v.tensor_copy(ys[:, q, :], p_y[q % 2]).then_inc(t_y, 1)

        def absorb(pool, n):
            wait(pool, absorbed, n)
            pool.tensor_tensor(padp[:, :], base[:, 0:1], base[:, 0:1], ALU.add).then_inc(absorbed, 1)

        def pool_step(pool, g, u):
            a = at(g, u, L_DOWN)
            if a:
                i, q, turn = a
                pool.wait_ge(t_to, i + 1)
                pool.wait_ge(t_y, i + 1)
                absorb(pool, i)
                pool.indirect_dma_start(y_d, CLS(ap=toi[:, q:q + 1], axis=0), ys[:, q, :], None,
                                        bounds_check=NRES - 1, oob_is_err=False).then_inc(stored[q], 16)

        def logits(pe, n):
            pe.wait_ge(xT_ready, n + 1)
            for c in range(2):
                mm = pe.matmul(p_logit[:, n * E:(n + 1) * E], xT_all[:, c, n, :], router[:, c, :],
                               start=(c == 0), stop=(c == 1))
            if n == NT - 1:
                mm.then_inc(logit_psum, 1)

        std_ready = sem("std_ready")
        absorbed, t_gs, h_half, planned, part_sum = sem("absorbed"), sem("t_gs"), sem("h_half"), sem("planned"), sem("part_sum")
        block = ctx.enter_context(nc.Block())

        @block.sync
        def _(sp):
            sp.dma_start(router[:, :, :], sb["router_d"].rearrange("(c p) n -> p c n", p=P)).then_inc(w_in, 16)
            sp.dma_start(bias[:, :], sb["bias_d"]).then_inc(w_in, 16)
            sp.dma_start(Wd[:, :, :], down_d).then_inc(wd_in, 16)
            sp.wait_ge(dummy_ready, 4)
            sp.dma_start(xs_d[E * REG:E * REG + P, :], dummy[:, :]).then_inc(tails_in, 16)
            sp.wait_ge(plan_ready, 3)
            with sp.Fori(0, E) as e:
                row = sp.value_load(tails[0:1, bass.ds(e, 1)], min_val=0, max_val=E * REG)
                sp.dma_start(xs_d[bass.ds(row, P), :], dummy[:, :]).then_inc(tails_in, 16)
            sp.wait_ge(tails_in, 16 * (E + 1))
            sp.wait_ge(sent, 16 * NT * K)
            turns(sp, sp_step, 0)
            for q in range(RING):
                sp.wait_ge(stored[q], 16 * MT // RING)
            y_v = y_d.rearrange("(t p k) d -> p t (k d)", p=P, k=K)
            def four_tiles(g):
                for q in range(BACK):
                    if not isinstance(g, int):
                        sp.wait_ge(summed, BACK * (g - 1) + q + 1)
                    sp.dma_start(yk[:, q], y_v[:, bass.ds(BACK * g + q, 1), :]).then_inc(back[q], 16)

            four_tiles(0)
            with sp.Fori(1, NT // BACK) as g:
                four_tiles(g)

        @block.gpsimd
        def _(pool):
            pool.memset(ones[:, :], 1.0).then_inc(set_up, 1)
            pool.memset(one_e[:, :], 1.0).then_inc(set_up, 1)
            pool.memset(count[:, :], 0.0).then_inc(set_up, 1)
            pool.memset(dummy[:, 0:D], 0.0).then_inc(dummy_ready, 1)
            pool.memset(dummy[:, D:D + K], -1.0).then_inc(dummy_ready, 1)
            pool.memset(dummy[:, D + K:ROW], 0.0).then_inc(dummy_ready, 1)
            pool.tensor_scalar(base[:, :], iota_e, float(REG), None, ALU.mult).then_inc(dummy_ready, 1)
            pool.wait_ge(set_up, 3)
            pool.wait_ge(dummy_ready, 4)
            for b in range(NB):
                pool.wait_ge(pos_ready, b + 1)
                for j in range(TJ):
                    for k in range(K):
                        pool.indirect_dma_start(xs_d, CLS(ap=posi[:, TJ * b + j, k:k + 1], axis=0),
                                                rows[:, TJ * b + j, :], None).then_inc(sent, 16)
            turns(pool, pool_step, L_DOWN)
            for q in range(RING):
                pool.wait_ge(stored[q], 16 * MT // RING)

        @block.scalar
        def _(act):
            act.wait_ge(stats_ready, 1)
            act.activation(rstd[:, :], mv[:, :, 1], ACT.Sqrt).then_inc(std_ready, 1)
            for n in range(NT):
                act.wait_ge(xT_psum, n + 1)
                act.activation(xT_all[:, :, n, :], p_xT[n % 2].rearrange("p (c n) -> p c n", c=2), ACT.Copy
                               ).then_inc(xT_ready, 1)
            act.wait_ge(logit_psum, 1)
            act.activation(mag[:, :], p_logit, ACT.Abs).then_inc(mag_ready, 1)
            act.wait_ge(mag_ready, 1)
            act.activation(ex[:, :], mag[:, :], ACT.Exp, scale=-1.0).then_inc(ex_ready, 1)
            act.wait_ge(plus1, 1)
            act.activation(lg1[:, :], sp[:, :], ACT.Ln).then_inc(ln_ready, 1)
            act.wait_ge(soft_ready, 1)
            act.activation(score[:, :, :].rearrange("p t e -> p (t e)"), sp[:, :], ACT.Sqrt).then_inc(score_ready, 1)

            def batch(b):
                act.wait_ge(clipped, b + 1)
                wait(act, h_ready, b)
                act.activation(s_sg[:, :], s_gu[:, 0, :], ACT.Sigmoid).then_inc(sig_ready, 1)

            batch(0)
            with act.Fori(1, NB) as b:
                batch(b)
            turns(act, act_step, L_DOWN)

        @block.tensor
        def _(pe):
            pe.wait_ge(w_in, 32)
            for n in range(NT):
                pe.wait_ge(xn_ready, n + 1)
                if n >= 2:
                    pe.wait_ge(xT_ready, n - 1)
                for c in range(2):
                    mm = pe.transpose(p_xT[n % 2][:, c * P:(c + 1) * P], rows[:, n, c * P:(c + 1) * P], ident)
                mm.then_inc(xT_psum, 1)
                if n >= 1:
                    logits(pe, n - 1)
            logits(pe, NT - 1)
            for b in range(NB):
                pe.wait_ge(mask_ready, b + 1)
                pe.matmul(p_rank, before_bf[:, :], mask[:, :, :].rearrange("p t e -> p (t e)"),
                          start=True, stop=False, skip_group_check=True)
                for j in range(TJ - 1):
                    pe.matmul(p_rank[:, (j + 1) * E:].rearrange("p (t e) -> p t e", e=E), ones_bf[:, :],
                              mask[:, j:j + 1, :].broadcast_to((P, TJ - 1 - j, E)), start=False, stop=False,
                              skip_group_check=True)
                for j in range(TJ):
                    mm = pe.matmul(p_total, ones_bf[:, :], mask[:, j, :], start=False, stop=(j == TJ - 1),
                                   skip_group_check=True)
                mm.then_inc(rank_psum, 1)
            pe.wait_ge(meta_ready, 1)
            pe.matmul(ps[0:1, 0, 0:P], meta[:, 6:7], ident, start=True, stop=True)
            pe.matmul(ps[0:1, 0, P:2 * P], meta[:, 5:6], ident, start=True, stop=True)
            pe.matmul(ps[:, 1, 0:P], ones[:, :], diag[:, :], start=True, stop=True).then_inc(plan_psum, 1)
            pe.wait_ge(sb["wgu_in"], 16)
            pe.wait_ge(wd_in, 16)

            def batch(b):
                wait(pe, clipped, b)
                for k in range(2):
                    for c in range(2):
                        mm = pe.matmul(p_sgu[k], Wgu[:, c, E, k * I:(k + 1) * I],
                                       xT_all[:, c, bass.ds(TJ * b, TJ), :].rearrange("p t n -> p (t n)"),
                                       start=(c == 0), stop=(c == 1))
                mm.then_inc(gu_psum, 1)
                pe.wait_ge(h_ready, b + 1)
                for j in range(TJ):
                    if j >= 2:
                        pe.wait_ge(x_added, TJ * b + j - 1)
                    else:
                        wait(pe, x_added, TJ * b)
                    pe.matmul(p_y[j % 2], s_gu[:, 0, j * P:(j + 1) * P], Wd[:, E, :], start=True, stop=True
                              ).then_inc(y_psum, 1)

            batch(0)
            with pe.Fori(1, NB) as b:
                batch(b)
            pe.wait_ge(plan_ready, 3)
            turns(pe, pe_step, L_DOWN)

        @block.vector
        def _(v):
            v.wait_ge(w_in, 32)
            v.wait_ge(set_up, 3)
            v.wait_ge(dummy_ready, 4)
            for n in range(NT):
                v.bn_stats(stats[:, n, :], X[:, n, :]).then_inc(bn_done, 1)
            v.wait_ge(bn_done, NT)
            for n in range(NT):
                v.bn_aggr(mv[:, n, :], stats[:, n, :]).then_inc(bn_done, 1)
            v.wait_ge(bn_done, 2 * NT)
            v.tensor_scalar(mv[:, :, 1], mv[:, :, 1], EPS, None, ALU.add).then_inc(stats_ready, 1)
            v.wait_ge(std_ready, 1)
            inverse_root(v, rstd, rt, mv[:, :, 1], rstd_ready)
            v.wait_ge(rstd_ready, 5)
            for n in range(NT):
                v.tensor_scalar(rows[:, n, 0:D], X[:, n, :], mv[:, n, 0:1], rstd[:, n:n + 1],
                                ALU.subtract, ALU.mult).then_inc(xn_ready, 1)
            v.wait_ge(ex_ready, 1)
            v.tensor_scalar(sp[:, :], ex[:, :], 1.0, None, ALU.add).then_inc(plus1, 1)
            v.wait_ge(plus1, 1)
            v.scalar_tensor_tensor(out=ex[:, :], in0=sp[:, :], scalar=1.0, in1=ex[:, :],
                                   op0=ALU.subtract, op1=ALU.subtract).then_inc(soft_part, 1)
            v.wait_ge(soft_part, 1)
            v.wait_ge(ln_ready, 1)
            v.tensor_tensor(ex[:, :], lg1[:, :], ex[:, :], ALU.subtract).then_inc(soft_part, 1)
            v.wait_ge(soft_part, 2)
            v.scalar_tensor_tensor(out=sp[:, :], in0=p_logit, scalar=0.0, in1=ex[:, :],
                                   op0=ALU.max, op1=ALU.add).then_inc(soft_ready, 1)
            v.wait_ge(score_ready, 1)
            PER = 18

            def batch(b):
                own = Count(dve_done, b * PER, PER)

                def then(ins):
                    ins.then_inc(dve_done, 1)
                    v.wait_ge(dve_done, own.next())

                sc = [score[:, bass.ds(TJ * b + j, 1), :] for j in range(TJ)]
                b4 = bias[:, :].rearrange("p (o e) -> p o e", o=1).broadcast_to((P, TJ, E))
                then(v.tensor_tensor(biased[:, :, :], score[:, bass.ds(TJ * b, TJ), :], b4, ALU.add))
                v.memset(pad[:, :], 0.0)
                for j in range(TJ):
                    last = v.max(top[:, j, :], biased[:, j, :])
                then(last)
                v.memset(pad[:, :], 0.0)
                for j in range(TJ):
                    last = v.max_index(topi[:, j, :], top[:, j, :], biased[:, j, :])
                then(last)
                then(v.tensor_copy(topf[:, :, :], topi[:, :, 0:K]))
                for j in range(TJ):
                    it = iota_e.rearrange("p (o e) -> p o e", o=1).broadcast_to((P, K, E))
                    tk = topf[:, j, :].rearrange("p (k o) -> p k o", o=1).broadcast_to((P, K, E))
                    last = v.tensor_tensor(hot[:, j], it, tk, ALU.is_equal)
                then(last)
                with nc.allow_low_precision(reason="zeros and ones, exact in bf16"):
                    v.tensor_reduce(mask[:, :, :], hot[:, :, :, :].rearrange("p t k e -> p t e k"), AX.X, ALU.add
                                    ).then_inc(mask_ready, 1)
                for j in range(TJ):
                    last = v.tensor_tensor(prod[:, j], hot[:, j], sc[j].broadcast_to((P, K, E)), ALU.mult)
                then(last)
                then(v.tensor_reduce(picked[:, :, :], prod[:, :, :, :], AX.X, ALU.add))
                then(v.tensor_reduce(total[:, :], picked[:, :, :], AX.X, ALU.add))
                then(v.tensor_scalar(total[:, :], total[:, :], 1e-20, None, ALU.add))
                then(v.reciprocal(total[:, :], total[:, :]))
                then(v.tensor_tensor(weight[:, bass.ds(TJ * b, TJ), :], picked[:, :, :],
                                     total[:, :].rearrange("p (t o) -> p t o", o=1).broadcast_to((P, TJ, K)), ALU.mult))
                v.wait_ge(rank_psum, b + 1)
                c4 = place0[:, :].rearrange("p (o e) -> p o e", o=1).broadcast_to((P, TJ, E))
                then(v.tensor_tensor(place0[:, :], base[:, :], count[:, :], ALU.add))
                then(v.tensor_tensor(place[:, :, :], p_rank.rearrange("p (t e) -> p t e", e=E), c4, ALU.add))
                then(v.tensor_tensor(count[:, :], count[:, :], p_total, ALU.add))
                for j in range(TJ):
                    last = v.tensor_tensor(prod[:, j], hot[:, j], place[:, j:j + 1, :].broadcast_to((P, K, E)), ALU.mult)
                then(last)
                then(v.tensor_reduce(posf[:, :, :], prod[:, :, :, :], AX.X, ALU.add))
                then(v.tensor_copy(rows[:, bass.ds(TJ * b, TJ), D:D + K], topf[:, :, :]))
                then(v.tensor_copy(rows[:, bass.ds(TJ * b, TJ), D + K:ROW], res_c[:, bass.ds(TJ * b, TJ), :]))
                v.tensor_copy(posi[:, bass.ds(TJ * b, TJ), :], posf[:, :, :]).then_inc(pos_ready, 1)
                own.close()

            with v.Fori(0, NB) as b:
                batch(b)
            chain = Count(planned)

            def then(ins):
                ins.then_inc(planned, 1)
                v.wait_ge(planned, chain.next())

            v.wait_ge(pos_ready, NB)
            v.wait_ge(dve_done, NB * PER)
            n3 = count[:, :].rearrange("p (e o) -> p e o", o=1).broadcast_to((P, E, 16))
            s3 = steps.rearrange("p (o s) -> p o s", o=1).broadcast_to((P, E, 16))
            then(v.tensor_tensor(many[:, :, :], n3, s3, ALU.is_gt))
            then(v.tensor_reduce(tiles_e[:, :], many[:, :, :], AX.X, ALU.add))
            then(v.tensor_tensor_scan(ends[:, :], one_e[:, :], tiles_e[:, :], 0.0, ALU.mult, ALU.add))
            then(v.tensor_tensor(starts[:, :], ends[:, :], tiles_e[:, :], ALU.subtract))
            then(v.tensor_scalar(hot_e[:, :], ends[:, :], iota_p, None, ALU.is_le))
            then(v.tensor_reduce(meta[:, 0:1], hot_e[:, :], AX.X, ALU.add))
            then(v.scalar_tensor_tensor(out=hot_e[:, :], in0=iota_e, scalar=meta[:, 0:1], in1=starts[:, :],
                                        op0=ALU.is_equal, op1=ALU.mult))
            then(v.tensor_reduce(meta[:, 1:2], hot_e[:, :], AX.X, ALU.add))
            then(v.tensor_tensor(meta[:, 2:3], iota_p, meta[:, 1:2], ALU.subtract))
            then(v.tensor_scalar(meta[:, 2:3], meta[:, 2:3], float(SLOT), -float(E * REG), ALU.mult, ALU.add))
            then(v.scalar_tensor_tensor(out=meta[:, 3:4], in0=meta[:, 0:1], scalar=float(REG), in1=meta[:, 2:3],
                                        op0=ALU.mult, op1=ALU.add))
            then(v.tensor_scalar(meta[:, 4:5], meta[:, 0:1], float(E), None, ALU.is_lt))
            then(v.tensor_tensor(meta[:, 5:6], meta[:, 3:4], meta[:, 4:5], ALU.mult))
            then(v.tensor_scalar(meta[:, 5:6], meta[:, 5:6], float(E * REG), None, ALU.add))
            then(v.tensor_scalar(meta[:, 6:7], meta[:, 0:1], float(E - 1), None, ALU.min))
            then(v.tensor_tensor(place0[:, :], base[:, :], count[:, :], ALU.add))
            v.tensor_scalar(diag[:, :], ident, meta[:, 0:1], None, ALU.mult).then_inc(meta_ready, 1)
            v.tensor_copy(tails[:, :], place0[0:1, :]).then_inc(plan_ready, 1)
            v.wait_ge(plan_psum, 1)
            v.tensor_copy(tile_e[:, :], ps[:, 1, 0:P]).then_inc(plan_ready, 1)
            v.tensor_copy(plan[:, :, :].rearrange("o a n -> o (a n)"), ps[0:1, 0, 0:2 * P]).then_inc(plan_ready, 1)
            v.wait_ge(plan_ready, 3)

            def shared(b):
                v.wait_ge(gu_psum, b + 1)
                wait(v, y_psum, TJ * b)
                for k in range(2):
                    ins = v.tensor_scalar(s_gu[:, k, :], p_sgu[k], CLIP, -CLIP, ALU.min, ALU.max)
                ins.then_inc(clipped, 1)
                v.wait_ge(sig_ready, b + 1)
                v.tensor_tensor(s_gu[:, 0, :], s_sg[:, :], s_gu[:, 0, :], ALU.mult).then_inc(h_half, 1)
                v.wait_ge(h_half, b + 1)
                v.tensor_tensor(s_gu[:, 0, :], s_gu[:, 0, :], s_gu[:, 1, :], ALU.mult).then_inc(h_ready, 1)
                for j in range(TJ):
                    v.wait_ge(y_psum, TJ * b + j + 1)
                    x = X[:, bass.ds(TJ * b + j, 1), :].rearrange("p o d -> p (o d)")
                    v.tensor_tensor(x, x, p_y[j % 2], ALU.add).then_inc(x_added, 1)

            shared(0)
            with v.Fori(1, NB) as b:
                shared(b)
            turns(v, dve_step, L_DOWN)
            with v.Fori(0, NT // BACK) as g:
                for k in range(K):
                    for q in range(BACK):
                        n = BACK * g + q
                        x = X[:, bass.ds(n, 1), :].rearrange("p o d -> p (o d)")
                        w = weight[:, bass.ds(n, 1), k:k + 1].rearrange("p o k -> p (o k)")
                        if k == 0:
                            v.wait_ge(back[q], 16 * (g + 1))
                        else:
                            v.wait_ge(part_sum, (K - 1) * BACK * g + BACK * (k - 1) + q + 1)
                        v.scalar_tensor_tensor(out=x, in0=yk[:, q, k, :], scalar=w, in1=x, op0=ALU.mult, op1=ALU.add
                                               ).then_inc(summed if k == K - 1 else part_sum, 1)
            v.wait_ge(summed, NT)
    return sems


def load_constants(nc, sb, x, const_d, gate_up):
    with nc.semaphore("c_in") as c_in, nc.semaphore("c_cast") as c_cast, nc.semaphore("c_ones") as c_ones, nc.Block() as block:
        @block.sync
        def _(sp):
            sp.dma_start(sb["const"][:, :], const_d).then_inc(c_in, 16)
            sp.dma_start(sb["X"][:, :, :], x.rearrange("(t p) d -> p t d", p=P)).then_inc(c_in, 16)
            sp.dma_start(sb["Wgu"][:, :, :, :], gate_up.rearrange("(c p) e n -> p c e n", p=P)).then_inc(sb["wgu_in"], 16)
            sp.wait_ge(c_in, 32)

        @block.gpsimd
        def _(pool):
            pool.memset(sb["ones_bf"][:, :], 1.0).then_inc(c_ones, 1)
            pool.wait_ge(c_ones, 1)

        @block.scalar
        def _(act):
            act.wait_ge(c_in, 32)
            for name, at in (("ident_bf", C_ID), ("mask_bf", C_MASK), ("maskT_bf", C_MASKT), ("before_bf", C_LT)):
                act.activation(sb[name][:, :], sb["const"][:, C_AT[at]:C_AT[at] + P], ACT.Copy).then_inc(c_cast, 1)
            act.wait_ge(c_cast, 4)


def store(nc, sb, out):
    with nc.semaphore("stored") as stored, nc.Block() as block:
        @block.sync
        def _(sp):
            sp.dma_start(out.rearrange("(t p) d -> p t d", p=P), sb["X"][:, :, :]).then_inc(stored, 16)
            sp.wait_ge(stored, 16)


def program(nc, x, const_d, wqkv_a, wout_a, ln_a, wqkv_b, wout_b, router, bias, gate_up, down, out, what="afbf"):
    with ExitStack() as ctx:
        def buf(name, shape, dt=F32):
            return ctx.enter_context(nc.sbuf_tensor(name + "_sb", shape, dt))

        sb = {"X": buf("X", [P, NT, D]), "const": buf("const", [P, C_AT[-1]]),
              "ps": ctx.enter_context(nc.psum_tensor("ps", [P, 8, 512], F32))}
        for name in ("ident_bf", "mask_bf", "maskT_bf", "before_bf", "ones_bf"):
            sb[name] = buf(name, [P, P], BF16)
        sb["Wgu"] = buf("Wgu", [P, 2, E + 1, 2 * I])
        sb["wgu_in"] = ctx.enter_context(nc.semaphore("wgu_in"))
        sb["router_d"], sb["bias_d"] = router, bias
        xs_d = nc.dram_tensor("dispatched", (E * REG + P, ROW), F32, kind="Internal").ap()
        y_d = nc.dram_tensor("results", (NRES, D), F32, kind="Internal").ap()
        sb["max_d"] = nc.dram_tensor("maxima", (3 * H, T), BF16, kind="Internal").ap()
        load_constants(nc, sb, x, const_d, gate_up)
        for n, w in enumerate(what):
            if w == "f":
                used = experts(nc, sb, xs_d, y_d, down, str(n))
            else:
                used = attention(nc, sb, w == "a", *((wqkv_a, wout_a) if w == "a" else (wqkv_b, wout_b)), ln_a)
            nc.clear_and_free_semaphores(used)
            nc.all_engine_barrier()
        store(nc, sb, out)


def layout(L0_attn_a_x, L0_attn_a_w_qkv, L0_attn_a_w_out, L0_attn_a_ln_scale, L0_attn_a_ln_bias, L0_attn_b_Wq,
           L0_attn_b_Wk, L0_attn_b_Wv, L0_attn_b_Wo, L0_ffn_router_w, L0_ffn_expert_bias, L0_ffn_gate_w, L0_ffn_up_w,
           L0_ffn_down_w, L0_ffn_shared_gate_w, L0_ffn_shared_up_w, L0_ffn_shared_down_w):
    def rows(*vectors):
        return np.ascontiguousarray(np.broadcast_to(np.stack(vectors)[None], (P, len(vectors), vectors[0].shape[0])))

    t = np.ascontiguousarray
    return {
        "x": L0_attn_a_x.reshape(NT * P, D),
        "const": constants(),
        "wqkv_a": L0_attn_a_w_qkv,
        "wout_a": L0_attn_a_w_out,
        "ln_a": rows(L0_attn_a_ln_scale, L0_attn_a_ln_bias),
        "wqkv_b": t(np.concatenate([L0_attn_b_Wq.T, L0_attn_b_Wk.T, L0_attn_b_Wv.T], axis=1)),
        "wout_b": t(L0_attn_b_Wo.T),
        "router": t(L0_ffn_router_w.T),
        "bias": t(np.broadcast_to(L0_ffn_expert_bias[None], (P, E))),
        "gate_up": t(np.concatenate([
            np.concatenate([L0_ffn_gate_w, L0_ffn_shared_gate_w[None]], 0).transpose(2, 0, 1),
            np.concatenate([L0_ffn_up_w, L0_ffn_shared_up_w[None]], 0).transpose(2, 0, 1)], axis=2)),
        "down": t(np.concatenate([L0_ffn_down_w, L0_ffn_shared_down_w[None]], 0).transpose(2, 0, 1)),
    }


def kernel(**inputs):
    import concourse.bacc as bacc
    from concourse.bass_utils import run_bass_kernel_spmd

    arrays = layout(**{name: np.asarray(a) for name, a in inputs.items()})
    nc = bacc.Bacc("TRN2", target_bir_lowering=False, num_devices=1)
    aps = [nc.dram_tensor(n, a.shape, mybir.dt.from_np(a.dtype), kind="ExternalInput").ap() for n, a in arrays.items()]
    out = nc.dram_tensor("out", (NT * P, D), F32, kind="ExternalOutput").ap()
    program(nc, *aps, out)
    r = run_bass_kernel_spmd(nc, [arrays], core_ids=[0])
    return r.results[0]["out"].reshape(NB, T, D)
```

```python
from contextlib import ExitStack

import numpy as np

import concourse.bass as bass
from concourse import mybir

F32 = mybir.dt.float32
BF16 = mybir.dt.bfloat16
I32 = mybir.dt.int32
U32 = mybir.dt.uint32
ALU = mybir.AluOpType
ACT = mybir.ActivationFunctionType
AX = mybir.AxisListType

P = 128
D = 256
NB, T = 4, 512
TJ = T // P
NT = NB * TJ
H, HD = 16, 16
HG = H // 4
QK = 2 * H * HD
EPS = 1e-5
E, I, K = 32, 128, 4
CLIP = 7.0
MASKED = -3.0e38

PARTS = 6
KS = PARTS * HD
Q_PARTS = {"h": (0, 2, 5), "m": (1, 3), "l": (4,)}
K_PARTS = {"h": (0, 1, 4), "m": (2, 3), "l": (5,)}

UNITS = [(0, 0, 0, 256, True), (0, 1, 128, 128, True),
         (1, 0, 0, 256, False), (1, 1, 0, 256, False), (1, 2, 0, 256, True), (1, 3, 128, 128, True)]
NU = len(UNITS)

SLOT = P
REG = T * NB + P
ROW = D + 2 * K
MT = NT * K + E
FAR = float(1 << 17)
NRES = NT * P * K

C_ID, C_KEEP, C_COS, C_SIN, C_IOTA, C_RES, C_LT, C_MASK, C_MASKT = range(9)
C_COLS = [P, P, TJ * HD, TJ * HD, E + 16 + 1 + 1, NT * K, P, P, P]
C_AT = [sum(C_COLS[:i]) for i in range(len(C_COLS) + 1)]
C_KEPT = C_AT[C_LT]


def constants():
    c = np.zeros((P, C_AT[-1]), np.float32)
    p = np.arange(P)[:, None]
    n = np.arange(P)[None, :]
    c[:, C_AT[C_ID]:C_AT[C_ID] + P] = p == n
    c[:, C_AT[C_LT]:C_AT[C_LT] + P] = p < n
    c[:, C_AT[C_KEEP]:C_AT[C_KEEP] + P] = n >= p
    c[:, C_AT[C_MASK]:C_AT[C_MASK] + P] = np.where(n > p, MASKED, 0.0)
    c[:, C_AT[C_MASKT]:C_AT[C_MASKT] + P] = np.where(p > n, MASKED, 0.0)
    inv = (1.0 / 10000.0 ** (np.arange(0, HD, 2, dtype=np.float32) / HD)).astype(np.float32)
    pos = (np.arange(TJ)[None, :] * P + p).astype(np.float32)
    ang = pos[:, :, None] * inv[None, None, :]
    cos, sin = np.cos(ang), np.sin(ang)
    c[:, C_AT[C_COS]:C_AT[C_COS + 1]] = np.concatenate([cos, cos], -1).reshape(P, -1)
    c[:, C_AT[C_SIN]:C_AT[C_SIN + 1]] = np.concatenate([-sin, sin], -1).reshape(P, -1)
    a = C_AT[C_IOTA]
    c[:, a:a + E] = np.arange(E)
    c[:, a + E:a + E + 16] = SLOT * np.arange(16)
    c[:, a + E + 16] = np.arange(P)
    token = np.arange(NT)[None, :, None] * P + np.arange(P)[:, None, None]
    c[:, C_AT[C_RES]:C_KEPT] = (K * token + np.arange(K) - FAR).reshape(P, -1)
    return c


def wait(eng, sem, n):
    if not isinstance(n, int) or n > 0:
        eng.wait_ge(sem, n)


class Count:

    def __init__(self, sem, base=0, per=None):
        self.sem, self.base, self.per, self.n = sem, base, per, 0

    def next(self):
        self.n += 1
        return self.base + self.n

    def close(self):
        assert self.per is None or self.n == self.per, (self.n, self.per)


def inverse_root(v, y, t, x, done):
    v.reciprocal(y[:, :], y[:, :]).then_inc(done, 1)
    v.wait_ge(done, 1)
    v.tensor_tensor(t[:, :], y[:, :], y[:, :], ALU.mult).then_inc(done, 1)
    v.wait_ge(done, 2)
    v.tensor_tensor(t[:, :], t[:, :], x, ALU.mult).then_inc(done, 1)
    v.wait_ge(done, 3)
    v.tensor_scalar(t[:, :], t[:, :], -0.5, 1.5, ALU.mult, ALU.add).then_inc(done, 1)
    v.wait_ge(done, 4)
    v.tensor_tensor(y[:, :], y[:, :], t[:, :], ALU.mult).then_inc(done, 1)


def attention(nc, sb, rotary, w_qkv, w_out, ln):
    X, ps, const = sb["X"], sb["ps"], sb["const"]
    ident_bf, mask_bf, maskT_bf = sb["ident_bf"], sb["mask_bf"], sb["maskT_bf"]
    keep = const[:, C_AT[C_KEEP]:C_AT[C_KEEP] + P]
    ident = const[:, C_AT[C_ID]:C_AT[C_ID] + P]
    cos = const[:, C_AT[C_COS]:C_AT[C_COS + 1]].rearrange("p (j d) -> p j d", j=TJ)
    sin = const[:, C_AT[C_SIN]:C_AT[C_SIN + 1]].rearrange("p (j d) -> p j d", j=TJ)
    KR = KS if rotary else KS + 3
    tag = "a" if rotary else "b"

    sems = []
    with ExitStack() as ctx:
        def buf(name, shape, dt=F32):
            return ctx.enter_context(nc.sbuf_tensor(f"{name}_{tag}_sb", shape, dt))

        def sem(name):
            sems.append(nc.alloc_semaphore(f"{name}_{tag}"))
            return sems[-1]

        wqkv = buf("wqkv", [P, 2, 3 * D])
        wout = buf("wout", [P, 2, D])
        lnv = buf("lnv", [P, 2, HD])
        stats = buf("stats", [P, NT, 6])
        mv = buf("mv", [P, NT, 2])
        rstd = buf("rstd", [P, NT])
        rt = buf("rt", [P, NT])
        std = buf("std", [P, 2, 2 * H])
        root = buf("root", [P, 2, 2 * H])
        xn = buf("xn", [P, D])
        xT = buf("xT", [P, 2, P])
        qk = buf("qk", [P, TJ, QK])
        tmp = buf("tmp", [P, 2, QK]) if rotary else None
        msum = buf("msum", [P, TJ, 2 * H])
        stk = buf("stk", [P, TJ, 2, H, KS], BF16)
        v_next = buf("v_next", [P, TJ, D])
        Vs = buf("Vs", [P, TJ, H, 32])
        st = buf("st", [KR, 2, H, T], BF16)
        s2 = buf("s2", [P, 3, 4, 256]) if rotary else None
        pr = buf("pr", [P, 3, 4, 256])
        oT = buf("oT", [P, 2, 256])
        rec = buf("rec", [P, 8])
        z = buf("z", [P, TJ, D])
        zT = pr[:, 0, :, :].rearrange("p i n -> p (i n)")[:, 0:4 * P].rearrange("p (k c n) -> p k c n", k=2, c=2)
        if not rotary:
            nm = buf("nm", [P, TJ, H])
            nmr = buf("nmr", [P, TJ, H])
            nms = buf("nms", [P, TJ, P // H, H], BF16)
            nmT = buf("nmT", [3 * H, T], BF16)

        scores = [ps[:, 2 * k:2 * k + 2, :].rearrange("p a (b n) -> p (a b) n", n=256) for k in range(2)]
        stackT = ps[:, 0:4, :].bitcast(BF16)
        max_banks = (0, 2, 6)
        oacc = ps[:, 4, 0:256]
        misc = ps[:, 5, 0:256]
        miscb = ps[:, 5, :].bitcast(BF16)
        p_qk = ps[:, 6, :]
        p_xT = ps[:, 7, 0:D]
        p_v = ps[:, 7, D:2 * D]
        p_zT = [ps[:, 6 + k, 0:D] for k in range(2)]
        p_o = [ps[:, 4 + k, 0:D] for k in range(2)]

        w_in = sem("w_in")
        v_ones = sem("v_ones")
        dve_done = sem("dve_done")
        pool_done = sem("pool_done")
        bn_done, stats_ready, std0_ready, rstd0_ready = (
            sem("bn_done"), sem("stats_ready"), sem("std0_ready"), sem("rstd0_ready"))
        var_ready, std_ready, scaled = sem("var_ready"), sem("std_ready"), sem("scaled")
        xn_ready, xT_psum, xT_ready = sem("xn_ready"), sem("xT_psum"), sem("xT_ready")
        qkv_psum, v_psum, qk_read, v_ready = sem("qkv_psum"), sem("v_psum"), sem("qk_read"), sem("v_ready")
        rot_parts, rotated, centred, squared = sem("rot_parts"), sem("rotated"), sem("centred"), sem("squared")
        normed, hi_ready, rest_ready = sem("normed"), sem("hi_ready"), sem("rest_ready")
        mid_ready, lo_ready, stack_ready = sem("mid_ready"), sem("lo_ready"), sem("stack_ready")
        stQ_psum, stK_psum, stA_ready, stD_ready = sem("stQ_psum"), sem("stK_psum"), sem("stA_ready"), sem("stD_ready")
        s_psum, s_read, s_masked, p_ready, pv_done = (
            sem("s_psum"), sem("s_read"), sem("s_masked"), sem("p_ready"), sem("pv_done"))
        oT_ready, o_psum, o_read = sem("oT_ready"), sem("o_psum"), sem("o_read")
        zT_psum, zT_ready, y_psum, x_added = sem("zT_psum"), sem("zT_ready"), sem("y_psum"), sem("x_added")
        m_psum, m_read, nms_ready, nmT_psum, nmT_ready, max_rows = (
            sem("m_psum"), sem("m_read"), sem("nms_ready"), sem("nmT_psum"), sem("nmT_ready"), sem("max_rows"))
        max_out, prep_done, vs_ready = sem("max_out"), sem("prep_done"), sem("vs_ready")

        NUB = HG * NU
        NMB = TJ * H // 2
        NQ = 2 * HG
        SLOTS = NUB
        BEHIND = 3 if rotary else 2
        GAP = 3 if rotary else 4
        AT_NORM, AT_TURN, AT_X, AT_VALUES, AT_PROJECT, AT_READ = (0, 1, 2, 3, 3, 4) if rotary else range(6)
        if rotary:
            AT_ADD, AT_CENTRE, AT_SQUARE, AT_VAR, AT_STD, AT_DIVIDE, AT_SCALE, AT_HIGH, AT_REST, AT_MID, AT_LOW = (
                range(5, 16))
        else:
            AT_HIGH, AT_REST, AT_MID, AT_LOW = range(6, 10)
        LATE = max(0, GAP * (TJ - 1) + AT_LOW + 1 - SLOTS)

        def stage(t, at):
            j, off = divmod(t - at, GAP)
            return [j] if off == 0 and 0 <= j < TJ else []

        def parts(t, which, s):
            return t[:, which, :, s * HD:(s + 1) * HD]

        def evac_stack(act, b, j):
            act.wait_ge(stQ_psum, TJ * b + j + 1)
            act.activation(st[0:KS, 0, :, j * P:(j + 1) * P],
                           stackT[0:KS, 0:2, :].rearrange("p g (h n) -> p (g h) n", n=P), ACT.Copy).then_inc(stA_ready, 1)

        def evac_out(act, b, c):
            last = NU * (c // 2) + (2 if c % 2 == 0 else NU)
            act.wait_ge(pv_done, NUB * b + last)
            if c >= 2:
                act.wait_ge(o_psum, NQ * b + c - 1)
            act.activation(oT[:, c % 2, :], oacc, ACT.Copy).then_inc(oT_ready, 1)

        def weigh(pe, b, g, u, qc, mt, off, w):
            c = 2 * g + qc
            pe.wait_ge(p_ready, NUB * b + u)
            if mt == 0 and c >= 1:
                pe.wait_ge(oT_ready, NQ * b + c)
            last = 1 if qc == 0 else 3
            for i in range(4):
                mm = pe.matmul(oacc[32 * i:32 * i + 32, off:off + w],
                               Vs[:, mt, 4 * g + i, :], pr[:, (u - 1) % 3, i, 0:w],
                               start=(mt == 0), stop=(mt == last), skip_group_check=True)
            mm.then_inc(pv_done, 1)
            if mt == last and c >= 1:
                turn_out(pe, b, c - 1)

        def turn_out(pe, b, c):
            pe.wait_ge(oT_ready, NQ * b + c + 1)
            if c >= 1:
                pe.wait_ge(o_read, NQ * b + c)
            elif not rotary:
                pe.wait_ge(nmT_ready, b + 1)
            for i in range(2):
                mm = pe.transpose(misc[:, i * P:(i + 1) * P],
                                  oT[:, c % 2, i * P:(i + 1) * P], ident)
            mm.then_inc(o_psum, 1)

        def rotate(v, b, j):
            v.wait_ge(qkv_psum, TJ * b + j + 1)
            src = p_qk.rearrange("p (h s d) -> p h s d", s=2, d=HD // 2)
            dst = tmp[:, j % 2, :].rearrange("p (h s d) -> p h s d", s=2, d=HD // 2)
            s8 = sin[:, j, :].rearrange("p (s d) -> p s d", s=2)
            for s in range(2):
                v.tensor_tensor(dst[:, :, s, :], src[:, :, 1 - s, :], s8[:, s:s + 1, :].broadcast_to((P, 2 * H, HD // 2)),
                                ALU.mult)
            v.tensor_tensor(qk[:, j, :].rearrange("p (h d) -> p h d", d=HD), p_qk.rearrange("p (h d) -> p h d", d=HD),
                            cos[:, j:j + 1, :].broadcast_to((P, 2 * H, HD)), ALU.mult).then_inc(rot_parts, 1)

        def normalise(v, b, c, own):
            v.wait_ge(o_psum, NQ * b + c + 1)
            o = misc.rearrange("p (i h d) -> p i h d", i=2, d=32)
            wait(v, o_read, NQ * b + c)
            r = rec[:, :].rearrange("p (i h o) -> p i h o", i=2, o=1)
            v.reciprocal(r, o[:, :, :, HD:HD + 1]).then_inc(dve_done, 1)
            v.wait_ge(dve_done, own.next())
            g, qc = c // 2, c % 2
            zz = z[:, 2 * qc:2 * qc + 2, 4 * HD * g:4 * HD * (g + 1)].rearrange("p i (h d) -> p i h d", d=HD)
            v.tensor_tensor(zz, o[:, :, :, 0:HD], r.broadcast_to((P, 2, 4, HD)), ALU.mult).then_inc(o_read, 1)

        block = ctx.enter_context(nc.Block())

        @block.sync
        def _(sp):
            sp.dma_start(wqkv[:, :, :], w_qkv.rearrange("(c p) n -> p c n", p=P)).then_inc(w_in, 16)
            sp.dma_start(wout[:, :, :], w_out.rearrange("(c p) n -> p c n", p=P)).then_inc(w_in, 16)
            sp.dma_start(lnv[:, :, :], ln).then_inc(w_in, 16)
            if rotary:
                sp.dma_start(sb["Wgu"][:, :, :, :], sb["gate_up_d"].rearrange("(c p) e n -> p c e n", p=P)
                             ).then_inc(sb["wgu_in"], 16)
            if not rotary:
                def batch(b):
                    sp.wait_ge(nmT_ready, b + 1)
                    sp.dma_start(sb["max_d"], nmT[:, :]).then_inc(max_out, 16)
                    sp.wait_ge(max_out, 16 * b + 16)
                    sp.dma_start(st[KS:KR, 0, :, :], sb["max_d"].rearrange("(a h) t -> a h t", a=3)).then_inc(max_rows, 16)

                batch(0)
                with sp.Fori(1, NB) as b:
                    batch(b)
                sp.wait_ge(max_rows, 16 * NB)

        @block.gpsimd
        def _(pool):
            pool.memset(Vs[:, :, :, HD:HD + 1], 1.0).then_inc(v_ones, 1)
            pool.memset(Vs[:, :, :, HD + 1:32], 0.0).then_inc(v_ones, 1)
            if not rotary:
                pool.memset(nms[:, :, :, :], 0.0).then_inc(v_ones, 1)
                pool.wait_ge(v_ones, 3)
                pool.memset(st[KS:KR, 1, :, :], 1.0).then_inc(v_ones, 1)
            pool.wait_ge(v_ones, 2 if rotary else 4)
            pool.wait_ge(w_in, 48)
            PER = TJ if rotary else 0

            def add_rotated(b, j):
                pool.wait_ge(rot_parts, TJ * b + j + 1)
                pool.tensor_tensor(qk[:, j, :], qk[:, j, :], tmp[:, j % 2, :], ALU.add).then_inc(rotated, 1)

            def subtract_high(b, j):
                v = qk[:, j, :].rearrange("p (w h d) -> p w h d", w=2, d=HD)
                pool.wait_ge(hi_ready, TJ * b + j + 1)
                pool.tensor_tensor(v, v, stk[:, j, :, :, 0:HD], ALU.subtract).then_inc(rest_ready, 1)

            def subtract_middle(b, j):
                v = qk[:, j, :].rearrange("p (w h d) -> p w h d", w=2, d=HD)
                pool.wait_ge(rest_ready, TJ * b + j + 1)
                pool.wait_ge(mid_ready, TJ * b + j + 1)
                for w, at in ((0, Q_PARTS), (1, K_PARTS)):
                    pool.tensor_tensor(parts(stk[:, j], w, at["l"][0]), v[:, w], parts(stk[:, j], w, at["m"][0]),
                                       ALU.subtract).then_inc(lo_ready, 1)

            def scale_and_bias(b, j, own):
                pool.wait_ge(scaled, TJ * b + j + 1)
                v = qk[:, j, :].rearrange("p (h d) -> p h d", d=HD)
                pool.tensor_tensor(v, v, lnv[:, 0:1, :].broadcast_to((P, 2 * H, HD)), ALU.mult).then_inc(pool_done, 1)
                pool.wait_ge(pool_done, own.next())
                pool.tensor_tensor(v, v, lnv[:, 1:2, :].broadcast_to((P, 2 * H, HD)), ALU.add).then_inc(normed, 1)

            def prepare(b, t, own):
                if rotary:
                    for j in stage(t, AT_ADD):
                        add_rotated(b, j)
                    for j in stage(t, AT_SCALE):
                        scale_and_bias(b, j, own)
                for j in stage(t, AT_REST):
                    subtract_high(b, j)
                for j in stage(t, AT_LOW):
                    subtract_middle(b, j)

            def turn(b, more):
                own = Count(pool_done, (b + 1) * PER, PER)
                u = 0
                for g in range(HG):
                    for n, (qc, mt, off, w, diag) in enumerate(UNITS):
                        u += 1
                        if rotary and diag:
                            pool.wait_ge(s_read, NUB * b + u)
                            d = s2[:, (u - 1) % 3, :, 0:P]
                            m = keep[:, :].rearrange("p (o n) -> p o n", o=1).broadcast_to((P, 4, P))
                            pool.tensor_tensor(d, d, m, ALU.mult).then_inc(s_masked, 1)
                        if more:
                            prepare(b + 1, u - 1, own)
                if more:
                    for t in range(LATE):
                        prepare(b + 1, SLOTS + t, own)

            first = Count(pool_done, 0, PER)
            for t in range(SLOTS + LATE):
                prepare(0, t, first)
            turn(0, True)
            with pool.Fori(1, NB - 1) as b:
                turn(b, True)
            turn(NB - 1, False)

        @block.scalar
        def _(act):
            act.wait_ge(stats_ready, 1)
            act.activation(rstd[:, :], mv[:, :, 1], ACT.Sqrt).then_inc(std0_ready, 1)

            def transposed_x(b, j):
                act.wait_ge(xT_psum, TJ * b + j + 1)
                wait(act, qkv_psum, TJ * b + j)
                act.activation(xT[:, :], p_xT.rearrange("p (c n) -> p c n", c=2), ACT.Copy).then_inc(xT_ready, 1)

            def values(b, j):
                act.wait_ge(v_psum, TJ * b + j + 1)
                if j == 0:
                    wait(act, vs_ready, b)
                act.activation(v_next[:, j, :], p_v, ACT.Copy).then_inc(v_ready, 1)

            def move_values(b):
                wait(act, pv_done, NUB * b)
                act.wait_ge(v_ready, TJ * b + TJ)
                act.activation(Vs[:, :, :, 0:HD], v_next[:, :, :].rearrange("p j (h d) -> p j h d", d=HD), ACT.Copy
                               ).then_inc(vs_ready, 1)

            def high(b, j):
                act.wait_ge(normed if rotary else qk_read, TJ * b + j + 1)
                wait(act, stK_psum, TJ * (b - 1) + j + 1)
                v = qk[:, j, :].rearrange("p (w h d) -> p w h d", w=2, d=HD)
                act.activation(stk[:, j, :, :, 0:HD], v, ACT.Copy).then_inc(hi_ready, 1)

            def middle(b, j):
                v = qk[:, j, :].rearrange("p (w h d) -> p w h d", w=2, d=HD)
                act.wait_ge(rest_ready, TJ * b + j + 1)
                act.activation(parts(stk[:, j], 0, Q_PARTS["m"][0]), v[:, 0], ACT.Copy)
                act.activation(parts(stk[:, j], 1, K_PARTS["m"][0]), v[:, 1], ACT.Copy).then_inc(mid_ready, 1)

            def prepare(b, t):
                for j in stage(t, AT_X):
                    transposed_x(b, j)
                for j in stage(t, AT_VALUES):
                    values(b, j)
                if rotary:
                    for j in stage(t, AT_SQUARE):
                        act.wait_ge(centred, TJ * b + j + 1)
                        act.activation(tmp[:, j % 2, :], qk[:, j, :], ACT.Square).then_inc(squared, 1)
                    for j in stage(t, AT_STD):
                        act.wait_ge(var_ready, TJ * b + j + 1)
                        act.activation(std[:, j % 2, :], msum[:, j, :], ACT.Sqrt).then_inc(std_ready, 1)
                for j in stage(t, AT_HIGH):
                    high(b, j)
                for j in stage(t, AT_MID):
                    middle(b, j)

            def turn(b, more):
                if not rotary:
                    act.wait_ge(nmT_psum, b + 1)
                    act.activation(nmT[:, :], miscb[0:3 * H, 0:T], ACT.Copy).then_inc(nmT_ready, 1)
                u = 0
                for g in range(HG):
                    for n, (qc, mt, off, w, diag) in enumerate(UNITS):
                        u += 1
                        act.wait_ge(s_psum, NUB * b + u)
                        src = scores[(u - 1) % 2][:, :, 0:w]
                        if rotary:
                            if u > 2:
                                act.wait_ge(p_ready, NUB * b + u - 2)
                            act.activation(s2[:, (u - 1) % 3, :, 0:w], src, ACT.Square).then_inc(s_read, 1)
                        else:
                            if u > 3:
                                act.wait_ge(pv_done, NUB * b + u - 3)
                            act.activation(pr[:, (u - 1) % 3, :, 0:w], src, ACT.Exp).then_inc(p_ready, 1)
                        if n == BEHIND - 1 and g >= 1:
                            evac_out(act, b, 2 * g - 1)
                        if n == BEHIND + 1:
                            evac_out(act, b, 2 * g)
                        if more:
                            prepare(b + 1, u - 1)
                evac_out(act, b, NQ - 1)
                if more:
                    for t in range(LATE):
                        prepare(b + 1, SLOTS + t)
                    move_values(b + 1)
                for j in range(TJ):
                    act.wait_ge(zT_psum, TJ * b + j + 1)
                    act.activation(zT[:, j % 2], p_zT[j % 2].rearrange("p (c n) -> p c n", c=2), ACT.Copy
                                   ).then_inc(zT_ready, 1)
                    if more:
                        evac_stack(act, b + 1, j)

            for t in range(SLOTS + LATE):
                prepare(0, t)
            act.wait_ge(v_ones, 2)
            move_values(0)
            for j in range(TJ):
                evac_stack(act, 0, j)
            turn(0, True)
            with act.Fori(1, NB - 1) as b:
                turn(b, True)
            turn(NB - 1, False)

        @block.tensor
        def _(pe):
            pe.wait_ge(w_in, 48)
            if not rotary:
                pe.wait_ge(v_ones, 4)
            def turn_x(b, j):
                pe.wait_ge(xn_ready, TJ * b + j + 1)
                wait(pe, v_ready, TJ * b + j)
                if j == 0:
                    wait(pe, zT_ready, TJ * (b - 1))
                for c in range(2):
                    mm = pe.transpose(p_xT[:, c * P:(c + 1) * P], xn[:, c * P:(c + 1) * P], ident)
                mm.then_inc(xT_psum, 1)

            def project_v(b, j):
                pe.wait_ge(xT_ready, TJ * b + j + 1)
                for c in range(2):
                    mm = pe.matmul(p_v, xT[:, c, :], wqkv[:, c, QK:], start=(c == 0), stop=(c == 1))
                mm.then_inc(v_psum, 1)

            def project_qk(b, j):
                wait(pe, rot_parts if rotary else qk_read, TJ * b + j)
                for c in range(2):
                    mm = pe.matmul(p_qk, xT[:, c, :], wqkv[:, c, 0:QK], start=(c == 0), stop=(c == 1))
                mm.then_inc(qkv_psum, 1)

            def prepare(b, t):
                for j in stage(t, AT_TURN):
                    turn_x(b, j)
                for j in stage(t, AT_VALUES):
                    project_v(b, j)
                for j in stage(t, AT_PROJECT):
                    project_qk(b, j)

            def transpose_stack(b, j):
                pe.wait_ge(stack_ready, TJ * b + j + 1)
                pe.wait_ge(lo_ready, 2 * (TJ * b + j + 1))
                if j == 0:
                    wait(pe, s_read if rotary else p_ready, NUB * b)
                for w, evacuated, done in ((0, stA_ready, stQ_psum), (1, stD_ready, stK_psum)):
                    wait(pe, evacuated, TJ * b + j)
                    for h in range(H):
                        mm = pe.transpose(stackT[0:KS, 2 * w + h // 8, (h % 8) * P:(h % 8 + 1) * P],
                                          stk[:, j, w, h, :], ident_bf[:, :])
                    mm.then_inc(done, 1)

            def turn(b, more):
                pe.wait_ge(stA_ready, TJ * b + TJ)
                pe.wait_ge(stD_ready, TJ * b + TJ)
                if not rotary:
                    pe.wait_ge(v_ready, TJ * b + TJ)
                    pe.wait_ge(qk_read, TJ * b + TJ)
                    n = 0
                    for j in range(TJ):
                        for hp in range(H // 2):
                            n += 1
                            if n > len(max_banks):
                                pe.wait_ge(m_read, NMB * b + n - len(max_banks))
                            for i in range(2):
                                h = 2 * hp + i
                                bank = max_banks[(n - 1) % len(max_banks)] + i
                                pe.matmul(ps[:, bank, 0:(j + 1) * P], st[0:KS, 0, h, j * P:(j + 1) * P],
                                          st[0:KS, 1, h, 0:(j + 1) * P], start=True, stop=False)
                                mm = pe.matmul(ps[:, bank, j * P:(j + 1) * P], ident_bf[:, :], mask_bf[:, :],
                                               start=False, stop=True)
                            mm.then_inc(m_psum, 1)
                    pe.wait_ge(nms_ready, b + 1)
                    for j in range(TJ):
                        mm = pe.transpose(miscb[:, j * P:(j + 1) * P],
                                          nms[:, j].rearrange("p a h -> p (a h)"), ident_bf[:, :])
                    mm.then_inc(nmT_psum, 1)
                    pe.wait_ge(m_read, NMB * b + NMB)
                    pe.wait_ge(max_rows, 16 * b + 16)
                pe.wait_ge(vs_ready, b + 1)
                wait(pe, x_added, TJ * b)
                u = 0
                todo = []
                for g in range(HG):
                    for n, (qc, mt, off, w, diag) in enumerate(UNITS):
                        u += 1
                        if u > 2:
                            pe.wait_ge(s_read if rotary else p_ready, NUB * b + u - 2)
                        for i in range(4):
                            h = 4 * g + i
                            masked = diag and not rotary
                            mm = pe.matmul(scores[(u - 1) % 2][:, i, 0:w], st[0:KR, 1, h, mt * P:(mt + 1) * P],
                                           st[0:KR, 0, h, qc * 256 + off:qc * 256 + off + w], start=True, stop=not masked)
                            if masked:
                                mm = pe.matmul(scores[(u - 1) % 2][:, i, 0:P], ident_bf[:, :], maskT_bf[:, :],
                                               start=False, stop=True)
                        mm.then_inc(s_psum, 1)
                        todo.append((g, u, qc, mt, off, w))
                        if len(todo) > BEHIND:
                            weigh(pe, b, *todo.pop(0))
                        if more:
                            prepare(b + 1, u - 1)
                while todo:
                    weigh(pe, b, *todo.pop(0))
                turn_out(pe, b, NQ - 1)
                for j in range(TJ):
                    pe.wait_ge(o_read, NQ * b + NQ)
                    if j >= 2:
                        pe.wait_ge(zT_ready, TJ * b + j - 1)
                    elif more:
                        pe.wait_ge(v_ready, TJ * b + 2 * TJ)
                        pe.wait_ge(rot_parts if rotary else qk_read, TJ * b + 2 * TJ)
                    for c in range(2):
                        mm = pe.transpose(p_zT[j % 2][:, c * P:(c + 1) * P], z[:, j, c * P:(c + 1) * P], ident)
                    mm.then_inc(zT_psum, 1)
                    if more:
                        transpose_stack(b + 1, j)
                    pe.wait_ge(zT_ready, TJ * b + j + 1)
                    if j >= 2:
                        pe.wait_ge(x_added, TJ * b + j - 1)
                    for c in range(2):
                        mm = pe.matmul(p_o[j % 2], zT[:, j % 2, c, :], wout[:, c, :], start=(c == 0), stop=(c == 1))
                    mm.then_inc(y_psum, 1)

            for t in range(SLOTS + LATE):
                prepare(0, t)
            for j in range(TJ):
                transpose_stack(0, j)
            turn(0, True)
            with pe.Fori(1, NB - 1) as b:
                turn(b, True)
            turn(NB - 1, False)

        @block.vector
        def _(v):
            for n in range(NT):
                v.bn_stats(stats[:, n, :], X[:, n, :]).then_inc(bn_done, 1)
            v.wait_ge(bn_done, NT)
            for n in range(NT):
                v.bn_aggr(mv[:, n, :], stats[:, n, :]).then_inc(bn_done, 1)
            v.wait_ge(bn_done, 2 * NT)
            v.tensor_scalar(mv[:, :, 1], mv[:, :, 1], EPS, None, ALU.add).then_inc(stats_ready, 1)
            v.wait_ge(std0_ready, 1)
            inverse_root(v, rstd, rt, mv[:, :, 1], rstd0_ready)
            v.wait_ge(rstd0_ready, 5)
            PER = NQ + (0 if rotary else 3)
            PREP = 6 * TJ if rotary else 0

            def standardise(b, j):
                wait(v, xT_psum, TJ * b + j)
                x = X[:, bass.ds(TJ * b + j, 1), :].rearrange("p o d -> p (o d)")
                v.tensor_scalar(xn[:, :], x, mv[:, bass.ds(TJ * b + j, 1), 0:1].rearrange("p o d -> p (o d)"),
                                rstd[:, bass.ds(TJ * b + j, 1)], ALU.subtract, ALU.mult).then_inc(xn_ready, 1)

            def copy_qk(b, j):
                v.wait_ge(qkv_psum, TJ * b + j + 1)
                v.tensor_scalar(qk[:, j, 0:D], p_qk[:, 0:D], HD ** -0.5, None, ALU.mult)
                v.tensor_copy(qk[:, j, D:QK], p_qk[:, D:QK]).then_inc(qk_read, 1)

            def centre(b, j, own):
                hv = qk[:, j, :].rearrange("p (h d) -> p h d", d=HD)
                v.wait_ge(rotated, TJ * b + j + 1)
                v.tensor_reduce(msum[:, j, :], hv, AX.X, ALU.add).then_inc(prep_done, 1)
                v.wait_ge(prep_done, own.next())
                m = msum[:, j, :].rearrange("p (h o) -> p h o", o=1).broadcast_to((P, 2 * H, HD))
                v.scalar_tensor_tensor(out=hv, in0=m, scalar=-1.0 / HD, in1=hv, op0=ALU.mult, op1=ALU.add
                                       ).then_inc(centred, 1)

            def variance(b, j, own):
                v.wait_ge(squared, TJ * b + j + 1)
                v.wait_ge(centred, TJ * b + j + 1)
                v.tensor_reduce(msum[:, j, :], tmp[:, j % 2, :].rearrange("p (h d) -> p h d", d=HD),
                                AX.X, ALU.add).then_inc(prep_done, 1)
                v.wait_ge(prep_done, own.next())
                v.tensor_scalar(msum[:, j, :], msum[:, j, :], 1.0 / HD, EPS, ALU.mult, ALU.add).then_inc(var_ready, 1)

            def divide(b, j, own):
                def then(ins):
                    ins.then_inc(prep_done, 1)
                    v.wait_ge(prep_done, own.next())

                y, t = std[:, j % 2, :], root[:, j % 2, :]
                v.wait_ge(std_ready, TJ * b + j + 1)
                then(v.reciprocal(y, y))
                then(v.scalar_tensor_tensor(out=t, in0=y, scalar=-0.5, in1=y, op0=ALU.mult, op1=ALU.mult))
                then(v.tensor_tensor(t, t, msum[:, j, :], ALU.mult))
                then(v.scalar_tensor_tensor(out=y, in0=t, scalar=1.5, in1=y, op0=ALU.add, op1=ALU.mult))
                hv = qk[:, j, :].rearrange("p (h d) -> p h d", d=HD)
                r = y.rearrange("p (h o) -> p h o", o=1).broadcast_to((P, 2 * H, HD))
                v.tensor_tensor(hv, hv, r, ALU.mult).then_inc(scaled, 1)

            def repeat_parts(b, j):
                v.wait_ge(hi_ready, TJ * b + j + 1)
                v.wait_ge(mid_ready, TJ * b + j + 1)
                for w, at in ((0, Q_PARTS), (1, K_PARTS)):
                    for p in "hm":
                        for s in at[p][1:]:
                            last = v.tensor_copy(parts(stk[:, j], w, s), parts(stk[:, j], w, at[p][0]))
                last.then_inc(stack_ready, 1)

            def keys_stack(b, j):
                v.wait_ge(stK_psum, TJ * b + j + 1)
                v.tensor_copy(st[0:KS, 1, :, j * P:(j + 1) * P],
                              stackT[0:KS, 2:4, :].rearrange("p g (h n) -> p (g h) n", n=P)).then_inc(stD_ready, 1)

            def prepare(b, t, own):
                for j in stage(t, AT_NORM):
                    standardise(b, j)
                for j in stage(t, AT_READ):
                    if rotary:
                        rotate(v, b, j)
                    else:
                        copy_qk(b, j)
                if rotary:
                    for j in stage(t, AT_VAR):
                        variance(b, j, own)
                    for j in stage(t, AT_DIVIDE):
                        divide(b, j, own)
                    for j in stage(t, AT_CENTRE):
                        centre(b, j, own)
                for j in stage(t, AT_LOW):
                    repeat_parts(b, j)

            def turn(b, more):
                own = Count(dve_done, b * PER, PER)
                ahead = Count(prep_done, (b + 1) * PREP, PREP)
                if not rotary:
                    n = 0
                    for j in range(TJ):
                        for hp in range(H // 2):
                            n += 1
                            v.wait_ge(m_psum, NMB * b + n)
                            bank = max_banks[(n - 1) % len(max_banks)]
                            v.tensor_reduce(nm[:, j, 2 * hp:2 * hp + 2], ps[:, bank:bank + 2, 0:(j + 1) * P],
                                            AX.X, ALU.max, negate=True).then_inc(m_read, 1)
                    v.wait_ge(m_read, NMB * b + NMB)
                    v.tensor_copy(nms[:, :, 0, :], nm[:, :, :]).then_inc(dve_done, 1)
                    v.wait_ge(dve_done, own.next())
                    v.tensor_tensor(nmr[:, :, :], nm[:, :, :], nms[:, :, 0, :], ALU.subtract).then_inc(dve_done, 1)
                    v.wait_ge(dve_done, own.next())
                    v.tensor_copy(nms[:, :, 1, :], nmr[:, :, :]).then_inc(dve_done, 1)
                    v.wait_ge(dve_done, own.next())
                    v.tensor_tensor(nms[:, :, 2, :], nmr[:, :, :], nms[:, :, 1, :], ALU.subtract).then_inc(nms_ready, 1)
                u = diags = 0
                for g in range(HG):
                    for n, (qc, mt, off, w, diag) in enumerate(UNITS):
                        u += 1
                        if rotary:
                            v.wait_ge(s_read, NUB * b + u)
                            if diag:
                                diags += 1
                                v.wait_ge(s_masked, 4 * HG * b + diags)
                            if u > 3:
                                v.wait_ge(pv_done, NUB * b + u - 3)
                            s = s2[:, (u - 1) % 3, :, 0:w]
                            v.tensor_tensor(pr[:, (u - 1) % 3, :, 0:w], s, s, ALU.mult).then_inc(p_ready, 1)
                        if n in (BEHIND - 1, BEHIND + 1) and g >= 1:
                            normalise(v, b, 2 * g - 2 + (n > BEHIND), own)
                        if more:
                            prepare(b + 1, u - 1, ahead)
                if more:
                    for t in range(LATE):
                        prepare(b + 1, SLOTS + t, ahead)
                normalise(v, b, NQ - 2, own)
                normalise(v, b, NQ - 1, own)
                for j in range(TJ):
                    if more:
                        keys_stack(b + 1, j)
                    v.wait_ge(y_psum, TJ * b + j + 1)
                    x = X[:, bass.ds(TJ * b + j, 1), :].rearrange("p o d -> p (o d)")
                    v.tensor_tensor(x, x, p_o[j % 2], ALU.add).then_inc(x_added, 1)
                own.close()

            first = Count(prep_done, 0, PREP)
            for t in range(SLOTS + LATE):
                prepare(0, t, first)
            for j in range(TJ):
                keys_stack(0, j)
            turn(0, True)
            with v.Fori(1, NB - 1) as b:
                turn(b, True)
            turn(NB - 1, False)
    return sems


def experts(nc, sb, xs_d, y_d, down_d, tag):
    X, ps, const, Wgu = sb["X"], sb["ps"], sb["const"], sb["Wgu"]
    before_bf, ones_bf = sb["before_bf"], sb["ones_bf"]
    ident = const[:, C_AT[C_ID]:C_AT[C_ID] + P]
    io = C_AT[C_IOTA]
    iota_e, steps, iota_p = const[:, io:io + E], const[:, io + E:io + E + 16], const[:, io + E + 16:io + E + 17]
    res_c = const[:, C_AT[C_RES]:C_KEPT].rearrange("p (t k) -> p t k", k=K)
    RING, BACK = 8, 8
    CLS = bass.IndirectOffsetOnAxis

    sems = []
    with ExitStack() as ctx:
        def buf(name, shape, dt=F32):
            return ctx.enter_context(nc.sbuf_tensor(f"{name}_{tag}_sb", shape, dt))

        def sem(name):
            sems.append(nc.alloc_semaphore(f"{name}_{tag}"))
            return sems[-1]

        Wd = buf("Wd", [P, E + 1, D])
        stats, mv, rstd = buf("stats", [P, NT, 6]), buf("mv", [P, NT, 2]), buf("rstd", [P, NT])
        rt = buf("rt", [P, NT])
        pad, padp = buf("pad", [P, 1]), buf("padp", [P, 1])
        rows = buf("rows", [P, NT, ROW])
        xT_all = buf("xT_all", [P, 2, NT, P])
        s_gu, s_sg = buf("s_gu", [P, 2, T]), buf("s_sg", [P, T])
        xT = buf("xT", [P, 2, 2, P])
        gu, sg, h, hT = buf("gu", [P, 4, 2 * I]), buf("sg", [P, 4, I]), buf("h", [P, 2, I]), buf("hT", [P, 2, P])
        mag, ex, lg1, sp = (buf(n, [P, NT * E]) for n in ("mag", "ex", "lg1", "sp"))
        score, biased = buf("score", [P, NT, E]), buf("biased", [P, TJ, E])
        top = buf("top", [P, TJ, 8])
        topi = buf("topi", [P, TJ, 8], U32)
        topf = buf("topf", [P, TJ, K])
        hot, prod = buf("hot", [P, TJ, K, E]), buf("prod", [P, TJ, K, E])
        mask = buf("mask", [P, TJ, E], BF16)
        place, place0 = buf("place", [P, TJ, E]), buf("place0", [P, E])
        count, base = buf("count", [P, E]), buf("base", [P, E])
        picked, total, posf = buf("picked", [P, TJ, K]), buf("total", [P, TJ]), buf("posf", [P, TJ, K])
        posi = buf("posi", [P, NT, K], I32)
        weight = buf("weight", [P, NT, K])
        dummy = buf("dummy", [P, ROW])
        many = buf("many", [P, E, 16])
        tiles_e, ends, starts, one_e = (buf(n, [P, E]) for n in ("tiles_e", "ends", "starts", "one_e"))
        hot_e = buf("hot_e", [P, E])
        meta = buf("meta", [P, 8])
        diag, ones = buf("diag", [P, P]), buf("ones", [P, P])
        tile_e = buf("tile_e", [P, P])
        plan = buf("plan", [1, 2, P], I32)
        tails = buf("tails", [1, E], I32)
        xs = buf("xs", [P, RING, ROW])
        ys = rows[:, :, :].rearrange("p t r -> p (t r)")[:, 0:RING * D].rearrange("p (q d) -> p q d", q=RING)
        toi = buf("toi", [P, RING], I32)
        tof = buf("tof", [P, RING])
        to4 = buf("to4", [P, RING, K])
        halves = [xT_all[:, :, :, :].rearrange("p c t n -> p (c t n)"),
                  rows[:, :, :].rearrange("p t r -> p (t r)")[:, 0:BACK // 2 * K * D]]
        yk = [halves[q * 2 // BACK].rearrange("p (q k d) -> p q k d", k=K, d=D)[:, q % (BACK // 2)] for q in range(BACK)]
        router = buf("router", [P, 2, E])
        bias = buf("bias", [P, E])

        p_logit = ps[:, 0, :]
        p_rank = ps[:, 1, 0:TJ * E]
        p_total = ps[:, 1, TJ * E:(TJ + 1) * E]
        p_gu = [ps[:, 2 + k, 0:2 * I] for k in range(2)]
        p_y = [ps[:, 4 + k, 0:D] for k in range(2)]
        p_xT = [ps[:, 6 + k, 0:D] for k in range(2)]
        p_hT = [ps[:, k, 0:P] for k in range(2)]
        p_sgu = [ps[:, 2 + k, :] for k in range(2)]

        w_in, wd_in, set_up = sem("w_in"), sem("wd_in"), sem("set_up")
        dve_done, stats_ready, rstd_ready, xn_ready = sem("dve_done"), sem("stats_ready"), sem("rstd_ready"), sem("xn_ready")
        bn_done, soft_part = sem("bn_done"), sem("soft_part")
        xT_psum, xT_ready, gu_psum, clipped = sem("xT_psum"), sem("xT_ready"), sem("gu_psum"), sem("clipped")
        sig_ready, h_ready = sem("sig_ready"), sem("h_ready")
        y_psum, x_added = sem("y_psum"), sem("x_added")
        logit_psum, mag_ready, ex_ready, plus1, ln_ready = (
            sem("logit_psum"), sem("mag_ready"), sem("ex_ready"), sem("plus1"), sem("ln_ready"))
        soft_ready, score_ready, mask_ready, rank_psum, pos_ready = (
            sem("soft_ready"), sem("score_ready"), sem("mask_ready"), sem("rank_psum"), sem("pos_ready"))
        sent = sem("sent")
        dummy_ready, meta_ready, plan_psum, plan_ready, tails_in = (
            sem("dummy_ready"), sem("meta_ready"), sem("plan_psum"), sem("plan_ready"), sem("tails_in"))
        loaded = [sem(f"loaded{k}") for k in range(RING)]
        stored = [sem(f"stored{k}") for k in range(RING)]
        t_xT_psum, t_xT, t_gu_psum, t_clip = sem("t_xT_psum"), sem("t_xT"), sem("t_gu_psum"), sem("t_clip")
        t_sig, t_h, t_hT_psum, t_hT = sem("t_sig"), sem("t_h"), sem("t_hT_psum"), sem("t_hT")
        t_y_psum, t_y, t_to, t_acc = sem("t_y_psum"), sem("t_y"), sem("t_to"), sem("t_acc")
        back = [sem(f"back{k}") for k in range(BACK)]
        summed = sem("summed")

        def turns(eng, step, n_lag):
            for g in range(2):
                for u in range(RING):
                    step(eng, g, u)
            with eng.Fori(2, MT // RING) as g:
                for u in range(RING):
                    step(eng, g, u)
            for u in range(n_lag):
                step(eng, MT // RING, u)

        def at(g, u, lag):
            i = RING * g + (u - lag)
            if isinstance(g, int) and not 0 <= i < MT:
                return None
            return i, (u - lag) % RING, g + (u - lag) // RING

        L_UP, L_SIG, L_H, L_TH, L_DOWN = 1, 2, 2, 3, 4

        def sp_step(sp, g, u):
            i, q, turn = at(g, u, 0)
            row = sp.value_load(plan[0:1, 1, bass.ds(i, 1)], min_val=0, max_val=E * REG)
            if not isinstance(g, int) or g >= 1:
                sp.wait_ge(t_xT_psum, i - RING + 1)
                sp.wait_ge(t_acc, i - RING + 1)
            sp.dma_start(xs[:, q, :], xs_d[bass.ds(row, P), :]).then_inc(loaded[q], 16)

        expert = {}

        def expert_of(pe, i, k):
            if k not in expert:
                expert[k] = pe.value_load(plan[0:1, 0, bass.ds(i, 1)], min_val=0, max_val=E - 1)
            return expert[k]

        def pe_step(pe, g, u):
            if u == 0:
                expert.clear()
            a = at(g, u, 0)
            if a:
                i, q, turn = a
                pe.wait_ge(loaded[q], 16 * (turn + 1))
                if not isinstance(i, int) or i >= 2:
                    pe.wait_ge(t_xT, i - 1)
                for c in range(2):
                    mm = pe.transpose(p_xT[q % 2][:, c * P:(c + 1) * P], xs[:, q, c * P:(c + 1) * P], ident)
                mm.then_inc(t_xT_psum, 1)
            a = at(g, u, L_UP)
            if a:
                i, q, turn = a
                e = expert_of(pe, i, u - L_UP)
                pe.wait_ge(t_xT, i + 1)
                if not isinstance(i, int) or i >= 2:
                    pe.wait_ge(t_clip, i - 1)
                for c in range(2):
                    mm = pe.matmul(p_gu[q % 2], xT[:, q % 2, c, :],
                                   Wgu[:, c, bass.ds(e, 1), :].rearrange("p o n -> p (o n)"), start=(c == 0), stop=(c == 1))
                mm.then_inc(t_gu_psum, 1)
            a = at(g, u, L_TH)
            if a:
                i, q, turn = a
                pe.wait_ge(t_h, i + 1)
                if not isinstance(i, int) or i >= 2:
                    pe.wait_ge(t_hT, i - 1)
                pe.transpose(p_hT[q % 2], h[:, q % 2, :], ident).then_inc(t_hT_psum, 1)
            a = at(g, u, L_DOWN)
            if a:
                i, q, turn = a
                e = expert_of(pe, i, u - L_DOWN)
                pe.wait_ge(t_hT, i + 1)
                if not isinstance(i, int) or i >= 2:
                    pe.wait_ge(t_y, i - 1)
                pe.matmul(p_y[q % 2], hT[:, q % 2, :], Wd[:, bass.ds(e, 1), :].rearrange("p o n -> p (o n)"),
                          start=True, stop=True).then_inc(t_y_psum, 1)

        def act_step(act, g, u):
            a = at(g, u, 0)
            if a:
                i, q, turn = a
                act.wait_ge(t_xT_psum, i + 1)
                if not isinstance(i, int) or i >= 2:
                    act.wait_ge(t_gu_psum, i - 1)
                act.activation(xT[:, q % 2], p_xT[q % 2].rearrange("p (c n) -> p c n", c=2), ACT.Copy).then_inc(t_xT, 1)
            a = at(g, u, L_SIG)
            if a:
                i, q, turn = a
                act.wait_ge(t_clip, i + 1)
                if not isinstance(i, int) or i >= 4:
                    act.wait_ge(t_h, i - 3)
                act.activation(sg[:, q % 4, :], gu[:, q % 4, 0:I], ACT.Sigmoid).then_inc(t_sig, 1)
            a = at(g, u, L_TH)
            if a:
                i, q, turn = a
                act.wait_ge(t_hT_psum, i + 1)
                if not isinstance(i, int) or i >= 2:
                    act.wait_ge(t_y_psum, i - 1)
                act.activation(hT[:, q % 2, :], p_hT[q % 2], ACT.Copy).then_inc(t_hT, 1)

        def dve_step(v, g, u):
            a = at(g, u, L_UP)
            if a:
                i, q, turn = a
                v.wait_ge(t_gu_psum, i + 1)
                if not isinstance(i, int) or i >= 4:
                    v.wait_ge(t_h, i - 3)
                v.tensor_scalar(gu[:, q % 4, :], p_gu[q % 2], CLIP, -CLIP, ALU.min, ALU.max).then_inc(t_clip, 1)
                v.wait_ge(loaded[q], 16 * (turn + 1))
                v.scalar_tensor_tensor(out=to4[:, q, :], in0=xs[:, q, D:D + K], scalar=tile_e[:, bass.ds(i, 1)],
                                       in1=xs[:, q, D + K:ROW], op0=ALU.is_equal, op1=ALU.mult,
                                       accum_out=tof[:, q:q + 1]).then_inc(t_acc, 1)
            a = at(g, u, L_H)
            if a:
                i, q, turn = a
                v.wait_ge(t_sig, i + 1)
                v.tensor_tensor(sg[:, q % 4, :], sg[:, q % 4, :], gu[:, q % 4, 0:I], ALU.mult).then_inc(t_gs, 1)
            a = at(g, u, L_UP)
            if a:
                i, q, turn = a
                v.wait_ge(t_acc, i + 1)
                if not isinstance(i, int) or i >= RING:
                    v.wait_ge(stored[q], 16 * turn)
                v.tensor_scalar(toi[:, q:q + 1], tof[:, q:q + 1], FAR, None, ALU.add).then_inc(t_to, 1)
            a = at(g, u, L_H)
            if a:
                i, q, turn = a
                v.wait_ge(t_gs, i + 1)
                if not isinstance(i, int) or i >= 2:
                    v.wait_ge(t_hT_psum, i - 1)
                v.tensor_tensor(h[:, q % 2, :], sg[:, q % 4, :], gu[:, q % 4, I:], ALU.mult).then_inc(t_h, 1)
            a = at(g, u, L_DOWN)
            if a:
                i, q, turn = a
                v.wait_ge(t_y_psum, i + 1)
                if not isinstance(i, int) or i >= RING:
                    v.wait_ge(stored[q], 16 * turn)
                v.tensor_copy(ys[:, q, :], p_y[q % 2]).then_inc(t_y, 1)

        def absorb(pool, n):
            wait(pool, absorbed, n)
            pool.tensor_tensor(padp[:, :], base[:, 0:1], base[:, 0:1], ALU.add).then_inc(absorbed, 1)

        def pool_step(pool, g, u):
            a = at(g, u, L_DOWN)
            if a:
                i, q, turn = a
                pool.wait_ge(t_to, i + 1)
                pool.wait_ge(t_y, i + 1)
                absorb(pool, i)
                pool.indirect_dma_start(y_d, CLS(ap=toi[:, q:q + 1], axis=0), ys[:, q, :], None,
                                        bounds_check=NRES - 1, oob_is_err=False).then_inc(stored[q], 16)

        def logits(pe, n):
            pe.wait_ge(xT_ready, n + 1)
            for c in range(2):
                mm = pe.matmul(p_logit[:, n * E:(n + 1) * E], xT_all[:, c, n, :], router[:, c, :],
                               start=(c == 0), stop=(c == 1))
            if n == NT - 1:
                mm.then_inc(logit_psum, 1)

        std_ready = sem("std_ready")
        absorbed, t_gs, h_half, planned, part_sum = sem("absorbed"), sem("t_gs"), sem("h_half"), sem("planned"), sem("part_sum")
        block = ctx.enter_context(nc.Block())

        @block.sync
        def _(sp):
            sp.dma_start(router[:, :, :], sb["router_d"].rearrange("(c p) n -> p c n", p=P)).then_inc(w_in, 16)
            sp.dma_start(bias[:, :], sb["bias_d"]).then_inc(w_in, 16)
            sp.dma_start(Wd[:, :, :], down_d).then_inc(wd_in, 16)
            sp.wait_ge(dummy_ready, 4)
            sp.dma_start(xs_d[E * REG:E * REG + P, :], dummy[:, :]).then_inc(tails_in, 16)
            sp.wait_ge(plan_ready, 3)
            with sp.Fori(0, E) as e:
                row = sp.value_load(tails[0:1, bass.ds(e, 1)], min_val=0, max_val=E * REG)
                sp.dma_start(xs_d[bass.ds(row, P), :], dummy[:, :]).then_inc(tails_in, 16)
            sp.wait_ge(tails_in, 16 * (E + 1))
            sp.wait_ge(sent, 16 * NT * K)
            turns(sp, sp_step, 0)
            for q in range(RING):
                sp.wait_ge(stored[q], 16 * MT // RING)
            y_v = y_d.rearrange("(t p k) d -> p t (k d)", p=P, k=K)
            for g in range(NT // BACK):
                for q in range(BACK):
                    if g >= 1:
                        sp.wait_ge(summed, BACK * (g - 1) + q + 1)
                    sp.dma_start(yk[q].rearrange("p (o k) d -> p o (k d)", o=1), y_v[:, BACK * g + q:BACK * g + q + 1, :]
                                 ).then_inc(back[q], 16)

        @block.gpsimd
        def _(pool):
            pool.memset(ones[:, :], 1.0).then_inc(set_up, 1)
            pool.memset(one_e[:, :], 1.0).then_inc(set_up, 1)
            pool.memset(count[:, :], 0.0).then_inc(set_up, 1)
            pool.memset(dummy[:, 0:D], 0.0).then_inc(dummy_ready, 1)
            pool.memset(dummy[:, D:D + K], -1.0).then_inc(dummy_ready, 1)
            pool.memset(dummy[:, D + K:ROW], 0.0).then_inc(dummy_ready, 1)
            pool.tensor_scalar(base[:, :], iota_e, float(REG), None, ALU.mult).then_inc(dummy_ready, 1)
            pool.wait_ge(set_up, 3)
            pool.wait_ge(dummy_ready, 4)
            for b in range(NB):
                pool.wait_ge(pos_ready, b + 1)
                for j in range(TJ):
                    for k in range(K):
                        pool.indirect_dma_start(xs_d, CLS(ap=posi[:, TJ * b + j, k:k + 1], axis=0),
                                                rows[:, TJ * b + j, :], None).then_inc(sent, 16)
            turns(pool, pool_step, L_DOWN)
            for q in range(RING):
                pool.wait_ge(stored[q], 16 * MT // RING)

        @block.scalar
        def _(act):
            act.wait_ge(stats_ready, 1)
            act.activation(rstd[:, :], mv[:, :, 1], ACT.Sqrt).then_inc(std_ready, 1)
            for n in range(NT):
                act.wait_ge(xT_psum, n + 1)
                act.activation(xT_all[:, :, n, :], p_xT[n % 2].rearrange("p (c n) -> p c n", c=2), ACT.Copy
                               ).then_inc(xT_ready, 1)
            act.wait_ge(logit_psum, 1)
            act.activation(mag[:, :], p_logit, ACT.Abs).then_inc(mag_ready, 1)
            act.wait_ge(mag_ready, 1)
            act.activation(ex[:, :], mag[:, :], ACT.Exp, scale=-1.0).then_inc(ex_ready, 1)
            act.wait_ge(plus1, 1)
            act.activation(lg1[:, :], sp[:, :], ACT.Ln).then_inc(ln_ready, 1)
            act.wait_ge(soft_ready, 1)
            act.activation(score[:, :, :].rearrange("p t e -> p (t e)"), sp[:, :], ACT.Sqrt).then_inc(score_ready, 1)

            def batch(b):
                act.wait_ge(clipped, b + 1)
                wait(act, h_ready, b)
                act.activation(s_sg[:, :], s_gu[:, 0, :], ACT.Sigmoid).then_inc(sig_ready, 1)

            batch(0)
            with act.Fori(1, NB) as b:
                batch(b)
            turns(act, act_step, L_DOWN)

        @block.tensor
        def _(pe):
            pe.wait_ge(w_in, 32)
            for n in range(NT):
                pe.wait_ge(xn_ready, n + 1)
                if n >= 2:
                    pe.wait_ge(xT_ready, n - 1)
                for c in range(2):
                    mm = pe.transpose(p_xT[n % 2][:, c * P:(c + 1) * P], rows[:, n, c * P:(c + 1) * P], ident)
                mm.then_inc(xT_psum, 1)
                if n >= 1:
                    logits(pe, n - 1)
            logits(pe, NT - 1)
            for b in range(NB):
                pe.wait_ge(mask_ready, b + 1)
                pe.matmul(p_rank, before_bf[:, :], mask[:, :, :].rearrange("p t e -> p (t e)"),
                          start=True, stop=False, skip_group_check=True)
                for j in range(TJ - 1):
                    pe.matmul(p_rank[:, (j + 1) * E:].rearrange("p (t e) -> p t e", e=E), ones_bf[:, :],
                              mask[:, j:j + 1, :].broadcast_to((P, TJ - 1 - j, E)), start=False, stop=False,
                              skip_group_check=True)
                for j in range(TJ):
                    mm = pe.matmul(p_total, ones_bf[:, :], mask[:, j, :], start=False, stop=(j == TJ - 1),
                                   skip_group_check=True)
                mm.then_inc(rank_psum, 1)
            pe.wait_ge(meta_ready, 1)
            pe.matmul(ps[0:1, 0, 0:P], meta[:, 6:7], ident, start=True, stop=True)
            pe.matmul(ps[0:1, 0, P:2 * P], meta[:, 5:6], ident, start=True, stop=True)
            pe.matmul(ps[:, 1, 0:P], ones[:, :], diag[:, :], start=True, stop=True).then_inc(plan_psum, 1)
            pe.wait_ge(sb["wgu_in"], 16)
            pe.wait_ge(wd_in, 16)

            def batch(b):
                wait(pe, clipped, b)
                for k in range(2):
                    for c in range(2):
                        mm = pe.matmul(p_sgu[k], Wgu[:, c, E, k * I:(k + 1) * I],
                                       xT_all[:, c, bass.ds(TJ * b, TJ), :].rearrange("p t n -> p (t n)"),
                                       start=(c == 0), stop=(c == 1))
                mm.then_inc(gu_psum, 1)
                pe.wait_ge(h_ready, b + 1)
                for j in range(TJ):
                    if j >= 2:
                        pe.wait_ge(x_added, TJ * b + j - 1)
                    else:
                        wait(pe, x_added, TJ * b)
                    pe.matmul(p_y[j % 2], s_gu[:, 0, j * P:(j + 1) * P], Wd[:, E, :], start=True, stop=True
                              ).then_inc(y_psum, 1)

            batch(0)
            with pe.Fori(1, NB) as b:
                batch(b)
            pe.wait_ge(plan_ready, 3)
            turns(pe, pe_step, L_DOWN)

        @block.vector
        def _(v):
            v.wait_ge(w_in, 32)
            v.wait_ge(set_up, 3)
            v.wait_ge(dummy_ready, 4)
            for n in range(NT):
                v.bn_stats(stats[:, n, :], X[:, n, :]).then_inc(bn_done, 1)
            v.wait_ge(bn_done, NT)
            for n in range(NT):
                v.bn_aggr(mv[:, n, :], stats[:, n, :]).then_inc(bn_done, 1)
            v.wait_ge(bn_done, 2 * NT)
            v.tensor_scalar(mv[:, :, 1], mv[:, :, 1], EPS, None, ALU.add).then_inc(stats_ready, 1)
            v.wait_ge(std_ready, 1)
            inverse_root(v, rstd, rt, mv[:, :, 1], rstd_ready)
            v.wait_ge(rstd_ready, 5)
            for n in range(NT):
                v.tensor_scalar(rows[:, n, 0:D], X[:, n, :], mv[:, n, 0:1], rstd[:, n:n + 1],
                                ALU.subtract, ALU.mult).then_inc(xn_ready, 1)
            v.wait_ge(ex_ready, 1)
            v.tensor_scalar(sp[:, :], ex[:, :], 1.0, None, ALU.add).then_inc(plus1, 1)
            v.wait_ge(plus1, 1)
            v.scalar_tensor_tensor(out=ex[:, :], in0=sp[:, :], scalar=1.0, in1=ex[:, :],
                                   op0=ALU.subtract, op1=ALU.subtract).then_inc(soft_part, 1)
            v.wait_ge(soft_part, 1)
            v.wait_ge(ln_ready, 1)
            v.tensor_tensor(ex[:, :], lg1[:, :], ex[:, :], ALU.subtract).then_inc(soft_part, 1)
            v.wait_ge(soft_part, 2)
            v.scalar_tensor_tensor(out=sp[:, :], in0=p_logit, scalar=0.0, in1=ex[:, :],
                                   op0=ALU.max, op1=ALU.add).then_inc(soft_ready, 1)
            v.wait_ge(score_ready, 1)
            PER = 18

            def batch(b):
                own = Count(dve_done, b * PER, PER)

                def then(ins):
                    ins.then_inc(dve_done, 1)
                    v.wait_ge(dve_done, own.next())

                sc = [score[:, bass.ds(TJ * b + j, 1), :] for j in range(TJ)]
                b4 = bias[:, :].rearrange("p (o e) -> p o e", o=1).broadcast_to((P, TJ, E))
                then(v.tensor_tensor(biased[:, :, :], score[:, bass.ds(TJ * b, TJ), :], b4, ALU.add))
                v.memset(pad[:, :], 0.0)
                for j in range(TJ):
                    last = v.max(top[:, j, :], biased[:, j, :])
                then(last)
                v.memset(pad[:, :], 0.0)
                for j in range(TJ):
                    last = v.max_index(topi[:, j, :], top[:, j, :], biased[:, j, :])
                then(last)
                then(v.tensor_copy(topf[:, :, :], topi[:, :, 0:K]))
                for j in range(TJ):
                    it = iota_e.rearrange("p (o e) -> p o e", o=1).broadcast_to((P, K, E))
                    tk = topf[:, j, :].rearrange("p (k o) -> p k o", o=1).broadcast_to((P, K, E))
                    last = v.tensor_tensor(hot[:, j], it, tk, ALU.is_equal)
                then(last)
                with nc.allow_low_precision(reason="zeros and ones, exact in bf16"):
                    v.tensor_reduce(mask[:, :, :], hot[:, :, :, :].rearrange("p t k e -> p t e k"), AX.X, ALU.add
                                    ).then_inc(mask_ready, 1)
                for j in range(TJ):
                    last = v.tensor_tensor(prod[:, j], hot[:, j], sc[j].broadcast_to((P, K, E)), ALU.mult)
                then(last)
                then(v.tensor_reduce(picked[:, :, :], prod[:, :, :, :], AX.X, ALU.add))
                then(v.tensor_reduce(total[:, :], picked[:, :, :], AX.X, ALU.add))
                then(v.tensor_scalar(total[:, :], total[:, :], 1e-20, None, ALU.add))
                then(v.reciprocal(total[:, :], total[:, :]))
                then(v.tensor_tensor(weight[:, bass.ds(TJ * b, TJ), :], picked[:, :, :],
                                     total[:, :].rearrange("p (t o) -> p t o", o=1).broadcast_to((P, TJ, K)), ALU.mult))
                v.wait_ge(rank_psum, b + 1)
                c4 = place0[:, :].rearrange("p (o e) -> p o e", o=1).broadcast_to((P, TJ, E))
                then(v.tensor_tensor(place0[:, :], base[:, :], count[:, :], ALU.add))
                then(v.tensor_tensor(place[:, :, :], p_rank.rearrange("p (t e) -> p t e", e=E), c4, ALU.add))
                then(v.tensor_tensor(count[:, :], count[:, :], p_total, ALU.add))
                for j in range(TJ):
                    last = v.tensor_tensor(prod[:, j], hot[:, j], place[:, j:j + 1, :].broadcast_to((P, K, E)), ALU.mult)
                then(last)
                then(v.tensor_reduce(posf[:, :, :], prod[:, :, :, :], AX.X, ALU.add))
                then(v.tensor_copy(rows[:, bass.ds(TJ * b, TJ), D:D + K], topf[:, :, :]))
                then(v.tensor_copy(rows[:, bass.ds(TJ * b, TJ), D + K:ROW], res_c[:, bass.ds(TJ * b, TJ), :]))
                v.tensor_copy(posi[:, bass.ds(TJ * b, TJ), :], posf[:, :, :]).then_inc(pos_ready, 1)
                own.close()

            with v.Fori(0, NB) as b:
                batch(b)
            chain = Count(planned)

            def then(ins):
                ins.then_inc(planned, 1)
                v.wait_ge(planned, chain.next())

            v.wait_ge(pos_ready, NB)
            v.wait_ge(dve_done, NB * PER)
            n3 = count[:, :].rearrange("p (e o) -> p e o", o=1).broadcast_to((P, E, 16))
            s3 = steps.rearrange("p (o s) -> p o s", o=1).broadcast_to((P, E, 16))
            then(v.tensor_tensor(many[:, :, :], n3, s3, ALU.is_gt))
            then(v.tensor_reduce(tiles_e[:, :], many[:, :, :], AX.X, ALU.add))
            then(v.tensor_tensor_scan(ends[:, :], one_e[:, :], tiles_e[:, :], 0.0, ALU.mult, ALU.add))
            then(v.tensor_tensor(starts[:, :], ends[:, :], tiles_e[:, :], ALU.subtract))
            then(v.tensor_scalar(hot_e[:, :], ends[:, :], iota_p, None, ALU.is_le))
            then(v.tensor_reduce(meta[:, 0:1], hot_e[:, :], AX.X, ALU.add))
            then(v.scalar_tensor_tensor(out=hot_e[:, :], in0=iota_e, scalar=meta[:, 0:1], in1=starts[:, :],
                                        op0=ALU.is_equal, op1=ALU.mult))
            then(v.tensor_reduce(meta[:, 1:2], hot_e[:, :], AX.X, ALU.add))
            then(v.tensor_tensor(meta[:, 2:3], iota_p, meta[:, 1:2], ALU.subtract))
            then(v.tensor_scalar(meta[:, 2:3], meta[:, 2:3], float(SLOT), -float(E * REG), ALU.mult, ALU.add))
            then(v.scalar_tensor_tensor(out=meta[:, 3:4], in0=meta[:, 0:1], scalar=float(REG), in1=meta[:, 2:3],
                                        op0=ALU.mult, op1=ALU.add))
            then(v.tensor_scalar(meta[:, 4:5], meta[:, 0:1], float(E), None, ALU.is_lt))
            then(v.tensor_tensor(meta[:, 5:6], meta[:, 3:4], meta[:, 4:5], ALU.mult))
            then(v.tensor_scalar(meta[:, 5:6], meta[:, 5:6], float(E * REG), None, ALU.add))
            then(v.tensor_scalar(meta[:, 6:7], meta[:, 0:1], float(E - 1), None, ALU.min))
            then(v.tensor_tensor(place0[:, :], base[:, :], count[:, :], ALU.add))
            v.tensor_scalar(diag[:, :], ident, meta[:, 0:1], None, ALU.mult).then_inc(meta_ready, 1)
            v.tensor_copy(tails[:, :], place0[0:1, :]).then_inc(plan_ready, 1)
            v.wait_ge(plan_psum, 1)
            v.tensor_copy(tile_e[:, :], ps[:, 1, 0:P]).then_inc(plan_ready, 1)
            v.tensor_copy(plan[:, :, :].rearrange("o a n -> o (a n)"), ps[0:1, 0, 0:2 * P]).then_inc(plan_ready, 1)
            v.wait_ge(plan_ready, 3)

            def shared(b):
                v.wait_ge(gu_psum, b + 1)
                wait(v, y_psum, TJ * b)
                for k in range(2):
                    ins = v.tensor_scalar(s_gu[:, k, :], p_sgu[k], CLIP, -CLIP, ALU.min, ALU.max)
                ins.then_inc(clipped, 1)
                v.wait_ge(sig_ready, b + 1)
                v.tensor_tensor(s_gu[:, 0, :], s_sg[:, :], s_gu[:, 0, :], ALU.mult).then_inc(h_half, 1)
                v.wait_ge(h_half, b + 1)
                v.tensor_tensor(s_gu[:, 0, :], s_gu[:, 0, :], s_gu[:, 1, :], ALU.mult).then_inc(h_ready, 1)
                for j in range(TJ):
                    v.wait_ge(y_psum, TJ * b + j + 1)
                    x = X[:, bass.ds(TJ * b + j, 1), :].rearrange("p o d -> p (o d)")
                    v.tensor_tensor(x, x, p_y[j % 2], ALU.add).then_inc(x_added, 1)

            shared(0)
            with v.Fori(1, NB) as b:
                shared(b)
            turns(v, dve_step, L_DOWN)
            with v.Fori(0, NT // BACK) as g:
                for pair in range(BACK // 2):
                    before = (K - 1) * (BACK * g + 2 * pair)
                    for k in range(K):
                        for i in range(2):
                            q = 2 * pair + i
                            n = BACK * g + q
                            x = X[:, bass.ds(n, 1), :].rearrange("p o d -> p (o d)")
                            w = weight[:, bass.ds(n, 1), k:k + 1].rearrange("p o k -> p (o k)")
                            if k == 0:
                                v.wait_ge(back[q], 16 * (g + 1))
                            else:
                                v.wait_ge(part_sum, before + 2 * (k - 1) + i + 1)
                            v.scalar_tensor_tensor(out=x, in0=yk[q][:, k, :], scalar=w, in1=x, op0=ALU.mult, op1=ALU.add
                                                   ).then_inc(summed if k == K - 1 else part_sum, 1)
            v.wait_ge(summed, NT)
    return sems


def load_constants(nc, sb, x, const_d):
    with (nc.semaphore("c_in") as c_in, nc.semaphore("c_cast") as c_cast, nc.semaphore("c_ones") as c_ones,
          nc.sbuf_tensor("masks_sb", [P, C_AT[-1] - C_KEPT], F32) as masks, nc.Block() as block):
        @block.sync
        def _(sp):
            sp.dma_start(sb["const"][:, :], const_d[:, 0:C_KEPT]).then_inc(c_in, 16)
            sp.dma_start(masks[:, :], const_d[:, C_KEPT:]).then_inc(c_in, 16)
            sp.dma_start(sb["X"][:, :, :], x.rearrange("(t p) d -> p t d", p=P)).then_inc(c_in, 16)
            sp.wait_ge(c_in, 48)

        @block.gpsimd
        def _(pool):
            pool.memset(sb["ones_bf"][:, :], 1.0).then_inc(c_ones, 1)
            pool.wait_ge(c_ones, 1)

        @block.scalar
        def _(act):
            act.wait_ge(c_in, 48)
            act.activation(sb["ident_bf"][:, :], sb["const"][:, C_AT[C_ID]:C_AT[C_ID] + P], ACT.Copy).then_inc(c_cast, 1)
            for name, at in (("mask_bf", C_MASK), ("maskT_bf", C_MASKT), ("before_bf", C_LT)):
                act.activation(sb[name][:, :], masks[:, C_AT[at] - C_KEPT:C_AT[at] - C_KEPT + P], ACT.Copy
                               ).then_inc(c_cast, 1)
            act.wait_ge(c_cast, 4)


def store(nc, sb, out):
    with nc.semaphore("stored") as stored, nc.Block() as block:
        @block.sync
        def _(sp):
            sp.dma_start(out.rearrange("(t p) d -> p t d", p=P), sb["X"][:, :, :]).then_inc(stored, 16)
            sp.wait_ge(stored, 16)


def program(nc, x, const_d, wqkv_a, wout_a, ln_a, wqkv_b, wout_b, router, bias, gate_up, down, out):
    with ExitStack() as ctx:
        def buf(name, shape, dt=F32):
            return ctx.enter_context(nc.sbuf_tensor(name + "_sb", shape, dt))

        sb = {"X": buf("X", [P, NT, D]), "const": buf("const", [P, C_KEPT]),
              "ps": ctx.enter_context(nc.psum_tensor("ps", [P, 8, 512], F32))}
        for name in ("ident_bf", "mask_bf", "maskT_bf", "before_bf", "ones_bf"):
            sb[name] = buf(name, [P, P], BF16)
        sb["Wgu"] = buf("Wgu", [P, 2, E + 1, 2 * I])
        sb["wgu_in"] = ctx.enter_context(nc.semaphore("wgu_in"))
        sb["router_d"], sb["bias_d"], sb["gate_up_d"] = router, bias, gate_up
        xs_d = nc.dram_tensor("dispatched", (E * REG + P, ROW), F32, kind="Internal").ap()
        y_d = nc.dram_tensor("results", (NRES, D), F32, kind="Internal").ap()
        sb["max_d"] = nc.dram_tensor("maxima", (3 * H, T), BF16, kind="Internal").ap()
        load_constants(nc, sb, x, const_d)
        for rotary, wqkv, wout in ((True, wqkv_a, wout_a), (False, wqkv_b, wout_b)):
            nc.clear_and_free_semaphores(attention(nc, sb, rotary, wqkv, wout, ln_a))
            nc.all_engine_barrier()
            nc.clear_and_free_semaphores(experts(nc, sb, xs_d, y_d, down, "mix_a" if rotary else "mix_b"))
            nc.all_engine_barrier()
        store(nc, sb, out)


def layout(L0_attn_a_x, L0_attn_a_w_qkv, L0_attn_a_w_out, L0_attn_a_ln_scale, L0_attn_a_ln_bias, L0_attn_b_Wq,
           L0_attn_b_Wk, L0_attn_b_Wv, L0_attn_b_Wo, L0_ffn_router_w, L0_ffn_expert_bias, L0_ffn_gate_w, L0_ffn_up_w,
           L0_ffn_down_w, L0_ffn_shared_gate_w, L0_ffn_shared_up_w, L0_ffn_shared_down_w):
    def rows(*vectors):
        return np.ascontiguousarray(np.broadcast_to(np.stack(vectors)[None], (P, len(vectors), vectors[0].shape[0])))

    t = np.ascontiguousarray
    return {
        "x": L0_attn_a_x.reshape(NT * P, D),
        "const": constants(),
        "wqkv_a": L0_attn_a_w_qkv,
        "wout_a": L0_attn_a_w_out,
        "ln_a": rows(L0_attn_a_ln_scale, L0_attn_a_ln_bias),
        "wqkv_b": t(np.concatenate([L0_attn_b_Wq.T, L0_attn_b_Wk.T, L0_attn_b_Wv.T], axis=1)),
        "wout_b": t(L0_attn_b_Wo.T),
        "router": t(L0_ffn_router_w.T),
        "bias": t(np.broadcast_to(L0_ffn_expert_bias[None], (P, E))),
        "gate_up": t(np.concatenate([
            np.concatenate([L0_ffn_gate_w, L0_ffn_shared_gate_w[None]], 0).transpose(2, 0, 1),
            np.concatenate([L0_ffn_up_w, L0_ffn_shared_up_w[None]], 0).transpose(2, 0, 1)], axis=2)),
        "down": t(np.concatenate([L0_ffn_down_w, L0_ffn_shared_down_w[None]], 0).transpose(2, 0, 1)),
    }


def kernel(**inputs):
    import concourse.bacc as bacc
    from concourse.bass_utils import run_bass_kernel_spmd

    arrays = layout(**{name: np.asarray(a) for name, a in inputs.items()})
    nc = bacc.Bacc("TRN2", target_bir_lowering=False, num_devices=1)
    aps = [nc.dram_tensor(n, a.shape, mybir.dt.from_np(a.dtype), kind="ExternalInput").ap() for n, a in arrays.items()]
    out = nc.dram_tensor("out", (NT * P, D), F32, kind="ExternalOutput").ap()
    program(nc, *aps, out)
    r = run_bass_kernel_spmd(nc, [arrays], core_ids=[0])
    return r.results[0]["out"].reshape(NB, T, D)
```
